# Optimizing a Trainium2 kernel written in Bass

```python
import numpy as np
import jax
import jax.numpy as jnp

def _softmax(x, axis=-1):
    return jax.nn.softmax(x, axis=axis)

def _gelu(x):
    return jax.nn.gelu(x, approximate=True)

def _silu(x):
    return jax.nn.silu(x)

def _sigmoid(x):
    return jax.nn.sigmoid(x)

def _layernorm(x, axis=-1, eps=1e-05):
    m = jnp.mean(x, axis=axis, keepdims=True)
    v = jnp.var(x, axis=axis, keepdims=True)
    return (x - m) / jnp.sqrt(v + eps)

def _scatter_add(tgt, idx, src, axis=0):
    return tgt.at[idx].add(src)

def _segment_sum(src, seg, n):
    return jax.ops.segment_sum(src, seg, n)
kernel_name = 'mk_flamingo_gated_d2_seqx_r4_3c6233'

def setup_inputs(seed: int=0):
    np.random.seed(seed)
    _w = jnp.asarray

    def _rec_inputs():
        import jax
        import jax.numpy as jnp
        _rk = jax.random.key(seed)
        x = -0.0002928 + 1 * jax.random.normal(jax.random.fold_in(_rk, 1), (4, 1024, 256), jnp.float32)
        _lenS = 1024 - jax.random.randint(jax.random.fold_in(_rk, 7), (4,), 0, max(1, 1024 // 4) + 1, jnp.int32)
        _lenS2 = 77 - jax.random.randint(jax.random.fold_in(_rk, 8), (4,), 0, max(1, 77 // 4) + 1, jnp.int32)
        _ctx_1024P = jax.random.normal(jax.random.fold_in(_rk, 11), (4, 16, 256), jnp.float32)
        _ctx_1024c = jax.random.dirichlet(jax.random.fold_in(_rk, 511), 0.3 * jnp.ones((16,), jnp.float32), (4, 77))
        _ctx_1024t = jnp.einsum('bsk,bkd->bsd', _ctx_1024c, _ctx_1024P)
        _ctx_1024t = _ctx_1024t * jax.lax.rsqrt(jnp.mean(jnp.square(_ctx_1024t)) + 1e-12) * 0.953939
        ctx_1024 = -1.39393e-06 + 0.999914 * (_ctx_1024t + 0.3 * jax.random.normal(jax.random.fold_in(_rk, 611), (4, 77, 256), jnp.float32))
        _validS = jnp.arange(1024)[None, :] < _lenS[:, None]
        _validS2 = jnp.arange(77)[None, :] < _lenS2[:, None]
        _causal = jnp.tril(jnp.ones((1024, 1024), dtype=bool))
        mask_1x1xSxS2_ik1 = jnp.where(jnp.broadcast_to(_validS2[0:1, None, None, :], (1, 1, 1024, 77)), 1, 0).astype(jnp.int32)
        _g = jax.random.normal(jax.random.fold_in(_rk, 9001), (2, 2), jnp.float32)
        _g = jnp.sign(_g) * jnp.maximum(jnp.abs(_g), 1.0) + (_g == 0) * 1.0
        g_xattn = _g[0]
        g_ffn = _g[1]
        return (x, ctx_1024, mask_1x1xSxS2_ik1, g_xattn, g_ffn)
    x, ctx_1024, mask_1x1xSxS2_ik1, g_xattn, g_ffn = _rec_inputs()

    def _L0_xattn_setup():
        import jax, jax.numpy as jnp
        import numpy as np
        D_MODEL = 256
        N_HEAD = 16
        HEAD = D_MODEL // N_HEAD

        def _split_heads(x):
            B, S, _ = x.shape
            return x.reshape(B, S, N_HEAD, HEAD).transpose(0, 2, 1, 3)
        key = jax.random.key(seed)
        ks = jax.random.split(key, 12)
        B, S = (2, 512)
        s = 1.0 / np.sqrt(D_MODEL)
        inp = {'q': jax.random.normal(ks[0], (B, S, D_MODEL), jnp.float32), 'k': jax.random.normal(ks[1], (B, S, D_MODEL), jnp.float32), 'v': jax.random.normal(ks[2], (B, S, D_MODEL), jnp.float32), 'mask': jax.random.randint(ks[3], (1, 1, S, S), 0, 2, jnp.int32), 'wq': jax.random.normal(ks[4], (D_MODEL, D_MODEL), jnp.float32) * s, 'bq': jnp.zeros((D_MODEL,), jnp.float32), 'wk': jax.random.normal(ks[5], (D_MODEL, D_MODEL), jnp.float32) * s, 'bk': jnp.zeros((D_MODEL,), jnp.float32), 'wv': jax.random.normal(ks[6], (D_MODEL, D_MODEL), jnp.float32) * s, 'bv': jnp.zeros((D_MODEL,), jnp.float32), 'wo': jax.random.normal(ks[7], (D_MODEL, D_MODEL), jnp.float32) * s, 'bo': jnp.zeros((D_MODEL,), jnp.float32)}
        return inp
    _L0_xattn_all = _L0_xattn_setup()
    _L0_xattn_in = {k: v for k, v in _L0_xattn_all.items() if k in ('wq', 'bq', 'wk', 'bk', 'wv', 'bv', 'wo', 'bo')}
    del _L0_xattn_all

    def _L0_ffn_setup():
        import jax, jax.numpy as jnp
        import numpy as np
        EXPERTS = 8
        TOP_K = 2

        def swiglu(x, w1, w2, w3):
            h = x @ w1
            return h * jax.nn.sigmoid(h) * (x @ w2) @ w3
        key = jax.random.key(seed)
        ks = jax.random.split(key, 9)
        B, S, D = (4, 512, 256)
        H = 2 * D
        s = 0.02
        x = jax.random.normal(ks[0], (B, S, D), dtype=jnp.float32)
        gate_w = jax.random.normal(ks[1], (D, EXPERTS), dtype=jnp.float32) * s
        ew1 = jax.random.normal(ks[2], (EXPERTS, D, H), dtype=jnp.float32) * s
        ew2 = jax.random.normal(ks[3], (EXPERTS, D, H), dtype=jnp.float32) * s
        ew3 = jax.random.normal(ks[4], (EXPERTS, H, D), dtype=jnp.float32) * s
        sw1 = jax.random.normal(ks[5], (D, H), dtype=jnp.float32) * s
        sw2 = jax.random.normal(ks[6], (D, H), dtype=jnp.float32) * s
        sw3 = jax.random.normal(ks[7], (H, D), dtype=jnp.float32) * s
        return {'x': x, 'gate_w': gate_w, 'ew1': ew1, 'ew2': ew2, 'ew3': ew3, 'sw1': sw1, 'sw2': sw2, 'sw3': sw3}
    _L0_ffn_all = _L0_ffn_setup()
    _L0_ffn_in = {k: v for k, v in _L0_ffn_all.items() if k in ('gate_w', 'ew1', 'ew2', 'ew3', 'sw1', 'sw2', 'sw3')}
    del _L0_ffn_all

    def _L1_xattn_setup():
        import jax, jax.numpy as jnp
        import numpy as np
        EPS = 1e-06

        def _rmsnorm(x, w, eps=EPS):
            x32 = x.astype(jnp.float32)
            var = jnp.mean(x32 * x32, axis=-1, keepdims=True)
            return (x32 * jax.lax.rsqrt(var + eps)).astype(x.dtype) * w
        key = jax.random.key(seed)
        ks = jax.random.split(key, 6)
        B, S, K, H = (4, 512, 64, 256)
        return {'hidden_states': jax.random.normal(ks[0], (B, S, H), jnp.float32), 'memory_state': jax.random.normal(ks[1], (B, K, H), jnp.float32), 'q_w': jax.random.normal(ks[2], (H, H), jnp.float32) * (1.0 / np.sqrt(H)), 'k_w': jax.random.normal(ks[3], (H, H), jnp.float32) * (1.0 / np.sqrt(H)), 'norm_w': jnp.ones((H,), jnp.float32), 'gate_w': jax.random.normal(ks[4], (H, H), jnp.float32) * 0.02, 'gate_b': jnp.zeros((H,), jnp.float32)}
    _L1_xattn_all = _L1_xattn_setup()
    _L1_xattn_in = {k: v for k, v in _L1_xattn_all.items() if k in ('q_w', 'k_w', 'norm_w', 'gate_w', 'gate_b')}
    del _L1_xattn_all

    def _L1_ffn_setup():
        import jax, jax.numpy as jnp
        import numpy as np
        B, S, D, E, H, K = (4, 512, 256, 8, 128, 2)
        key = jax.random.key(seed)
        ks = jax.random.split(key, 11)
        sc = 0.02
        return {'x': jax.random.normal(ks[0], (B, S, D), dtype=jnp.float32), 'gate_W': jax.random.normal(ks[1], (D, E), dtype=jnp.float32) * sc, 'W1': jax.random.normal(ks[2], (E, D, H), dtype=jnp.float32) * sc, 'b1': jnp.zeros((E, H), dtype=jnp.float32), 'W2': jax.random.normal(ks[3], (E, H, D), dtype=jnp.float32) * sc, 'b2': jnp.zeros((E, D), dtype=jnp.float32), 'Ws1': jax.random.normal(ks[4], (D, H), dtype=jnp.float32) * sc, 'bs1': jnp.zeros((H,), dtype=jnp.float32), 'Ws2': jax.random.normal(ks[5], (H, D), dtype=jnp.float32) * sc, 'bs2': jnp.zeros((D,), dtype=jnp.float32), 'route_scale': jnp.ones((), dtype=jnp.float32)}
    _L1_ffn_all = _L1_ffn_setup()
    _L1_ffn_in = {k: v for k, v in _L1_ffn_all.items() if k in ('gate_W', 'W1', 'b1', 'W2', 'b2', 'Ws1', 'bs1', 'Ws2', 'bs2', 'route_scale')}
    del _L1_ffn_all
    return {'x': x, 'ctx_1024': ctx_1024, 'mask_1x1xSxS2_ik1': mask_1x1xSxS2_ik1, 'g_xattn': g_xattn, 'g_ffn': g_ffn, 'L0_xattn_wq': _L0_xattn_in['wq'], 'L0_xattn_bq': _L0_xattn_in['bq'], 'L0_xattn_wk': _L0_xattn_in['wk'], 'L0_xattn_bk': _L0_xattn_in['bk'], 'L0_xattn_wv': _L0_xattn_in['wv'], 'L0_xattn_bv': _L0_xattn_in['bv'], 'L0_xattn_wo': _L0_xattn_in['wo'], 'L0_xattn_bo': _L0_xattn_in['bo'], 'L0_ffn_gate_w': _L0_ffn_in['gate_w'], 'L0_ffn_ew1': _L0_ffn_in['ew1'], 'L0_ffn_ew2': _L0_ffn_in['ew2'], 'L0_ffn_ew3': _L0_ffn_in['ew3'], 'L0_ffn_sw1': _L0_ffn_in['sw1'], 'L0_ffn_sw2': _L0_ffn_in['sw2'], 'L0_ffn_sw3': _L0_ffn_in['sw3'], 'L1_xattn_q_w': _L1_xattn_in['q_w'], 'L1_xattn_k_w': _L1_xattn_in['k_w'], 'L1_xattn_norm_w': _L1_xattn_in['norm_w'], 'L1_xattn_gate_w': _L1_xattn_in['gate_w'], 'L1_xattn_gate_b': _L1_xattn_in['gate_b'], 'L1_ffn_gate_W': _L1_ffn_in['gate_W'], 'L1_ffn_W1': _L1_ffn_in['W1'], 'L1_ffn_b1': _L1_ffn_in['b1'], 'L1_ffn_W2': _L1_ffn_in['W2'], 'L1_ffn_b2': _L1_ffn_in['b2'], 'L1_ffn_Ws1': _L1_ffn_in['Ws1'], 'L1_ffn_bs1': _L1_ffn_in['bs1'], 'L1_ffn_Ws2': _L1_ffn_in['Ws2'], 'L1_ffn_bs2': _L1_ffn_in['bs2'], 'L1_ffn_route_scale': _L1_ffn_in['route_scale']}

def reference(x, ctx_1024, mask_1x1xSxS2_ik1, g_xattn, g_ffn, L0_xattn_wq, L0_xattn_bq, L0_xattn_wk, L0_xattn_bk, L0_xattn_wv, L0_xattn_bv, L0_xattn_wo, L0_xattn_bo, L0_ffn_gate_w, L0_ffn_ew1, L0_ffn_ew2, L0_ffn_ew3, L0_ffn_sw1, L0_ffn_sw2, L0_ffn_sw3, L1_xattn_q_w, L1_xattn_k_w, L1_xattn_norm_w, L1_xattn_gate_w, L1_xattn_gate_b, L1_ffn_gate_W, L1_ffn_W1, L1_ffn_b1, L1_ffn_W2, L1_ffn_b2, L1_ffn_Ws1, L1_ffn_bs1, L1_ffn_Ws2, L1_ffn_bs2, L1_ffn_route_scale):
    import jax
    import jax.numpy as jnp

    def _L0_xattn_ref(q, k, v, mask, wq, bq, wk, bk, wv, bv, wo, bo):
        import jax, jax.numpy as jnp
        import numpy as np
        D_MODEL = 256
        N_HEAD = 16
        HEAD = D_MODEL // N_HEAD

        def _split_heads(x):
            B, S, _ = x.shape
            return x.reshape(B, S, N_HEAD, HEAD).transpose(0, 2, 1, 3)
        q_s = _split_heads(q @ wq.T + bq)
        k_s = _split_heads(k @ wk.T + bk)
        v_s = _split_heads(v @ wv.T + bv)
        scale = 1.0 / np.sqrt(HEAD)
        score = jnp.einsum('bhqd,bhkd->bhqk', q_s, k_s) * scale
        score = jnp.where(mask == 0, jnp.float32(-10000.0), score)
        attn = jax.nn.softmax(score, axis=-1)
        out = jnp.einsum('bhqk,bhkd->bhqd', attn, v_s)
        B, H, S, Dh = out.shape
        out = out.transpose(0, 2, 1, 3).reshape(B, S, H * Dh)
        return out @ wo.T + bo

    def _L0_ffn_ref(x, gate_w, ew1, ew2, ew3, sw1, sw2, sw3):
        import jax, jax.numpy as jnp
        import numpy as np
        EXPERTS = 8
        TOP_K = 2

        def swiglu(x, w1, w2, w3):
            h = x @ w1
            return h * jax.nn.sigmoid(h) * (x @ w2) @ w3
        B, S, D = x.shape
        gate_out = x @ gate_w
        top_v, top_i = jax.lax.top_k(gate_out, TOP_K)
        masked = jnp.full_like(gate_out, -1e+20)
        bi = jnp.arange(B)[:, None, None]
        si = jnp.arange(S)[None, :, None]
        masked = masked.at[bi, si, top_i].set(top_v)
        probs = jax.nn.softmax(masked, axis=-1)
        chosen = jnp.zeros_like(gate_out, dtype=bool).at[bi, si, top_i].set(True)
        w = jnp.where(chosen, probs, 0.0)

        def one_expert(w1, w2, w3, we):
            return swiglu(x, w1, w2, w3) * we[..., None]
        out = jax.vmap(one_expert, in_axes=(0, 0, 0, 2))(ew1, ew2, ew3, w).sum(0)
        out = out + swiglu(x, sw1, sw2, sw3)
        return out

    def _L1_xattn_ref(hidden_states, memory_state, q_w, k_w, norm_w, gate_w, gate_b):
        import jax, jax.numpy as jnp
        import numpy as np
        EPS = 1e-06

        def _rmsnorm(x, w, eps=EPS):
            x32 = x.astype(jnp.float32)
            var = jnp.mean(x32 * x32, axis=-1, keepdims=True)
            return (x32 * jax.lax.rsqrt(var + eps)).astype(x.dtype) * w
        B, S, H = hidden_states.shape
        K = memory_state.shape[1]
        scale = 1.0 / np.sqrt(H)
        normed = _rmsnorm(hidden_states, norm_w)
        v_pool = jnp.concatenate([normed, memory_state], axis=1)
        q = jnp.einsum('bsh,oh->bso', normed, q_w)
        k = jnp.einsum('bth,oh->bto', v_pool, k_w)
        logits = jnp.einsum('bsd,btd->bst', q, k) * scale
        local = jnp.tril(jnp.ones((S, S), bool))
        mask = jnp.concatenate([local, jnp.ones((S, K), bool)], axis=1)
        logits = jnp.where(mask[None], logits, -jnp.inf)
        attn = jax.nn.softmax(logits, axis=-1)
        h_tilde = jnp.einsum('bst,bth->bsh', attn, v_pool)
        alpha = jax.nn.sigmoid(jnp.einsum('bsh,oh->bso', hidden_states, gate_w) + gate_b)
        return (1.0 - alpha) * hidden_states + alpha * h_tilde

    def _L1_ffn_ref(x, gate_W, W1, b1, W2, b2, Ws1, bs1, Ws2, bs2, route_scale):
        import jax, jax.numpy as jnp
        import numpy as np
        B, S, D, E, H, K = (4, 512, 256, 8, 128, 2)
        scores = jax.nn.sigmoid(x @ gate_W) * route_scale
        topk_scores, topk_idx = jax.lax.top_k(scores, K)
        topk_w = topk_scores / topk_scores.sum(-1, keepdims=True)
        onehot = jax.nn.one_hot(topk_idx, E, dtype=x.dtype)
        gate_full = jnp.einsum('bsk,bske->bse', topk_w, onehot)
        h = jax.nn.gelu(jnp.einsum('bsd,edh->bseh', x, W1) + b1, approximate=False)
        y = jnp.einsum('bseh,ehd->bsed', h, W2) + b2
        expert_out = jnp.einsum('bse,bsed->bsd', gate_full, y)
        shared = jax.nn.gelu(x @ Ws1 + bs1, approximate=False) @ Ws2 + bs2
        return expert_out + shared
    x = x + jnp.tanh(g_xattn[0]) * _L0_xattn_ref(_layernorm(x, axis=-1), ctx_1024, ctx_1024, mask_1x1xSxS2_ik1, L0_xattn_wq, L0_xattn_bq, L0_xattn_wk, L0_xattn_bk, L0_xattn_wv, L0_xattn_bv, L0_xattn_wo, L0_xattn_bo)
    x = x + jnp.tanh(g_ffn[0]) * _L0_ffn_ref(_layernorm(x, axis=-1), L0_ffn_gate_w, L0_ffn_ew1, L0_ffn_ew2, L0_ffn_ew3, L0_ffn_sw1, L0_ffn_sw2, L0_ffn_sw3)
    x = x + jnp.tanh(g_xattn[1]) * _L1_xattn_ref(_layernorm(x, axis=-1), ctx_1024, L1_xattn_q_w, L1_xattn_k_w, L1_xattn_norm_w, L1_xattn_gate_w, L1_xattn_gate_b)
    x = x + jnp.tanh(g_ffn[1]) * _L1_ffn_ref(_layernorm(x, axis=-1), L1_ffn_gate_W, L1_ffn_W1, L1_ffn_b1, L1_ffn_W2, L1_ffn_b2, L1_ffn_Ws1, L1_ffn_bs1, L1_ffn_Ws2, L1_ffn_bs2, L1_ffn_route_scale)
    return x

_drawn_inputs = setup_inputs


def setup_inputs(seed=0):
    import zlib

    import numpy as np

    out = dict(_drawn_inputs(seed))
    spreads = {'g_ffn': (-1.0, 0.6),
     'L0_xattn_bq': (0.0, 0.446),
     'L0_xattn_bk': (0.0, 2.0),
     'L0_xattn_bv': (0.0, 0.1),
     'L0_xattn_bo': (0.0, 0.1),
     'L1_xattn_norm_w': (1.0, 0.2),
     'L1_xattn_gate_b': (0.0, 0.276),
     'L1_ffn_b1': (0.0, 0.646),
     'L1_ffn_b2': (0.0, 0.1),
     'L1_ffn_bs1': (0.0, 0.496),
     'L1_ffn_bs2': (0.0, 0.1)}
    factors = {'L0_ffn_gate_w': 3.935,
     'L0_ffn_ew1': 3.483,
     'L0_ffn_ew2': 3.532,
     'L0_ffn_ew3': 3.448,
     'L0_ffn_sw1': 2.977,
     'L0_ffn_sw2': 3.071,
     'L0_ffn_sw3': 2.989}
    for name, (base, spread) in spreads.items():
        noise = np.random.default_rng([zlib.crc32(name.encode()), seed]).standard_normal(out[name].shape)
        drawn = base * np.exp(spread * noise) if base else spread * noise
        out[name] = jnp.asarray(drawn.astype(out[name].dtype))
    for name, factor in factors.items():
        out[name] = (out[name] * factor).astype(out[name].dtype)
    return out
```

```python
from contextlib import ExitStack

import numpy as np

import concourse.bass as bass
from concourse import mybir

F32 = mybir.dt.float32
F32R = mybir.dt.float32r
BF16 = mybir.dt.bfloat16
I32 = mybir.dt.int32
U32 = mybir.dt.uint32
ACT = mybir.ActivationFunctionType
ALU = mybir.AluOpType
AX = mybir.AxisListType

P = 128
B, S, D = 4, 1024, 256
KEYS = 77
HEADS, HEAD = 16, 16
KD = D // P
POS = S // P
NT = B * POS
E = 8
H0 = 512
H1 = 128
EPS_LN = 1e-5
EPS_RMS = 1e-6
MASKED = -10000.0
BANK = 512

PER_BANK = 6
PLACES = 3 * PER_BANK
GROUP = PER_BANK * KEYS
EVEN = KEYS + KEYS % 2
PCH = -(-HEADS * KEYS // P)
VW = HEAD + 1
MAXH = 3

T = B * S
SPARE = E * T
SPARE_ROWS = 1024
SHARED = SPARE + SPARE_ROWS
ROWS = SHARED + T
ROUTED_TILES = 2 * T // P + E - 1
TILES = -(-(NT + ROUTED_TILES) // 4) * 4


def chunk_heads(c):
    first = c * P // KEYS
    return first, min((c * P + P - 1) // KEYS, HEADS - 1) - first + 1


class Step:

    def __init__(self, round_, slot, width):
        self.round, self.slot, self.width = round_, slot, width

    @property
    def index(self):
        return self.round * self.width + self.slot

    @property
    def count(self):
        return self.round * self.width + (self.slot + 1)

    def before(self, back):
        return self.round * self.width + (self.slot + 1 - back)

    def after(self, back):
        return not isinstance(self.round, int) or self.index >= back


def pipeline(eng, tiles, depth, width, body, pause=None):
    first = -(-depth // width) * width
    last = tiles // width * width

    def fixed(s):
        def at(lag):
            t = s - lag
            return Step(t // width, t % width, width) if 0 <= t < tiles else None
        return at

    for s in range(first):
        body(fixed(s))
    cuts = [first, last]
    if pause:
        cuts.insert(1, pause[0])
    for n, (start, end) in enumerate(zip(cuts, cuts[1:])):
        if n:
            pause[1]()
        with eng.Fori(start // width, end // width) as i:
            for p in range(width):
                body(lambda lag: Step(i + (p - lag) // width, (p - lag) % width, width))
    for s in range(last, tiles + depth):
        body(fixed(s))


def three_passes(pe, out, left, right, start, stop):
    pe.matmul(out, left[0], right[0], start=start, stop=False, skip_group_check=True)
    pe.matmul(out, left[0], right[1], start=False, stop=False, skip_group_check=True)
    return pe.matmul(out, left[1], right[0], start=False, stop=stop, skip_group_check=True)


def wait_apart(eng, k, *waits):
    waits = [(sem, value if isinstance(value, int) else eng.to_reg(value)) for sem, value in waits]
    eng.wait_ge(k.started, 1)
    for sem, value in waits:
        eng.wait_ge(sem, value)


def run(at, *stages):
    for lag, stage in stages:
        t = at(lag)
        if t:
            stage(t)


class Bank:

    def __init__(self, tiles, users):
        self.tiles, self.users = tiles, users

    def last(self, name, t, lag=None):
        names = [u[0] for u in self.users]
        at = names.index(name) if name in names else len(names)
        lag = self.users[at][1] if lag is None else lag
        for back in range(3 * len(names)):
            i = at - 1 - back
            _, other, sem = self.users[i % len(names)]
            shift = lag - other + i // len(names)
            if isinstance(t.round, int):
                if not 0 <= t.index + shift < self.tiles:
                    continue
            return sem, t.before(-shift)
        return None

    def used(self, name, t):
        return self.last(name, t) is not None

    def freed(self, name, t, lag=None):
        return self.last(name, t, lag)


class Named:
    pass


class Scope:

    def __init__(self, nc, prefix):
        self.nc, self.prefix, self.stack = nc, prefix, ExitStack()
        self.held = []

    def __enter__(self):
        return self

    def __exit__(self, *a):
        done = self.stack.__exit__(*a)
        if self.held:
            self.nc.clear_and_free_semaphores(self.held)
            self.nc.all_engine_barrier()
        return done

    def sb(self, name, shape, dt=F32):
        return self.stack.enter_context(self.nc.sbuf_tensor(f"{self.prefix}_{name}", shape, dt))

    def ps(self, name, shape, dt=F32):
        return self.stack.enter_context(self.nc.psum_tensor(f"{self.prefix}_{name}", shape, dt))

    def sem(self, name):
        self.held.append(self.nc.alloc_semaphore(f"{self.prefix}_{name}"))
        return self.held[-1]

    def sems(self, names):
        return [self.sem(name) for name in names.split()]

    def block(self):
        return self.stack.enter_context(self.nc.Block())




def allocate_kept(nc, s):
    k = Named()
    k.ident = s.sb("ident", [P, P])
    k.neghalf = s.sb("neghalf", [P, 1])
    k.iota8 = s.sb("iota8", [P, E])
    k.tanh_g = s.sb("tanh_g", [P, 4])
    k.count = s.sb("count", [P, 5, E])
    k.slots = s.sb("slots", [P, POS * 2 * B], I32)
    k.weights = s.sb("weights", [P, POS * 2 * B])
    k.plan = s.sb("plan", [1, 2, 1 + TILES], I32)
    k.gates = s.sb("gates", [P, NT * (E + 1)])
    k.ones32 = s.sb("ones32", [P, NT])
    k.eps = s.sb("eps", [P, 2])
    k.started = s.sem("started")
    k.x1 = nc.dram_tensor("x1_scratch", (T, D), F32, kind="Internal").ap()
    k.xn = nc.dram_tensor("xn_scratch", (T, D), F32, kind="Internal").ap()
    k.table = nc.dram_tensor("table_scratch", (ROWS, 1), I32, kind="Internal").ap()
    k.y = nc.dram_tensor("y_scratch", (TILES * P, D), F32, kind="Internal").ap()
    k.x3 = nc.dram_tensor("x3_scratch", (T, D), F32, kind="Internal").ap()
    k.xn4T = nc.dram_tensor("xn4T_scratch", (D, T), F32, kind="Internal").ap()
    return k


def prepare_cross(nc, a, k, w):
    with Scope(nc, "prep") as s:
        wkT = s.sb("wkT", [P, KD, D])
        wvT = s.sb("wvT", [P, KD, D])
        wq_raw = s.sb("wq_raw", [P, KD, D])
        wo_raw = s.sb("wo_raw", [P, KD, D])
        wo_scaled = s.sb("wo_scaled", [P, KD, D])
        ctxT = s.sb("ctxT", [P, KD, B, KEYS])
        bk = s.sb("bk", [P, KD])
        bv = s.sb("bv", [P, D])
        bo = s.sb("bo", [P, D])
        g = s.sb("g", [P, 4])
        head_mask = s.sb("head_mask", [P, HEADS // KD])
        keysT = s.sb("keysT", [P, KD, B * KEYS])
        keysT_hi = s.sb("keysT_hi", [P, KD, B * KEYS], F32R)
        keysT_lo = s.sb("keysT_lo", [P, KD, B * KEYS], F32R)
        values = s.sb("values", [KEYS, B, D])
        zeros = s.sb("zeros", [P, SHARED // P], I32)
        k_ps = s.ps("k_ps", [P, KD, BANK])
        v_ps = s.ps("v_ps", [P, B, D])

        loaded = s.sem("loaded")
        pattern_loaded = s.sem("pattern_loaded")
        zeros_set = s.sem("zeros_set")
        table_cleared = s.sem("table_cleared")
        tanh_ready = s.sem("tanh_ready")
        keys_done = s.sem("keys_done")
        values_done = s.sem("values_done")
        keysT_ready = s.sem("keysT_ready")
        keys_hi_ready = s.sem("keys_hi_ready")
        keys_lo_ready = s.sem("keys_lo_ready")
        values_ready = s.sem("values_ready")
        values_placed = s.sem("values_placed")
        wo_scaled_ready = s.sem("wo_scaled_ready")
        w_hi_ready = s.sem("w_hi_ready")
        const_set = s.sem("const_set")
        prepared = s.sem("prepared")

        loads = [
            (ctxT[:, :, :, :], a["ctxT"].rearrange("(k p) b n -> p k b n", p=P)),
            (wkT[:, :, :], a["L0_xattn_wk"].rearrange("(k p) n -> p k n", p=P)),
            (wvT[:, :, :], a["L0_xattn_wv"].rearrange("(k p) n -> p k n", p=P)),
            (bk[:, :], a["L0_xattn_bk"]),
            (bv[:, :], a["L0_xattn_bv"].partition_broadcast(P)),
            (head_mask[:, :], a["c_head_mask"]),
            (wq_raw[:, :, :], a["L0_xattn_wq"].rearrange("(k p) n -> p k n", p=P)),
            (wo_raw[:, :, :], a["L0_xattn_wo"].rearrange("(k p) n -> p k n", p=P)),
            (bo[:, :], a["L0_xattn_bo"].partition_broadcast(P)),
            (g[:, :], a["gates"].partition_broadcast(P)),
            (w.bq[:, :], a["L0_xattn_bq"]),
            (w.mask[:, :].rearrange("p (t n) -> p t n", n=KEYS), a["mask"].rearrange("(t p) n -> p t n", p=P)),
            (w.gate[:, :, :], a["L0_ffn_gate_w"].rearrange("(k p) n -> p k n", p=P)),
            (w.token[:, :], a["c_token"]),
            (w.upper[:, :], a["c_upper"]),
            (k.ident[:, :], a["c_ident"]),
            (k.iota8[:, :], a["c_iota8"]),
            (k.count[:, B, :], a["c_region"]),
        ]
        block = s.block()

        @block.sync
        def _(sp):
            for to, of in loads:
                sp.dma_start(to, of).then_inc(loaded, 16)
            for b in range(B):
                sp.dma_start(w.values[:, b, :, :], a["c_values"]).then_inc(pattern_loaded, 16)
            sp.wait_ge(pattern_loaded, 16 * B)
            sp.wait_ge(values_ready, 1)
            placed = 0
            for h in range(HEADS):
                r = h * KEYS
                while r < (h + 1) * KEYS:
                    c = r // P
                    n = min((h + 1) * KEYS, (c + 1) * P) - r
                    col = (h - chunk_heads(c)[0]) * VW
                    sp.dma_start(w.values[r - c * P:r - c * P + n, :, c, col:col + HEAD],
                                 values[r - h * KEYS:r - h * KEYS + n, :, h * HEAD:(h + 1) * HEAD]
                                 ).then_inc(values_placed, 16)
                    placed += 1
                    r += n
            sp.wait_ge(values_placed, 16 * placed)

        @block.gpsimd
        def _(pool):
            pool.memset(zeros[:, :], 0).then_inc(zeros_set, 1)
            pool.memset(w.masked[:, :, :], MASKED * HEAD ** 0.5).then_inc(const_set, 1)
            pool.memset(k.ones32[:, :], 1.0).then_inc(k.started, 1)
            pool.memset(k.neghalf[:, :], -0.5).then_inc(const_set, 1)
            pool.memset(k.eps[:, 0:1], EPS_LN).then_inc(const_set, 1)
            pool.memset(k.eps[:, 1:2], EPS_RMS).then_inc(const_set, 1)
            pool.memset(w.ones[:, :], 1.0).then_inc(const_set, 1)
            pool.wait_ge(zeros_set, 1)
            pool.dma_start(k.table[0:SHARED, :].rearrange("(p n) o -> p (n o)", p=P),
                           zeros[:, :]).then_inc(table_cleared, 16)
            pool.dma_start(k.table[SHARED:ROWS, :].rearrange("(p n) o -> p (n o)", p=P),
                           a["c_order"].rearrange("(p n) -> p n", p=P)).then_inc(table_cleared, 16)
            pool.wait_ge(loaded, 16 * len(loads))
            pool.tensor_copy(w.wq[0][:, :, :], wq_raw[:, :, :]).then_inc(w_hi_ready, 1)
            pool.wait_ge(wo_scaled_ready, 1)
            pool.tensor_copy(w.wo[0][:, :, :], wo_scaled[:, :, :]).then_inc(w_hi_ready, 1)
            pool.wait_ge(table_cleared, 32)

        @block.tensor
        def _(pe):
            pe.wait_ge(loaded, 16 * len(loads))
            for c in range(KD):
                for kk in range(KD):
                    mm = pe.matmul(k_ps[:, c, 0:B * KEYS], wkT[:, kk, c * P:(c + 1) * P],
                                   ctxT[:, kk, :, :].rearrange("p b n -> p (b n)"),
                                   start=(kk == 0), stop=(kk == KD - 1))
            mm.then_inc(keys_done, 1)
            for b in range(B):
                for kk in range(KD):
                    mm = pe.matmul(v_ps[0:KEYS, b, :], ctxT[:, kk, b, :], wvT[:, kk, :],
                                   start=(kk == 0 and b % 2 == 0), stop=(kk == KD - 1),
                                   skip_group_check=True)
            mm.then_inc(values_done, 1)

        @block.scalar
        def _(act):
            act.wait_ge(loaded, 16 * len(loads))
            act.activation(k.tanh_g[:, :], g[:, :], ACT.Tanh).then_inc(tanh_ready, 1)
            act.wait_ge(keys_done, 1)
            for c in range(KD):
                act.activation(keysT[:, c, :], k_ps[:, c, 0:B * KEYS], ACT.Identity,
                               bias=bk[:, c:c + 1]).then_inc(keysT_ready, 1)
            act.wait_ge(keysT_ready, KD)
            act.activation(keysT_hi[:, :, :], keysT[:, :, :], ACT.Copy).then_inc(keys_hi_ready, 1)

        @block.vector
        def _(dve):
            dve.wait_ge(tanh_ready, 1)
            dve.tensor_scalar(wo_scaled[:, :, :], wo_raw[:, :, :], k.tanh_g[:, 0:1], None,
                              ALU.mult).then_inc(wo_scaled_ready, 1)
            dve.tensor_scalar(w.bo[:, :], bo[:, :], k.tanh_g[:, 0:1], None, ALU.mult).then_inc(prepared, 1)
            dve.wait_ge(values_done, 1)
            dve.tensor_tensor(values[:, :, :], v_ps[0:KEYS, :, :],
                              bv[0:KEYS, :].unsqueeze(1).to_broadcast([KEYS, B, D]),
                              ALU.add).then_inc(values_ready, 1)
            dve.wait_ge(keys_hi_ready, 1)
            dve.tensor_tensor(keysT_lo[:, :, :], keysT[:, :, :], keysT_hi[:, :, :].bitcast(F32),
                              ALU.subtract).then_inc(keys_lo_ready, 1)
            dve.wait_ge(keys_lo_ready, 1)
            for c in range(KD):
                for b in range(B):
                    for part, of in ((0, keysT_hi), (1, keysT_lo)):
                        src = of[:, c, b * KEYS:(b + 1) * KEYS].bitcast(F32)
                        dve.tensor_tensor(
                            w.keys[part][:, b, c, :].rearrange("p (h n) -> p h n", n=KEYS),
                            src.unsqueeze(1).to_broadcast([P, HEADS // KD, KEYS]),
                            head_mask[:, :].unsqueeze(2).to_broadcast([P, HEADS // KD, KEYS]),
                            ALU.mult).then_inc(prepared, 1)
            dve.wait_ge(w_hi_ready, 2)
            dve.tensor_tensor(w.wq[1][:, :, :], wq_raw[:, :, :], w.wq[0][:, :, :].bitcast(F32),
                              ALU.subtract).then_inc(prepared, 1)
            dve.tensor_tensor(w.wo[1][:, :, :], wo_scaled[:, :, :], w.wo[0][:, :, :].bitcast(F32),
                              ALU.subtract).then_inc(prepared, 1)
            dve.memset(w.scores_tail, 0.0).then_inc(prepared, 1)


def cross_attention(nc, a, k):
    with Scope(nc, "cross") as s:
        w = Named()
        w.wq = [s.sb(f"wq{i}", [P, KD, D], F32R) for i in range(2)]
        w.wo = [s.sb(f"wo{i}", [P, KD, D], F32R) for i in range(2)]
        w.keys = [s.sb(f"keys{i}", [P, B, KD, HEADS // KD * KEYS], F32R) for i in range(2)]
        w.values = s.sb("values", [P, B, PCH, MAXH * VW])
        w.bq = s.sb("bq", [P, KD])
        w.bo = s.sb("bo", [P, D])
        w.gate = s.sb("gate", [P, KD, E])
        w.mask = s.sb("mask", [P, POS * KEYS], I32)
        w.token = s.sb("token", [P, POS * B], I32)
        w.upper = s.sb("upper", [P, P])
        w.ones = s.sb("ones", [P, P])
        w.masked = s.sb("masked", [P, 2, PLACES * KEYS])
        scores = s.ps("scores", [P, 3, BANK])
        w.scores_tail = scores[:, 2, (HEADS - 2 * PER_BANK) * KEYS:GROUP]
        prepare_cross(nc, a, k, w)

        mask_now = s.sb("mask_now", [P, KEYS], I32)
        x = s.sb("x", [P, 4, D])
        x_again = s.sb("x_again", [P, 4, D])
        stats = s.sb("stats", [P, 4, 6])
        moments = s.sb("moments", [P, 4, 2])
        var_eps = s.sb("var_eps", [P, 4])
        rstd = s.sb("rstd", [P, 4])
        shift_x = s.sb("shift_x", [P, 4])
        shift_x1 = s.sb("shift_x1", [P, 4])
        xn = s.sb("xn", [P, 2, D])
        xT = [s.sb(f"xT{i}", [P, 2, KD * P], F32R) for i in range(2)]
        qT = [s.sb(f"qT{i}", [P, 2, KD * P], F32R) for i in range(2)]
        rowmax = s.sb("rowmax", [P, 2, PLACES])
        shifted = s.sb("shifted", [P, 2, PLACES * KEYS])
        probs = s.sb("probs", [P, 2, PCH * P])
        probsT = s.sb("probsT", [P, 2, PCH * P])
        rden = s.sb("rden", [P, 2, HEADS])
        att = s.sb("att", [P, 2, D])
        attT = [s.sb(f"attT{i}", [P, 2, KD * P], F32R) for i in range(2)]
        base = s.sb("base", [P, 2, D])
        x1 = s.sb("x1", [P, 4, D])
        stats1 = s.sb("stats1", [P, 4, 6])
        moments1 = s.sb("moments1", [P, 4, 2])
        var_eps1 = s.sb("var_eps1", [P, 4])
        rstd1 = s.sb("rstd1", [P, 4])
        xn1 = s.sb("xn1", [P, 4, D])
        xn1T = s.sb("xn1T", [P, 2, KD * P])
        logits = s.sb("logits", [P, 4, E])
        top = s.sb("top", [P, 4, 8])
        top_at = s.sb("top_at", [P, 4, 8], U32)
        gap = s.sb("gap", [P, 4])
        gap_exp = s.sb("gap_exp", [P, 4])
        total = s.sb("total", [P, 4])
        rtotal = s.sb("rtotal", [P, 4])
        chosen_at = s.sb("chosen_at", [P, 4, 2])
        chosen = s.sb("chosen", [P, 4, 2, E])
        either = s.sb("either", [P, 4, E])
        rank = s.sb("rank", [P, 4, E])
        ranked = s.sb("ranked", [P, 4, 2, E])
        slot_f = s.sb("slot_f", [P, 4, 2])
        slot = s.sb("slot", [P, 2 * B], I32)
        token = s.sb("token_now", [P, 4], I32)

        turn_ps = s.ps("turn_ps", [P, BANK])
        q_ps = s.ps("q_ps", [P, BANK])
        pT_ps = s.ps("pT_ps", [P, 2, BANK])
        pv_ps = s.ps("pv_ps", [P, BANK])

        q = Named()
        (q.shift_ready, q.shift1_ready) = s.sems("shift_ready shift1_ready")
        (q.stats_ready, q.moments_ready, q.var_ready, q.rstd_ready, q.xn_ready) = s.sems(
            "stats_ready moments_ready var_ready rstd_ready xn_ready")
        (q.xT_done, q.xT_hi, q.xT_lo, q.q_done, q.q_hi, q.q_lo, q.scores_done) = s.sems(
            "xT_done xT_hi xT_lo q_done q_hi q_lo scores_done")
        (q.masked_ready, q.rowmax_ready, q.shifted_ready, q.refilled, q.probs_ready) = s.sems(
            "masked_ready rowmax_ready shifted_ready refilled probs_ready")
        (q.pT_done, q.pT_ready, q.pv_done, q.rden_ready, q.att_ready, q.attT_done) = s.sems(
            "pT_done pT_ready pv_done rden_ready att_ready attT_done")
        (q.attT_hi, q.attT_lo, q.proj_done, q.base_ready, q.x1_ready, q.stats1_ready) = s.sems(
            "attT_hi attT_lo proj_done base_ready x1_ready stats1_ready")
        (q.moments1_ready, q.var1_ready, q.rstd1_ready, q.xn1_ready, q.xn1T_done) = s.sems(
            "moments1_ready var1_ready rstd1_ready xn1_ready xn1T_done")
        (q.xn1T_ready, q.logits_done, q.logits_ready, q.top_ready, q.top_at_ready) = s.sems(
            "xn1T_ready logits_done logits_ready top_ready top_at_ready")
        (q.gap_ready, q.gap_exp_ready, q.total_ready, q.rtotal_ready, q.weight_ready) = s.sems(
            "gap_ready gap_exp_ready total_ready rtotal_ready weight_ready")
        (q.weights_ready, q.chosen_at_ready, q.chosen_ready, q.either_ready) = s.sems(
            "weights_ready chosen_at_ready chosen_ready either_ready")
        (q.ranks_done, q.count_ready, q.rank_ready, q.ranked_ready, q.slot_f_ready) = s.sems(
            "ranks_done count_ready rank_ready ranked_ready slot_f_ready")
        (q.slot_ready, q.token_ready, q.table_written, q.slots_kept, q.counts_ready) = s.sems(
            "slot_ready token_ready table_written slots_kept counts_ready")
        q.mask_copied = s.sem("mask_copied")
        x_loaded = [s.sem(f"x_loaded{i}") for i in range(4)]
        x_reloaded = [s.sem(f"x_reloaded{i}") for i in range(4)]
        x1_stored = [s.sem(f"x1_stored{i}") for i in range(4)]
        xn1_stored = [s.sem(f"xn1_stored{i}") for i in range(4)]

        def rows(t):
            return bass.ds(t.round * P + t.slot * S, P)

        LOAD, MOMENTS, XN, QUERIES, SCORE, SHIFT, PROBS, ATTEND, ATT, PROJ, XN1, LOGITS, ROUTE, RANK = \
            0, 1, 2, 2, 2, 3, 3, 3, 4, 4, 5, 6, 6, 7
        DEPTH = 19
        turn_bank = Bank(NT, [("att", 11, q.attT_lo), ("xn", 3, q.xT_lo), ("xn1", 14, q.xn1T_ready)])
        q_bank = Bank(NT, [("queries", 5, q.q_lo), ("proj", 12, q.x1_ready)])
        pv_bank = Bank(NT, [("logits", 15, q.logits_ready), ("attend", 10, q.att_ready)])
        HALF = HEADS // KD
        block = s.block()

        @block.sync
        def _(sp):
            def load(t):
                if t.after(4):
                    sp.wait_ge(q.xn_ready, t.before(4))
                sp.dma_start(x[:, t.slot, :], a["x"][rows(t), :]).then_inc(x_loaded[t.slot], 16)

            def load_again(t):
                if t.after(4):
                    sp.wait_ge(q.base_ready, t.before(4))
                sp.dma_start(x_again[:, t.slot, :], a["x"][rows(t), :]).then_inc(x_reloaded[t.slot], 16)

            def store_x1(t):
                sp.wait_ge(q.x1_ready, t.count)
                sp.dma_start(k.x1[rows(t), :], x1[:, t.slot, :]).then_inc(x1_stored[t.slot], 16)

            def store_xn1(t):
                sp.wait_ge(q.xn1_ready, t.count)
                sp.dma_start(k.xn[rows(t), :], xn1[:, t.slot, :]).then_inc(xn1_stored[t.slot], 16)

            def body(at):
                run(at, (0, load), (9, load_again), (13, store_xn1), (12, store_x1))

            pipeline(sp, NT, DEPTH, 4, body)
            for i in range(4):
                sp.wait_ge(x1_stored[i], 16 * POS)
                sp.wait_ge(xn1_stored[i], 16 * POS)

        @block.gpsimd
        def _(pool):
            def shift(t):
                i = t.slot % 2
                pool.wait_ge(q.rowmax_ready, t.count)
                if t.after(2):
                    pool.wait_ge(q.probs_ready, t.before(2))
                pool.tensor_tensor(
                    shifted[:, i, :].rearrange("p (h n) -> p h n", n=KEYS),
                    w.masked[:, i, :].rearrange("p (h n) -> p h n", n=KEYS),
                    rowmax[:, i, :].unsqueeze(2).to_broadcast([P, PLACES, KEYS]),
                    ALU.subtract).then_inc(q.shifted_ready, 1)
                if t.slot >= 2:
                    wait_apart(pool, k, (q.shifted_ready, t.count))
                    pool.memset(w.masked[:, i, :], MASKED * HEAD ** 0.5).then_inc(q.refilled, 1)

            def residual(t):
                pool.wait_ge(x_reloaded[t.slot], t.round * 16 + 16)
                if t.after(2):
                    pool.wait_ge(q.x1_ready, t.before(2))
                pool.tensor_tensor(base[:, t.slot % 2, :], x_again[:, t.slot, :], w.bo[:, :],
                                   ALU.add).then_inc(q.base_ready, 1)

            def reciprocal_std(t, moments, var, std, shift, moments_ready, var_ready, rstd_ready, shift_ready):
                i = t.slot
                pool.wait_ge(moments_ready, t.count)
                pool.tensor_tensor(var[:, i:i + 1], moments[:, i, 1:2], k.eps[:, 0:1],
                                   ALU.add).then_inc(var_ready, 1)
                pool.wait_ge(var_ready, t.count)
                pool.tensor_tensor(std[:, i:i + 1], var[:, i:i + 1], k.neghalf[:, :],
                                   ALU.pow).then_inc(rstd_ready, 1)
                wait_apart(pool, k, (rstd_ready, t.count))
                pool.tensor_scalar(shift[:, i:i + 1], moments[:, i, 0:1], std[:, i:i + 1], -1.0,
                                   ALU.mult, ALU.mult).then_inc(shift_ready, 1)

            def rstd_x(t):
                reciprocal_std(t, moments, var_eps, rstd, shift_x, q.moments_ready, q.var_ready, q.rstd_ready,
                               q.shift_ready)

            def rstd_x1(t):
                reciprocal_std(t, moments1, var_eps1, rstd1, shift_x1, q.moments1_ready, q.var1_ready,
                               q.rstd1_ready, q.shift1_ready)

            def scatter(t):
                r, b = t.round, t.slot
                if b == 0:
                    if t.after(4):
                        pool.wait_ge(q.table_written, r * (16 * 2 * B))
                    pool.tensor_copy(token[:, :], w.token[:, bass.ds(r * B, B)]).then_inc(q.token_ready, 1)
                wait_apart(pool, k, (q.token_ready, r + 1), (q.slot_ready, r + 1))
                for c in range(2):
                    pool.indirect_dma_start(
                        out=k.table[:, :],
                        out_offset=bass.IndirectOffsetOnAxis(ap=slot[:, 2 * b + c:2 * b + c + 1], axis=0),
                        in_=token[:, b:b + 1], in_offset=None).then_inc(q.table_written, 16)

            def body(at):
                run(at, (2, rstd_x), (11, residual), (7, shift), (12, rstd_x1), (19, scatter))

            pipeline(pool, NT, DEPTH, 4, body)
            pool.wait_ge(q.table_written, NT * 2 * 16)

        @block.tensor
        def _(pe):
            def turn(of, done):
                for c in range(KD):
                    mm = pe.transpose(turn_ps[:, c * P:(c + 1) * P], of[:, c * P:(c + 1) * P], k.ident[:, :])
                mm.then_inc(done, 1)

            def turn_att(t):
                pe.wait_ge(q.att_ready, t.count)
                if turn_bank.used("att", t):
                    pe.wait_ge(*turn_bank.freed("att", t))
                turn(att[:, t.slot % 2, :], q.attT_done)

            def turn_xn(t):
                pe.wait_ge(q.xn_ready, t.count)
                if turn_bank.used("xn", t):
                    pe.wait_ge(*turn_bank.freed("xn", t))
                turn(xn[:, t.slot % 2, :], q.xT_done)

            def turn_xn1(t):
                pe.wait_ge(q.xn1_ready, t.count)
                if turn_bank.used("xn1", t):
                    pe.wait_ge(*turn_bank.freed("xn1", t))
                turn(xn1[:, t.slot, :], q.xn1T_done)

            def turn_probs(t):
                i = t.slot % 2
                pe.wait_ge(q.probs_ready, t.count)
                for group in range(3):
                    if group == 0 and t.after(1):
                        pe.wait_ge(q.pT_ready, t.index * 3)
                    if group == 2:
                        pe.wait_ge(q.pT_ready, t.index * 3 + 1)
                    for c in range(4 * group, min(4 * group + 4, PCH)):
                        mm = pe.transpose(pT_ps[:, group % 2, (c % 4) * P:(c % 4 + 1) * P],
                                          probs[:, i, c * P:(c + 1) * P], k.ident[:, :])
                    mm.then_inc(q.pT_done, 1)

            def queries(t):
                i = t.slot % 2
                pe.wait_ge(q.xT_lo, t.count)
                if q_bank.used("queries", t):
                    pe.wait_ge(*q_bank.freed("queries", t))
                for c in range(KD):
                    for kk in range(KD):
                        mm = three_passes(
                            pe, q_ps[:, c * P:(c + 1) * P],
                            [part[:, kk, c * P:(c + 1) * P] for part in w.wq],
                            [part[:, i, kk * P:(kk + 1) * P] for part in xT],
                            start=(kk == 0 and c == 0), stop=(kk == KD - 1))
                mm.then_inc(q.q_done, 1)

            def attend(t):
                i = t.slot % 2
                pe.wait_ge(q.pT_ready, t.index * 3 + 3)
                if pv_bank.used("attend", t):
                    pe.wait_ge(*pv_bank.freed("attend", t))
                wait_ranks(t, -5)
                for c in range(PCH):
                    h, n = chunk_heads(c)
                    mm = pe.matmul(pv_ps[:, h * VW:(h + n) * VW], probsT[:, i, c * P:(c + 1) * P],
                                   w.values[:, t.slot, c, 0:n * VW], start=(c == 0), stop=(c == PCH - 1),
                                   skip_group_check=True)
                mm.then_inc(q.pv_done, 1)

            def project(t):
                i = t.slot % 2
                pe.wait_ge(q.attT_lo, t.count)
                if q_bank.used("proj", t):
                    pe.wait_ge(*q_bank.freed("proj", t))
                for kk in range(KD):
                    mm = three_passes(pe, q_ps[:, 0:D],
                                      [part[:, i, kk * P:(kk + 1) * P] for part in attT],
                                      [part[:, kk, :] for part in w.wo],
                                      start=(kk == 0), stop=(kk == KD - 1))
                mm.then_inc(q.proj_done, 1)

            def score(t):
                i = t.slot % 2
                pe.wait_ge(q.q_lo, t.count)
                if t.after(1):
                    pe.wait_ge(q.masked_ready, t.before(1))
                for bank in range(3):
                    for c in range(KD):
                        h0 = max(bank * PER_BANK, c * HALF)
                        h1 = min((bank + 1) * PER_BANK, (c + 1) * HALF)
                        if h0 < h1:
                            o = (h0 - bank * PER_BANK) * KEYS
                            r = (h0 - c * HALF) * KEYS
                            n = (h1 - h0) * KEYS
                            mm = three_passes(
                                pe, scores[:, bank, o:o + n],
                                [part[:, i, c * P:(c + 1) * P] for part in qT],
                                [part[:, t.slot, c, r:r + n] for part in w.keys],
                                start=(o == 0), stop=True)
                mm.then_inc(q.scores_done, 1)

            def wait_ranks(t, ahead):
                rounds = t.round + (t.slot + ahead) // 4
                if not isinstance(rounds, int) or rounds > 0:
                    pe.wait_ge(q.count_ready, rounds)

            def gate_logits(t):
                i = t.slot % 2
                pe.wait_ge(q.xn1T_ready, t.count)
                if pv_bank.used("logits", t):
                    pe.wait_ge(*pv_bank.freed("logits", t))
                wait_ranks(t, -1)
                for kk in range(KD):
                    mm = pe.matmul(pv_ps[:, 0:E], xn1T[:, i, kk * P:(kk + 1) * P], w.gate[:, kk, :],
                                   start=(kk == 0), stop=(kk == KD - 1))
                mm.then_inc(q.logits_done, 1)

            def ranks(t):
                if t.slot != 3:
                    return
                pe.wait_ge(q.either_ready, t.round + 1)
                pe.wait_ge(*pv_bank.freed("attend", t, 16))
                mask = either[:, :, :].rearrange("p b e -> p (b e)")
                pe.matmul(pv_ps[:, 0:4 * E], w.upper[:, :], mask, start=True, stop=True,
                          skip_group_check=True)
                pe.matmul(pv_ps[:, 4 * E:8 * E], w.ones[:, :], mask, start=False, stop=True,
                          skip_group_check=True).then_inc(q.ranks_done, 1)

            def body(at):
                run(at, (11, turn_att), (5, queries), (15, gate_logits), (3, turn_xn), (12, project), (10, turn_probs), (6, score), (14, turn_xn1), (16, ranks), (10, attend))

            pipeline(pe, NT, DEPTH, 4, body)

        @block.scalar
        def _(act):
            def normalise_x(t):
                act.wait_ge(q.shift_ready, t.count)
                if t.after(2):
                    act.wait_ge(q.xT_done, t.before(2))
                act.activation(xn[:, t.slot % 2, :], x[:, t.slot, :], ACT.Identity,
                               scale=rstd[:, t.slot:t.slot + 1], bias=shift_x[:, t.slot:t.slot + 1]).then_inc(q.xn_ready, 1)

            def normalise_x1(t):
                i = t.slot
                act.wait_ge(q.shift1_ready, t.count)
                if t.after(4):
                    act.wait_ge(xn1_stored[i], t.round * 16)
                    act.wait_ge(q.xn1T_done, t.before(4))
                act.activation(xn1[:, i, :], x1[:, i, :], ACT.Identity, scale=rstd1[:, i:i + 1],
                               bias=shift_x1[:, i:i + 1]).then_inc(q.xn1_ready, 1)

            def att_hi(t):
                if t.after(2):
                    act.wait_ge(q.proj_done, t.before(2))
                act.wait_ge(q.attT_done, t.count)
                act.activation(attT[0][:, t.slot % 2, :], turn_ps[:, 0:D], ACT.Copy).then_inc(q.attT_hi, 1)

            def xn_hi(t):
                if t.after(2):
                    act.wait_ge(q.q_done, t.before(2))
                act.wait_ge(q.xT_done, t.count)
                act.activation(xT[0][:, t.slot % 2, :], turn_ps[:, 0:D], ACT.Copy).then_inc(q.xT_hi, 1)

            def exponent(t):
                i = t.slot % 2
                act.wait_ge(q.shifted_ready, t.count)
                if t.after(2):
                    act.wait_ge(q.pT_done, t.index * 3 - 3)
                act.activation(probs[:, i, :], shifted[:, i, 0:PCH * P], ACT.Exp,
                               scale=HEAD ** -0.5).then_inc(q.probs_ready, 1)

            def copy_probsT(t):
                i = t.slot % 2
                if t.after(2):
                    act.wait_ge(q.pv_done, t.before(2))
                for group in range(3):
                    n = min(4, PCH - 4 * group) * P
                    act.wait_ge(q.pT_done, t.index * 3 + group + 1)
                    act.activation(probsT[:, i, group * BANK:group * BANK + n], pT_ps[:, group % 2, 0:n],
                                   ACT.Copy).then_inc(q.pT_ready, 1)

            def q_hi(t):
                i = t.slot % 2
                if t.after(2):
                    act.wait_ge(q.scores_done, t.before(2))
                act.wait_ge(q.q_done, t.count)
                for c in range(KD):
                    cols = slice(c * P, (c + 1) * P)
                    ins = act.activation(qT[0][:, i, cols], q_ps[:, cols], ACT.Identity,
                                         bias=w.bq[:, c:c + 1])
                ins.then_inc(q.q_hi, 1)

            def copy_xn1T(t):
                if t.after(2):
                    act.wait_ge(q.logits_done, t.before(2))
                act.wait_ge(q.xn1T_done, t.count)
                act.activation(xn1T[:, t.slot % 2, :], turn_ps[:, 0:D], ACT.Copy).then_inc(q.xn1T_ready, 1)

            def gap_exponent(t):
                if t.slot == 3:
                    act.wait_ge(q.gap_ready, t.round + 1)
                    act.activation(gap_exp[:, :], gap[:, :], ACT.Exp).then_inc(q.gap_exp_ready, 1)

            def body(at):
                run(at, (3, normalise_x), (14, normalise_x1), (11, att_hi), (9, exponent), (5, q_hi), (3, xn_hi), (10, copy_probsT), (14, copy_xn1T), (15, gap_exponent))

            pipeline(act, NT, DEPTH, 4, body)

        @block.vector
        def _(dve):
            def normalise_att(t):
                i = t.slot % 2
                dve.wait_ge(q.pv_done, t.count)
                pv = pv_ps[:, 0:HEADS * VW].rearrange("p (h n) -> p h n", n=VW)
                dve.reciprocal(rden[:, i, :], pv[:, :, HEAD]).then_inc(q.rden_ready, 1)
                dve.wait_ge(q.rden_ready, t.count)
                if t.after(2):
                    dve.wait_ge(q.attT_done, t.before(2))
                dve.tensor_tensor(att[:, i, :].rearrange("p (h n) -> p h n", n=HEAD), pv[:, :, 0:HEAD],
                                  rden[:, i, :].unsqueeze(2).to_broadcast([P, HEADS, HEAD]),
                                  ALU.mult).then_inc(q.att_ready, 1)

            def att_lo(t):
                i = t.slot % 2
                dve.wait_ge(q.attT_hi, t.count)
                dve.tensor_tensor(attT[1][:, i, :], turn_ps[:, 0:D], attT[0][:, i, :].bitcast(F32),
                                  ALU.subtract).then_inc(q.attT_lo, 1)

            def xn_lo(t):
                i = t.slot % 2
                dve.wait_ge(q.xT_hi, t.count)
                dve.tensor_tensor(xT[1][:, i, :], turn_ps[:, 0:D], xT[0][:, i, :].bitcast(F32),
                                  ALU.subtract).then_inc(q.xT_lo, 1)

            def q_lo(t):
                i = t.slot % 2
                dve.wait_ge(q.q_hi, t.count)
                for c in range(KD):
                    cols = slice(c * P, (c + 1) * P)
                    ins = dve.scalar_tensor_tensor(out=qT[1][:, i, cols], in0=q_ps[:, cols],
                                                   scalar=w.bq[:, c:c + 1],
                                                   in1=qT[0][:, i, cols].bitcast(F32),
                                                   op0=ALU.add, op1=ALU.subtract)
                ins.then_inc(q.q_lo, 1)

            def add_residual(t):
                i = t.slot
                dve.wait_ge(q.proj_done, t.count)
                dve.wait_ge(q.base_ready, t.count)
                if t.after(4):
                    dve.wait_ge(x1_stored[i], t.round * 16)
                    dve.wait_ge(q.xn1_ready, t.before(4))
                dve.tensor_tensor(x1[:, i, :], q_ps[:, 0:D], base[:, i % 2, :],
                                  ALU.add).then_inc(q.x1_ready, 1)

            def x1_moments(t):
                i = t.slot
                dve.wait_ge(q.x1_ready, t.count)
                dve.bn_stats(stats1[:, i, :], x1[:, i, :]).then_inc(q.stats1_ready, 1)
                wait_apart(dve, k, (q.stats1_ready, t.count))
                dve.bn_aggr(moments1[:, i, :], stats1[:, i, :]).then_inc(q.moments1_ready, 1)

            def mask_scores(t):
                i = t.slot % 2
                if t.slot == 0:
                    dve.tensor_copy(mask_now[:, :], w.mask[:, bass.ds(t.round * KEYS, KEYS)]
                                    ).then_inc(q.mask_copied, 1)
                waits = [(q.scores_done, t.count), (q.mask_copied, t.round + 1)]
                if t.after(2) and t.slot >= 2:
                    waits.append((q.shifted_ready, t.before(2)))
                elif t.after(4):
                    waits.append((q.refilled, t.round * 2 - (1 - t.slot)))
                wait_apart(dve, k, *waits)
                for bank in range(3):
                    ins = dve.copy_predicated(
                        w.masked[:, i, bank * GROUP:(bank + 1) * GROUP].rearrange("p (h n) -> p h n", n=KEYS),
                        mask_now[:, :].unsqueeze(1).to_broadcast([P, PER_BANK, KEYS]), scores[:, bank, 0:GROUP].rearrange("p (h n) -> p h n", n=KEYS))
                ins.then_inc(q.masked_ready, 1)

            def row_maxima(t):
                i = t.slot % 2
                dve.wait_ge(q.masked_ready, t.count)
                if t.after(2):
                    dve.wait_ge(q.shifted_ready, t.before(2))
                dve.tensor_reduce(rowmax[:, i, :], w.masked[:, i, :].rearrange("p (h n) -> p h n", n=KEYS),
                                  AX.X, ALU.max).then_inc(q.rowmax_ready, 1)

            def x_moments(t):
                i = t.slot
                dve.wait_ge(x_loaded[i], t.round * 16 + 16)
                dve.bn_stats(stats[:, i, :], x[:, i, :]).then_inc(q.stats_ready, 1)
                wait_apart(dve, k, (q.stats_ready, t.count))
                dve.bn_aggr(moments[:, i, :], stats[:, i, :]).then_inc(q.moments_ready, 1)

            def top_two(t):
                i = t.slot
                dve.wait_ge(q.logits_done, t.count)
                dve.tensor_copy(logits[:, i, :], pv_ps[:, 0:E]).then_inc(q.logits_ready, 1)
                wait_apart(dve, k, (q.logits_ready, t.count))
                dve.max(top[:, i, :], logits[:, i, :]).then_inc(q.top_ready, 1)
                wait_apart(dve, k, (q.top_ready, t.count))
                dve.max_index(top_at[:, i, :], top[:, i, :], logits[:, i, :]).then_inc(q.top_at_ready, 1)

            def route(t):
                if t.slot != 3:
                    return
                r = t.round
                dve.wait_ge(q.top_at_ready, t.count)
                if t.after(4):
                    dve.wait_ge(q.gap_exp_ready, r)
                dve.tensor_tensor(gap[:, :], top[:, :, 1], top[:, :, 0], ALU.subtract).then_inc(q.gap_ready, 1)
                dve.tensor_copy(chosen_at[:, :, :], top_at[:, :, 0:2]).then_inc(q.chosen_at_ready, 1)
                dve.wait_ge(q.chosen_at_ready, r + 1)
                dve.tensor_tensor(chosen[:, :, :, :].rearrange("p b c e -> p (b c) e"),
                                  k.iota8[:, :].unsqueeze(1).to_broadcast([P, 2 * B, E]),
                                  chosen_at[:, :, :].rearrange("p b c -> p (b c)").unsqueeze(2)
                                  .to_broadcast([P, 2 * B, E]), ALU.is_equal).then_inc(q.chosen_ready, 1)
                dve.wait_ge(q.chosen_ready, r + 1)
                if t.after(4):
                    dve.wait_ge(q.ranks_done, r)
                dve.tensor_tensor(either[:, :, :], chosen[:, :, 0, :], chosen[:, :, 1, :],
                                  ALU.add).then_inc(q.either_ready, 1)
                dve.wait_ge(q.gap_exp_ready, r + 1)
                dve.tensor_scalar(total[:, :], gap_exp[:, :], 1.0, None, ALU.add).then_inc(q.total_ready, 1)
                dve.wait_ge(q.total_ready, r + 1)
                dve.reciprocal(rtotal[:, :], total[:, :]).then_inc(q.rtotal_ready, 1)
                dve.wait_ge(q.rtotal_ready, r + 1)
                here = k.weights[:, bass.ds(r * (2 * B), 2 * B)].rearrange("p (b c) -> p b c", c=2)
                dve.tensor_scalar(here[:, :, 0], rtotal[:, :], k.tanh_g[:, 1:2], None,
                                  ALU.mult).then_inc(q.weight_ready, 1)
                dve.scalar_tensor_tensor(out=here[:, :, 1], in0=gap_exp[:, :], scalar=k.tanh_g[:, 1:2],
                                         in1=rtotal[:, :], op0=ALU.mult, op1=ALU.mult
                                         ).then_inc(q.weights_ready, 1)

            def place(t):
                if t.slot != 3:
                    return
                r = t.round
                dve.tensor_copy(k.count[:, 0, :], k.count[:, B, :]).then_inc(q.counts_ready, 1)
                dve.wait_ge(q.ranks_done, r + 1)
                for b in range(B):
                    dve.wait_ge(q.counts_ready, r * (B + 1) + (b + 1))
                    dve.tensor_tensor(k.count[:, b + 1, :], k.count[:, b, :],
                                      pv_ps[:, (4 + b) * E:(5 + b) * E], ALU.add).then_inc(q.counts_ready, 1)
                dve.wait_ge(q.counts_ready, (r + 1) * (B + 1))
                dve.tensor_tensor(rank[:, :, :], k.count[:, 0:B, :],
                                  pv_ps[:, 0:4 * E].rearrange("p (b e) -> p b e", e=E),
                                  ALU.add).then_inc(q.count_ready, 1)
                dve.wait_ge(q.count_ready, r + 1)
                dve.tensor_tensor(ranked[:, :, :, :], chosen[:, :, :, :],
                                  rank[:, :, :].unsqueeze(2).to_broadcast([P, B, 2, E]),
                                  ALU.mult).then_inc(q.ranked_ready, 1)
                dve.wait_ge(q.ranked_ready, r + 1)
                dve.tensor_reduce(slot_f[:, :, :], ranked[:, :, :, :], AX.X, ALU.add
                                  ).then_inc(q.slot_f_ready, 1)
                dve.wait_ge(q.slot_f_ready, r + 1)
                if t.after(4):
                    dve.wait_ge(q.table_written, r * (16 * 2 * B))
                dve.tensor_copy(slot[:, :], slot_f[:, :, :].rearrange("p b c -> p (b c)")
                                ).then_inc(q.slot_ready, 1)
                dve.tensor_copy(k.slots[:, bass.ds(r * (2 * B), 2 * B)],
                                slot_f[:, :, :].rearrange("p b c -> p (b c)")).then_inc(q.slots_kept, 1)

            def body(at):
                run(at, (11, normalise_att), (7, mask_scores), (11, att_lo), (5, q_lo), (7, row_maxima), (12, add_residual), (12, x1_moments), (3, xn_lo), (1, x_moments), (15, top_two), (16, place), (15, route))

            pipeline(dve, NT, DEPTH, 4, body)


def plan_tiles(nc, k):
    with Scope(nc, "plan") as s:
        W = POS * 2 * B
        counts = s.sb("counts", [P, E])
        upped = s.sb("upped", [P, E], I32)
        filled_i = s.sb("filled_i", [P, E], I32)
        sizes = s.sb("sizes", [P, E + 1])
        ends = s.sb("ends", [P, E + 1])
        tile = s.sb("tile", [1, TILES])
        passed = s.sb("passed", [1, TILES, E + 1])
        passed_sizes = s.sb("passed_sizes", [1, TILES, E + 1])
        expert = s.sb("expert", [1, TILES])
        start = s.sb("start", [1, TILES])
        local = s.sb("local", [1, TILES])
        row = s.sb("row", [1, TILES])
        is_shared = s.sb("is_shared", [1, TILES])
        region = s.sb("region", [P, E])
        step = s.sb("step", [P, E])
        at_least = s.sb("at_least", [P, W, E])
        steps = s.sb("steps", [P, W, E])
        moved = s.sb("moved", [P, W])
        table_rows = s.sb("table_rows", [P, W])
        numbered = s.sem("numbered")
        chain = s.sem("chain")
        block = s.block()

        @block.gpsimd
        def _(pool):
            pool.iota(tile[:, :], [[1, TILES]], base=0, channel_multiplier=0,
                      allow_small_or_imprecise_dtypes=True).then_inc(numbered, 1)

        @block.vector
        def _(dve):
            dve.scalar_tensor_tensor(out=counts[:, :], in0=k.iota8[:, :], scalar=-float(T),
                                     in1=k.count[:, B, :], op0=ALU.mult, op1=ALU.add).then_inc(chain, 1)
            dve.wait_ge(chain, 1)
            dve.tensor_scalar(upped[:, :], counts[:, :], float(P - 1), None, ALU.add).then_inc(chain, 1)
            dve.wait_ge(chain, 2)
            dve.tensor_scalar(filled_i[:, :], upped[:, :], 7, None,
                              ALU.logical_shift_right).then_inc(chain, 1)
            dve.memset(sizes[:, 0:1], float(NT)).then_inc(chain, 1)
            dve.memset(ends[:, 0:1], float(NT)).then_inc(chain, 1)
            dve.wait_ge(chain, 5)
            dve.tensor_copy(sizes[:, 1:E + 1], filled_i[:, :]).then_inc(chain, 1)
            for e in range(E):
                dve.wait_ge(chain, 6 + e)
                dve.tensor_tensor(ends[:, e + 1:e + 2], ends[:, e:e + 1], sizes[:, e + 1:e + 2],
                                  ALU.add).then_inc(chain, 1)
            n = 6 + E
            dve.wait_ge(chain, n)
            dve.wait_ge(numbered, 1)
            dve.tensor_tensor(passed[:, :, :], ends[0:1, :].unsqueeze(1).to_broadcast([1, TILES, E + 1]),
                              tile[:, :].unsqueeze(2).to_broadcast([1, TILES, E + 1]),
                              ALU.is_le).then_inc(chain, 1)
            dve.tensor_scalar(region[:, :], k.iota8[:, :], float(T), None, ALU.mult).then_inc(chain, 1)
            dve.tensor_scalar(step[:, :], sizes[:, 0:E], float(P), -float(T), ALU.mult,
                              ALU.add).then_inc(chain, 1)
            dve.tensor_copy(table_rows[:, :], k.slots[:, :]).then_inc(chain, 1)
            dve.wait_ge(chain, n + 4)
            dve.tensor_reduce(expert[:, :], passed[:, :, :], AX.X, ALU.add).then_inc(chain, 1)
            dve.tensor_tensor(passed_sizes[:, :, :], passed[:, :, :],
                              sizes[0:1, :].unsqueeze(1).to_broadcast([1, TILES, E + 1]),
                              ALU.mult).then_inc(chain, 1)
            dve.tensor_scalar(step[:, 0:1], step[:, 0:1], float(T), None, ALU.add).then_inc(chain, 1)
            dve.tensor_tensor(at_least[:, :, :], table_rows[:, :].unsqueeze(2).to_broadcast([P, W, E]),
                              region[:, :].unsqueeze(1).to_broadcast([P, W, E]),
                              ALU.is_ge).then_inc(chain, 1)
            dve.wait_ge(chain, n + 8)
            dve.tensor_reduce(start[:, :], passed_sizes[:, :, :], AX.X, ALU.add).then_inc(chain, 1)
            dve.tensor_scalar(is_shared[:, :], expert[:, :], 0.0, float(SHARED + T), ALU.is_equal,
                              ALU.mult).then_inc(chain, 1)
            dve.tensor_tensor(steps[:, :, :], at_least[:, :, :],
                              step[:, :].unsqueeze(1).to_broadcast([P, W, E]), ALU.mult).then_inc(chain, 1)
            dve.wait_ge(chain, n + 11)
            dve.tensor_tensor(local[:, :], tile[:, :], start[:, :], ALU.subtract).then_inc(chain, 1)
            dve.scalar_tensor_tensor(out=row[:, :], in0=expert[:, :], scalar=float(T), in1=is_shared[:, :],
                                     op0=ALU.mult, op1=ALU.add).then_inc(chain, 1)
            dve.tensor_reduce(moved[:, :], steps[:, :, :], AX.X, ALU.add).then_inc(chain, 1)
            dve.wait_ge(chain, n + 14)
            dve.scalar_tensor_tensor(out=row[:, :], in0=local[:, :], scalar=float(P), in1=row[:, :],
                                     op0=ALU.mult, op1=ALU.add).then_inc(chain, 1)
            dve.tensor_tensor(k.slots[:, :], table_rows[:, :], moved[:, :], ALU.add).then_inc(chain, 1)
            dve.wait_ge(chain, n + 16)
            dve.memset(k.plan[:, :, 0:1], 0).then_inc(chain, 1)
            dve.tensor_scalar(k.plan[:, 0, 1:], row[:, :], -float(T), None, ALU.add).then_inc(chain, 1)
            dve.tensor_scalar(k.plan[:, 1, 1:], expert[:, :], float(E), None, ALU.min).then_inc(chain, 1)


def expert_tiles(nc, a, k):
    with Scope(nc, "expert") as s:
        w1 = s.sb("w1", [P, (E + 1) * KD * H0])
        w2 = s.sb("w2", [P, (E + 1) * KD * H0])
        w3 = s.sb("w3", [P, (E + 1) * (H0 // P) * D])
        ids = s.sb("ids", [P, 4], I32)
        x = s.sb("x", [P, 4, D])
        xT = s.sb("xT", [P, 2, D])
        act_h = s.sb("act_h", [P, 2, H0])
        gated = s.sb("gated", [P, 2, H0])
        gatedT = s.sb("gatedT", [P, 2, H0])
        y = s.sb("y", [P, 4, D])
        x_ps = s.ps("x_ps", [P, BANK])
        h1_ps = s.ps("h1_ps", [P, 2, BANK])
        h2_ps = s.ps("h2_ps", [P, 2, BANK])
        g_ps = s.ps("g_ps", [P, BANK])
        y_ps = s.ps("y_ps", [P, 2, BANK])
        shared_loaded = s.sem("shared_loaded")
        experts_loaded = s.sem("experts_loaded")
        ids_loaded = [s.sem(f"ids_loaded{i}") for i in range(4)]
        x_gathered = [s.sem(f"x_gathered{i}") for i in range(4)]
        y_stored = [s.sem(f"y_stored{i}") for i in range(4)]
        q = Named()
        (q.turned, q.copied, q.h1_done, q.h2_done, q.act_ready, q.gated_ready) = s.sems(
            "turned copied h1_done h2_done act_ready gated_ready")
        (q.g_turned, q.g_copied, q.y_done, q.y_ready) = s.sems(
            "g_turned g_copied y_done y_ready")
        IDS, GATHER, TURN, HIDDEN, GATED, OUT = 0, 1, 3, 4, 5, 5
        STORE = 5
        DEPTH = 5
        block = s.block()

        def plan_at(eng, which, t, top):
            return eng.value_load(k.plan[0:1, which, bass.ds(t.index + 1, 1)], min_val=0, max_val=top)

        @block.sync
        def _(sp):
            for to, of, chunks, sem in ((w1, a["L0_ffn_sw1"], KD, shared_loaded),
                                        (w2, a["L0_ffn_sw2"], KD, shared_loaded),
                                        (w3, a["L0_ffn_sw3"], H0 // P, shared_loaded)):
                n = chunks * of.shape[1]
                sp.dma_start(to[:, 0:n].rearrange("p (c n) -> p c n", c=chunks),
                             of.rearrange("(c p) n -> p c n", p=P)).then_inc(sem, 16)

            def load_ids(t):
                row = plan_at(sp, 0, t, ROWS - P)
                if t.after(4):
                    wait_apart(sp, k, (x_gathered[t.slot], t.round * 16))
                sp.dma_start(ids[:, t.slot:t.slot + 1], k.table[bass.ds(row, P), :]
                             ).then_inc(ids_loaded[t.slot], 16)

            def store(t):
                sp.wait_ge(q.y_ready, t.count)
                sp.dma_start(k.y[bass.ds(t.index * P, P), :], y[:, t.slot, :]).then_inc(y_stored[t.slot], 16)

            pipeline(sp, TILES, DEPTH, 4, lambda at: run(at, (IDS, load_ids), (STORE, store)))
            for i in range(4):
                sp.wait_ge(y_stored[i], 16 * (TILES // 4))

        @block.gpsimd
        def _(pool):
            for e in range(E):
                for to, of, chunks in ((w1, a["L0_ffn_ew1"], KD), (w2, a["L0_ffn_ew2"], KD),
                                       (w3, a["L0_ffn_ew3"], H0 // P)):
                    n = chunks * of.shape[2]
                    pool.dma_start(to[:, (e + 1) * n:(e + 2) * n].rearrange("p (c n) -> p c n", c=chunks),
                                   of[e].rearrange("(c p) n -> p c n", p=P)).then_inc(experts_loaded, 16)

            def gather(t):
                i = t.slot
                waits = [(ids_loaded[i], t.round * 16 + 16)]
                if t.after(4):
                    waits.append((q.turned, t.before(4)))
                wait_apart(pool, k, *waits)
                pool.indirect_dma_start(
                    out=x[:, i, :], out_offset=None, in_=k.xn[:, :],
                    in_offset=bass.IndirectOffsetOnAxis(ap=ids[:, i:i + 1], axis=0)
                    ).then_inc(x_gathered[i], 16)

            pipeline(pool, TILES, DEPTH, 4, lambda at: run(at, (GATHER, gather)))

        @block.tensor
        def _(pe):
            pe.wait_ge(shared_loaded, 16 * 3)

            def turn_x(t):
                pe.wait_ge(x_gathered[t.slot], t.round * 16 + 16)
                if t.after(1):
                    pe.wait_ge(q.copied, t.before(1))
                for c in range(KD):
                    mm = pe.transpose(x_ps[:, c * P:(c + 1) * P], x[:, t.slot, c * P:(c + 1) * P],
                                      k.ident[:, :])
                mm.then_inc(q.turned, 1)

            def hidden(t):
                i = t.slot % 2
                pe.wait_ge(q.copied, t.count)
                expert = experts[t.slot + 1]
                for w, out, done, free in ((w1, h1_ps, q.h1_done, q.act_ready),
                                           (w2, h2_ps, q.h2_done, q.gated_ready)):
                    if t.after(2):
                        pe.wait_ge(free, t.before(2))
                    for c in range(KD):
                        mm = pe.matmul(out[:, i, :], xT[:, i, c * P:(c + 1) * P],
                                       w[:, bass.ds(expert * (KD * H0) + c * H0, H0)],
                                       start=(c == 0), stop=(c == KD - 1))
                    mm.then_inc(done, 1)

            def turn_gated(t):
                i = t.slot % 2
                pe.wait_ge(q.gated_ready, t.count)
                if t.after(1):
                    pe.wait_ge(q.g_copied, t.before(1))
                for c in range(H0 // P):
                    mm = pe.transpose(g_ps[:, c * P:(c + 1) * P], gated[:, i, c * P:(c + 1) * P],
                                      k.ident[:, :])
                mm.then_inc(q.g_turned, 1)

            def out(t):
                i = t.slot % 2
                expert = experts[(t.slot + 1) % 4]
                pe.wait_ge(q.g_copied, t.count)
                if t.after(2):
                    pe.wait_ge(q.y_ready, t.before(2))
                for c in range(H0 // P):
                    mm = pe.matmul(y_ps[:, i, 0:D], gatedT[:, i, c * P:(c + 1) * P],
                                   w3[:, bass.ds(expert * (H0 // P * D) + c * D, D)],
                                   start=(c == 0), stop=(c == H0 // P - 1))
                mm.then_inc(q.y_done, 1)

            experts = [None] * 5

            def body(at):
                t = at(HIDDEN)
                if t and t.slot == 0:
                    _, experts[:] = nc.values_load_multi_w_load_instructions(
                        k.plan[0:1, 1, bass.ds(t.round * 4, 5)], engines=[mybir.EngineType.PE],
                        min_val=0, max_val=E)
                elif not t:
                    experts[0] = experts[4]
                run(at, (GATED, turn_gated), (HIDDEN, hidden), (OUT, out), (TURN, turn_x))

            pipeline(pe, TILES, DEPTH, 4, body,
                     pause=(NT, lambda: pe.wait_ge(experts_loaded, 16 * 3 * E)))

        @block.scalar
        def _(act):
            def copy_x(t):
                act.wait_ge(q.turned, t.count)
                if t.after(2):
                    act.wait_ge(q.h2_done, t.before(2))
                act.activation(xT[:, t.slot % 2, :], x_ps[:, 0:D], ACT.Copy).then_inc(q.copied, 1)

            def silu(t):
                i = t.slot % 2
                act.wait_ge(q.h1_done, t.count)
                if t.after(2):
                    act.wait_ge(q.gated_ready, t.before(2))
                act.activation(act_h[:, i, :], h1_ps[:, i, :], ACT.Silu).then_inc(q.act_ready, 1)

            def copy_gated(t):
                i = t.slot % 2
                act.wait_ge(q.g_turned, t.count)
                if t.after(2):
                    act.wait_ge(q.y_done, t.before(2))
                act.activation(gatedT[:, i, :], g_ps[:, :], ACT.Copy).then_inc(q.g_copied, 1)

            pipeline(act, TILES, DEPTH, 4,
                     lambda at: run(at, (GATED, copy_gated), (HIDDEN, silu), (TURN, copy_x)))

        @block.vector
        def _(dve):
            def gate(t):
                i = t.slot % 2
                dve.wait_ge(q.h2_done, t.count)
                dve.wait_ge(q.act_ready, t.count)
                if t.after(2):
                    dve.wait_ge(q.g_turned, t.before(2))
                dve.tensor_tensor(gated[:, i, :], h2_ps[:, i, :], act_h[:, i, :],
                                  ALU.mult).then_inc(q.gated_ready, 1)

            def copy_y(t):
                dve.wait_ge(q.y_done, t.count)
                if t.after(4):
                    dve.wait_ge(y_stored[t.slot], t.round * 16)
                dve.tensor_copy(y[:, t.slot, :], y_ps[:, t.slot % 2, 0:D]).then_inc(q.y_ready, 1)

            pipeline(dve, TILES, DEPTH, 4, lambda at: run(at, (HIDDEN, gate), (OUT, copy_y)))


def prepare_causal(nc, a, k, w):
    with Scope(nc, "prep3") as s:
        q_w = s.sb("q_w", [P, KD, D])
        k_w = s.sb("k_w", [P, KD, D])
        gate_raw = s.sb("gate_raw", [P, KD, D])
        ctxT = s.sb("ctxT", [P, KD, B * EVEN])
        qk_ps = s.ps("qk_ps", [P, KD, D])
        loaded = s.sem("loaded")
        padded = s.sem("padded")
        product_done = s.sem("product_done")
        hi_ready = s.sem("hi_ready")
        qk_hi_ready = s.sem("qk_hi_ready")
        prepared = s.sem("prepared")
        loads = [
            (q_w[:, :, :], a["L1_xattn_q_w"].rearrange("(k p) n -> p k n", p=P)),
            (k_w[:, :, :], a["L1_xattn_k_w"].rearrange("(k p) n -> p k n", p=P)),
            (gate_raw[:, :, :], a["L1_xattn_gate_w"].rearrange("(k p) n -> p k n", p=P)),
            *((ctxT[:, kk, :].rearrange("p (b n) -> p b n", n=EVEN)[:, :, 0:KEYS],
               a["ctxT"][kk * P:(kk + 1) * P, :, :]) for kk in range(KD)),
            (w.ctx[:, :].rearrange("n (b d) -> n b d", d=D), a["ctx"].rearrange("b n d -> n b d")),
            (w.norm_w[:, :], a["L1_xattn_norm_w"].partition_broadcast(P)),
            (w.gate_b[:, :], a["L1_xattn_gate_b"].partition_broadcast(P)),
            (w.above[:, :], a["c_above"]),
            (w.gate8[:, :, :], a["L1_ffn_gate_W"].rearrange("(k p) n -> p k n", p=P)),
            (w.route_scale[:, :], a["L1_ffn_route_scale"].partition_broadcast(P)),
        ]
        block = s.block()

        @block.sync
        def _(sp):
            for to, of in loads:
                sp.dma_start(to, of).then_inc(loaded, 16)

        @block.gpsimd
        def _(pool):
            pool.memset(ctxT[:, :, :].rearrange("p k (b n) -> p k b n", n=EVEN)[:, :, :, KEYS:EVEN], 0.0
                        ).then_inc(padded, 1)
            pool.memset(w.neg_scale[:, :], -D ** -0.5).then_inc(prepared, 1)

        @block.tensor
        def _(pe):
            pe.wait_ge(loaded, 16 * len(loads))
            for c in range(KD):
                for kk in range(KD):
                    mm = pe.matmul(qk_ps[:, c, :], q_w[:, kk, c * P:(c + 1) * P], k_w[:, kk, :],
                                   start=(kk == 0 and c == 0), stop=(kk == KD - 1), skip_group_check=True)
            mm.then_inc(product_done, 1)

        @block.scalar
        def _(act):
            act.wait_ge(loaded, 16 * len(loads))
            act.activation(w.gate[0][:, :, :], gate_raw[:, :, :], ACT.Copy).then_inc(hi_ready, 1)
            act.wait_ge(padded, 1)
            act.activation(w.ctxT[0][:, :, :], ctxT[:, :, :], ACT.Copy).then_inc(hi_ready, 1)
            act.wait_ge(product_done, 1)
            act.activation(w.qk[0][:, :, :], qk_ps[:, :, :], ACT.Copy).then_inc(qk_hi_ready, 1)

        @block.vector
        def _(dve):
            dve.wait_ge(hi_ready, 2)
            dve.tensor_tensor(w.gate[1][:, :, :], gate_raw[:, :, :], w.gate[0][:, :, :].bitcast(F32),
                              ALU.subtract).then_inc(prepared, 1)
            dve.tensor_tensor(w.ctxT[1][:, :, :], ctxT[:, :, :], w.ctxT[0][:, :, :].bitcast(F32),
                              ALU.subtract).then_inc(prepared, 1)
            dve.wait_ge(qk_hi_ready, 1)
            dve.tensor_tensor(w.qk[1][:, :, :], qk_ps[:, :, :], w.qk[0][:, :, :].bitcast(F32),
                              ALU.subtract).then_inc(prepared, 1)
            dve.tensor_scalar(w.half_g[:, :], k.tanh_g[:, 2:3], 0.5, None, ALU.mult).then_inc(prepared, 1)


def causal_attention(nc, a, k):
    with Scope(nc, "causal") as s:
        w = Named()
        w.qk = [s.sb(f"qk{i}", [P, KD, D], F32R) for i in range(2)]
        w.gate = [s.sb(f"gate{i}", [P, KD, D], F32R) for i in range(2)]
        w.ctxT = [s.sb(f"ctxT{i}", [P, KD, B * EVEN], F32R) for i in range(2)]
        w.ctx = s.sb("ctx", [KEYS, B * D])
        w.norm_w = s.sb("norm_w", [P, D])
        w.gate_b = s.sb("gate_b", [P, D])
        w.above = s.sb("above", [P, P])
        w.gate8 = s.sb("gate8", [P, KD, E])
        w.route_scale = s.sb("route_scale", [P, 1])
        w.half_g = s.sb("half_g", [P, 1])
        w.neg_scale = s.sb("neg_scale", [P, 1])
        prepare_causal(nc, a, k, w)

        keysT = [s.sb(f"keysT{i}", [P, 2 * KD * S], F32R) for i in range(2)]
        pool_v = s.sb("pool_v", [P, 2 * POS * D])
        rows_at = s.sb("rows_at", [P, 2 * 4], I32)
        x1 = s.sb("x1", [P, 4, D])
        y0 = s.sb("y0", [P, 4, D])
        y1 = s.sb("y1", [P, 4, D])
        ys = s.sb("ys", [P, 4, D])
        part1 = s.sb("part1", [P, 2, D])
        part2 = s.sb("part2", [P, 2, D])
        x2 = s.sb("x2", [P, 4, D])
        stats = s.sb("stats", [P, 8, 6])
        moments = s.sb("moments", [P, 8, 2])
        var_eps = s.sb("var_eps", [P, 8])
        shift = s.sb("shift", [P, 8])
        shift3 = s.sb("shift3", [P, 8])
        rstd = s.sb("rstd", [P, 8])
        h = s.sb("h", [P, 8, D])
        square = s.sb("square", [P, D])
        sum_sq = s.sb("sum_sq", [P, 8])
        mean_sq = s.sb("mean_sq", [P, 8])
        rrms = s.sb("rrms", [P, 8])
        normed = s.sb("normed", [P, 2, D])
        hT = [s.sb(f"hT{i}", [P, 2, D], F32R) for i in range(2)]
        gated_h = s.sb("gated_h", [P, 2, D])
        base = s.sb("base", [P, 8, D])
        z = s.sb("z", [P, 2, D])
        tanh_z = s.sb("tanh_z", [P, 4, D])
        qT = [s.sb(f"qT{i}", [P, 2, D], F32R) for i in range(2)]
        rowmax = s.sb("rowmax", [P, 8])
        neg_max = s.sb("neg_max", [P, 8])
        probs = s.sb("probs", [P, 2, S + P])
        den = s.sb("den", [P, 8])
        rden = s.sb("rden", [P, 8])
        probsT = s.sb("probsT", [P, 2, (POS + 1) * P])
        diff = s.sb("diff", [P, 2, D])
        mixed = s.sb("mixed", [P, 2, D])
        x3 = s.sb("x3", [P, 4, D])
        stats3 = s.sb("stats3", [P, 8, 6])
        moments3 = s.sb("moments3", [P, 8, 2])
        var_eps3 = s.sb("var_eps3", [P, 8])
        rstd3 = s.sb("rstd3", [P, 8])
        xn3 = s.sb("xn3", [P, 2, D])
        xn3T = s.sb("xn3T", [P, 4, D])
        logits = s.sb("logits", [P, 4, E])
        exp_l = s.sb("exp_l", [P, 4, E])
        one_plus = s.sb("one_plus", [P, 4, E])
        sigmoid = s.sb("sigmoid", [P, 4, E])
        gate_s = s.sb("gate_s", [P, 4, E])
        top = s.sb("top", [P, 4, 8])
        top_at = s.sb("top_at", [P, 4, 8], U32)
        total = s.sb("total", [P, 4])
        rtotal = s.sb("rtotal", [P, 4])
        chosen_at = s.sb("chosen_at", [P, 4, 2])
        chosen_w = s.sb("chosen_w", [P, 4, 2])
        chosen = s.sb("chosen", [P, 4, 2, E])
        weighed = s.sb("weighed", [P, 4, 2, E])

        logits_ps = s.ps("logits_ps", [P, 3 * BANK])
        pT_ps = s.ps("pT_ps", [P, 2, BANK])
        turn_ps = s.ps("turn_ps", [P, BANK])
        mm_ps = s.ps("mm_ps", [P, BANK])
        out_ps = s.ps("out_ps", [P, BANK])

        q = Named()
        (q.shift_ready, q.shift3_ready) = s.sems("shift_ready shift3_ready")
        (q.rows_ready, q.part1_ready, q.part2_ready, q.x2_ready, q.stats_ready) = s.sems(
            "rows_ready part1_ready part2_ready x2_ready stats_ready")
        (q.moments_ready, q.var_ready, q.rstd_ready, q.h_ready, q.square_ready) = s.sems(
            "moments_ready var_ready rstd_ready h_ready square_ready")
        (q.mean_ready, q.rrms_ready, q.normed_ready, q.hT_done, q.hT_hi, q.hT_lo) = s.sems(
            "mean_ready rrms_ready normed_ready hT_done hT_hi hT_lo")
        (q.nT_done, q.nT_hi, q.nT_lo, q.gate_done, q.z_ready, q.tanh_ready, q.q_done) = s.sems(
            "nT_done nT_hi nT_lo gate_done z_ready tanh_ready q_done")
        (q.q_hi, q.q_lo, q.logits_done, q.rowmax_ready, q.neg_max_ready) = s.sems(
            "q_hi q_lo logits_done rowmax_ready neg_max_ready")
        (q.probs_ready, q.pT_done, q.pT_ready, q.pv_done, q.rden_ready, q.diff_ready) = s.sems(
            "probs_ready pT_done pT_ready pv_done rden_ready diff_ready")
        (q.mixed_ready, q.gated_h_ready, q.base_ready, q.x3_ready, q.stats3_ready) = s.sems(
            "mixed_ready gated_h_ready base_ready x3_ready stats3_ready")
        (q.moments3_ready, q.var3_ready, q.rstd3_ready, q.xn3_ready, q.xn3T_done) = s.sems(
            "moments3_ready var3_ready rstd3_ready xn3_ready xn3T_done")
        (q.xn3T_ready, q.glogits_done, q.glogits_ready, q.exp_ready) = s.sems(
            "xn3T_ready glogits_done glogits_ready exp_ready")
        (q.one_plus_ready, q.probs_cleared, q.sigmoid_ready, q.gate_s_ready) = s.sems(
            "one_plus_ready probs_cleared sigmoid_ready gate_s_ready")
        (q.top_ready, q.top_at_ready, q.total_ready, q.rtotal_ready) = s.sems(
            "top_ready top_at_ready total_ready rtotal_ready")
        (q.chosen_at_ready, q.weight_ready, q.chosen_w_ready, q.chosen_ready) = s.sems(
            "chosen_at_ready weight_ready chosen_w_ready chosen_ready")
        (q.weighed_ready, q.gates_ready, q.pooled) = s.sems(
            "weighed_ready gates_ready pooled")
        x1_loaded = [s.sem(f"x1_loaded{i}") for i in range(4)]
        ys_loaded = [s.sem(f"ys_loaded{i}") for i in range(4)]
        y0_gathered = [s.sem(f"y0_gathered{i}") for i in range(4)]
        y1_gathered = [s.sem(f"y1_gathered{i}") for i in range(4)]
        x3_stored = [s.sem(f"x3_stored{i}") for i in range(4)]
        xn3T_stored = [s.sem(f"xn3T_stored{i}") for i in range(4)]

        LOAD, COMBINE, H, NORMED, GATE, QUERIES, LOGITS, PROBS, ATTEND, ATT, XN3, GLOGITS, ROUTE = \
            0, 2, 3, 4, 5, 5, 6, 7, 7, 8, 9, 10, 10
        DEPTH = 14
        turn_bank = Bank(NT, [("n", 5, q.nT_lo), ("h", 5, q.hT_lo), ("x3", 13, q.xn3T_ready)])
        mm_bank = Bank(NT, [("gate", 6, q.z_ready), ("queries", 6, q.q_lo)])
        out_bank = Bank(NT, [("glogits", 14, q.glogits_ready), ("attend", 10, q.diff_ready)])

        def rows(t):
            return bass.ds(t.index * P, P)

        def fours(t):
            return t.round * 2 + t.slot // 4

        def groups(pos):
            return -(-(pos + 2) // 4)

        GROUPS = sum(groups(p) for p in range(POS))

        def groups_before(t):
            return t.round * GROUPS + sum(groups(p) for p in range(t.slot))

        def half(t):
            return t.round % 2

        def keys_at(t, kk, start, n):
            return bass.ds(half(t) * (KD * S) + (kk * S + start), n)

        block = s.block()

        @block.sync
        def _(sp):
            def load(t):
                i = t.slot % 4
                if t.after(4):
                    sp.wait_ge(q.x2_ready, t.before(4))
                sp.dma_start(x1[:, i, :], k.x1[rows(t), :]).then_inc(x1_loaded[i], 16)
                sp.dma_start(ys[:, i, :], k.y[bass.ds(t.index * P, P), :]).then_inc(ys_loaded[i], 16)

            def store_x3(t):
                i = t.slot % 4
                wait_apart(sp, k, (q.x3_ready, t.count))
                sp.dma_start(k.x3[rows(t), :], x3[:, i, :]).then_inc(x3_stored[i], 16)

            def store_xn3T(t):
                i = t.slot % 4
                wait_apart(sp, k, (q.xn3T_ready, t.count))
                sp.dma_start(k.xn4T.rearrange("(k p) t -> p k t", p=P)[:, :, bass.ds(t.index * P, P)],
                             xn3T[:, i, :].rearrange("p (k t) -> p k t", k=KD)).then_inc(xn3T_stored[i], 16)

            pipeline(sp, NT, DEPTH, POS,
                     lambda at: run(at, (12, store_x3), (0, load), (13, store_xn3T)))
            for i in range(4):
                sp.wait_ge(x3_stored[i], 16 * (NT // 4))
                sp.wait_ge(xn3T_stored[i], 16 * (NT // 4))

        @block.gpsimd
        def _(pool):
            def gather(t):
                i = t.slot % 4
                if t.after(4):
                    pool.wait_ge(y0_gathered[i], fours(t) * 16)
                    pool.wait_ge(y1_gathered[i], fours(t) * 16)
                    pool.wait_ge(q.part2_ready, t.before(4))
                pool.tensor_copy(rows_at[:, 2 * i:2 * i + 2],
                                 k.slots[:, bass.ds(t.round * 2 + t.slot * (2 * B), 2)]
                                 ).then_inc(q.rows_ready, 1)
                wait_apart(pool, k, (q.rows_ready, t.count))
                for c, to, sem in ((0, y0, y0_gathered[i]), (1, y1, y1_gathered[i])):
                    pool.indirect_dma_start(
                        out=to[:, i, :], out_offset=None, in_=k.y[:, :],
                        in_offset=bass.IndirectOffsetOnAxis(ap=rows_at[:, 2 * i + c:2 * i + c + 1], axis=0)
                        ).then_inc(sem, 16)

            def power(t, to, of, moved, eps, ready, moved_ready, done):
                i = t.slot
                pool.wait_ge(ready, t.count)
                pool.tensor_tensor(moved[:, i:i + 1], of, k.eps[:, eps:eps + 1], ALU.add
                                   ).then_inc(moved_ready, 1)
                pool.wait_ge(moved_ready, t.count)
                pool.tensor_tensor(to[:, i:i + 1], moved[:, i:i + 1], k.neghalf[:, :],
                                   ALU.pow).then_inc(done, 1)

            def negate_shift(t, to, mean, std, ready, done):
                i = t.slot
                wait_apart(pool, k, (ready, t.count))
                pool.tensor_scalar(to[:, i:i + 1], mean, std[:, i:i + 1], -1.0, ALU.mult, ALU.mult
                                   ).then_inc(done, 1)

            def rstd_x2(t):
                power(t, rstd, moments[:, t.slot, 1:2], var_eps, 0, q.moments_ready, q.var_ready,
                      q.rstd_ready)
                negate_shift(t, shift, moments[:, t.slot, 0:1], rstd, q.rstd_ready, q.shift_ready)

            def rrms_h(t):
                power(t, rrms, sum_sq[:, t.slot:t.slot + 1], mean_sq, 1, q.square_ready,
                      q.mean_ready, q.rrms_ready)

            def rstd_x3(t):
                power(t, rstd3, moments3[:, t.slot, 1:2], var_eps3, 0, q.moments3_ready,
                      q.var3_ready, q.rstd3_ready)
                negate_shift(t, shift3, moments3[:, t.slot, 0:1], rstd3, q.rstd3_ready, q.shift3_ready)

            def ungated(t):
                i = t.slot
                pool.wait_ge(q.h_ready, t.count)
                pool.tensor_tensor(gated_h[:, i % 2, :], h[:, i, :],
                                   k.tanh_g[:, 2:3].to_broadcast([P, D]), ALU.mult).then_inc(q.gated_h_ready, 1)
                pool.wait_ge(q.gated_h_ready, t.count)
                pool.tensor_tensor(base[:, i, :], gated_h[:, i % 2, :], x2[:, i % 4, :],
                                   ALU.add).then_inc(q.base_ready, 1)

            def negate_max(t):
                i = t.slot
                pool.wait_ge(q.rowmax_ready, t.count)
                pool.tensor_tensor(neg_max[:, i:i + 1], rowmax[:, i:i + 1], w.neg_scale[:, :],
                                   ALU.mult).then_inc(q.neg_max_ready, 1)

            pool.memset(probs[:, :, :], 0.0).then_inc(q.probs_cleared, 1)
            pipeline(pool, NT, DEPTH, POS,
                     lambda at: run(at, (0, gather), (11, rstd_x3), (8, negate_max), (3, rstd_x2), (4, rrms_h), (5, ungated)))

        @block.tensor
        def _(pe):
            def turn(of, done):
                for c in range(KD):
                    mm = pe.transpose(turn_ps[:, c * P:(c + 1) * P], of[:, c * P:(c + 1) * P], k.ident[:, :])
                mm.then_inc(done, 1)

            def turn_h(t):
                pe.wait_ge(q.h_ready, t.count)
                if turn_bank.used("h", t):
                    pe.wait_ge(*turn_bank.freed("h", t))
                turn(h[:, t.slot, :], q.hT_done)

            def turn_n(t):
                pe.wait_ge(q.normed_ready, t.count)
                if turn_bank.used("n", t):
                    pe.wait_ge(*turn_bank.freed("n", t))
                turn(normed[:, t.slot % 2, :], q.nT_done)

            def turn_x3(t):
                pe.wait_ge(q.xn3_ready, t.count)
                if turn_bank.used("x3", t):
                    pe.wait_ge(*turn_bank.freed("x3", t))
                turn(xn3[:, t.slot % 2, :], q.xn3T_done)

            def gate_logits(t):
                pe.wait_ge(q.xn3T_ready, t.count)
                if out_bank.used("glogits", t):
                    pe.wait_ge(*out_bank.freed("glogits", t))
                for kk in range(KD):
                    mm = pe.matmul(out_ps[:, 0:E], xn3T[:, t.slot % 4, kk * P:(kk + 1) * P],
                                   w.gate8[:, kk, :], start=(kk == 0), stop=(kk == KD - 1))
                mm.then_inc(q.glogits_done, 1)

            def turn_probs(t):
                i = t.slot % 2
                pe.wait_ge(q.probs_ready, t.count)
                for group in range(groups(t.slot)):
                    n = groups_before(t) + group
                    if not isinstance(n, int) or n >= 2:
                        pe.wait_ge(q.pT_ready, n - 1)
                    bank = (sum(groups(p) for p in range(t.slot)) + group) % 2
                    for c in range(4 * group, min(4 * group + 4, t.slot + 2)):
                        mm = pe.transpose(pT_ps[:, bank, (c % 4) * P:(c % 4 + 1) * P],
                                          probs[:, i, c * P:(c + 1) * P], k.ident[:, :])
                    mm.then_inc(q.pT_done, 1)

            def gate(t):
                i = t.slot % 2
                pe.wait_ge(q.hT_lo, t.count)
                if mm_bank.used("gate", t):
                    pe.wait_ge(*mm_bank.freed("gate", t))
                for kk in range(KD):
                    mm = three_passes(pe, mm_ps[:, 0:D], [part[:, i, kk * P:(kk + 1) * P] for part in hT],
                                      [part[:, kk, :] for part in w.gate],
                                      start=(kk == 0), stop=(kk == KD - 1))
                mm.then_inc(q.gate_done, 1)

            def attend(t):
                i = t.slot % 2
                pe.wait_ge(q.pT_ready, groups_before(t) + groups(t.slot))
                pe.wait_ge(q.pooled, t.count)
                if out_bank.used("attend", t):
                    pe.wait_ge(*out_bank.freed("attend", t))
                for c in range(t.slot + 1):
                    pe.matmul(out_ps[:, 0:D], probsT[:, i, c * P:(c + 1) * P],
                              pool_v[:, bass.ds(half(t) * (POS * D) + c * D, D)],
                              start=(c == 0), stop=False)
                mm = pe.matmul(out_ps[:, 0:D], probsT[0:KEYS, i, (t.slot + 1) * P:(t.slot + 2) * P],
                               w.ctx[:, bass.ds(t.round * D, D)], start=False, stop=True)
                mm.then_inc(q.pv_done, 1)

            def queries(t):
                pe.wait_ge(q.nT_lo, t.count)
                if mm_bank.used("queries", t):
                    pe.wait_ge(*mm_bank.freed("queries", t))
                for c in range(KD):
                    for kk in range(KD):
                        mm = three_passes(pe, mm_ps[:, c * P:(c + 1) * P],
                                          [part[:, kk, c * P:(c + 1) * P] for part in w.qk],
                                          [part[:, keys_at(t, kk, t.slot * P, P)] for part in keysT],
                                          start=(kk == 0 and c == 0), stop=(kk == KD - 1))
                mm.then_inc(q.q_done, 1)

            def score(t):
                i = t.slot % 2
                pe.wait_ge(q.q_lo, t.count)
                if t.after(1):
                    pe.wait_ge(q.probs_ready, t.before(1))
                own = t.slot * P
                for at in range(0, own + P, BANK):
                    n = min(own + P - at, BANK)
                    for kk in range(KD):
                        three_passes(pe, logits_ps[:, at:at + n],
                                     [part[:, i, kk * P:(kk + 1) * P] for part in qT],
                                     [part[:, keys_at(t, kk, at, n)] for part in keysT],
                                     start=(kk == 0), stop=False)
                pe.matmul(logits_ps[:, own:own + P], k.ident[:, :], w.above[:, :], start=False, stop=True,
                          skip_group_check=True)
                at = own + P
                for kk in range(KD):
                    mm = three_passes(pe, logits_ps[:, at:at + EVEN],
                                      [part[:, i, kk * P:(kk + 1) * P] for part in qT],
                                      [part[:, kk, bass.ds(t.round * EVEN, EVEN)] for part in w.ctxT],
                                      start=(kk == 0 and at % BANK == 0), stop=(kk == KD - 1))
                mm.then_inc(q.logits_done, 1)

            pipeline(pe, NT, DEPTH, POS,
                     lambda at: run(at, (14, gate_logits), (5, turn_n), (6, gate), (6, queries), (5, turn_h), (9, turn_probs), (13, turn_x3), (10, attend), (7, score)))

        @block.scalar
        def _(act):
            def normalise(t):
                i = t.slot
                act.wait_ge(q.shift_ready, t.count)
                if t.after(8):
                    act.wait_ge(q.diff_ready, t.before(8))
                    act.wait_ge(q.base_ready, t.before(8))
                act.activation(h[:, i, :], x2[:, i % 4, :], ACT.Identity, scale=rstd[:, i:i + 1],
                               bias=shift[:, i:i + 1]).then_inc(q.h_ready, 1)

            def normalise_x3(t):
                i = t.slot
                act.wait_ge(q.shift3_ready, t.count)
                if t.after(2):
                    act.wait_ge(q.xn3T_done, t.before(2))
                act.activation(xn3[:, i % 2, :], x3[:, i % 4, :], ACT.Identity, scale=rstd3[:, i:i + 1],
                               bias=shift3[:, i:i + 1]).then_inc(q.xn3_ready, 1)

            def to_pool(t):
                act.wait_ge(q.normed_ready, t.count)
                act.activation(pool_v[:, bass.ds(half(t) * (POS * D) + t.slot * D, D)],
                               normed[:, t.slot % 2, :], ACT.Copy).then_inc(q.pooled, 1)

            def square_h(t):
                act.wait_ge(q.h_ready, t.count)
                if t.after(1):
                    act.wait_ge(q.square_ready, t.before(1))
                act.activation(square[:, :], h[:, t.slot, :], ACT.Square, scale=D ** -0.5,
                               accum_out=sum_sq[:, t.slot:t.slot + 1]).then_inc(q.square_ready, 1)

            def h_hi(t):
                if t.after(2):
                    act.wait_ge(q.gate_done, t.before(2))
                act.wait_ge(q.hT_done, t.count)
                act.activation(hT[0][:, t.slot % 2, :], turn_ps[:, 0:D], ACT.Copy).then_inc(q.hT_hi, 1)

            def n_hi(t):
                act.wait_ge(q.nT_done, t.count)
                for kk in range(KD):
                    ins = act.activation(keysT[0][:, keys_at(t, kk, t.slot * P, P)],
                                         turn_ps[:, kk * P:(kk + 1) * P], ACT.Copy)
                ins.then_inc(q.nT_hi, 1)

            def copy_probsT(t):
                i = t.slot % 2
                if t.after(2):
                    act.wait_ge(q.pv_done, t.before(2))
                for group in range(groups(t.slot)):
                    n = (min(4 * group + 4, t.slot + 2) - 4 * group) * P
                    bank = (sum(groups(p) for p in range(t.slot)) + group) % 2
                    act.wait_ge(q.pT_done, groups_before(t) + (group + 1))
                    act.activation(probsT[:, i, group * BANK:group * BANK + n], pT_ps[:, bank, 0:n],
                                   ACT.Copy).then_inc(q.pT_ready, 1)

            def copy_x3(t):
                i = t.slot % 4
                if t.after(4):
                    act.wait_ge(xn3T_stored[i], fours(t) * 16)
                    act.wait_ge(q.glogits_done, t.before(4))
                act.wait_ge(q.xn3T_done, t.count)
                act.activation(xn3T[:, i, :], turn_ps[:, 0:D], ACT.Copy).then_inc(q.xn3T_ready, 1)

            def tanh(t):
                act.wait_ge(q.z_ready, t.count)
                if t.after(4):
                    act.wait_ge(q.mixed_ready, t.before(4))
                act.activation(tanh_z[:, t.slot % 4, :], z[:, t.slot % 2, :], ACT.Tanh,
                               scale=0.5).then_inc(q.tanh_ready, 1)

            def q_hi(t):
                if t.after(2):
                    act.wait_ge(q.logits_done, t.before(2))
                act.wait_ge(q.q_done, t.count)
                act.activation(qT[0][:, t.slot % 2, :], mm_ps[:, 0:D], ACT.Copy).then_inc(q.q_hi, 1)

            def exponent(t):
                i = t.slot
                n = KEYS + (i + 1) * P
                act.wait_ge(q.neg_max_ready, t.count)
                if t.after(2):
                    act.wait_ge(q.pT_done, groups_before(t) - groups((i - 1) % POS))
                act.activation(probs[:, i % 2, 0:n], logits_ps[:, 0:n], ACT.Exp, bias=neg_max[:, i:i + 1],
                               scale=D ** -0.5, accum_out=den[:, i:i + 1]).then_inc(q.probs_ready, 1)

            def exp_logits(t):
                if t.slot % 4 == 3:
                    act.wait_ge(q.glogits_ready, t.count)
                    act.activation(exp_l[:, :, :], logits[:, :, :], ACT.Exp, scale=-1.0
                                   ).then_inc(q.exp_ready, 1)

            act.wait_ge(q.probs_cleared, 1)
            pipeline(act, NT, DEPTH, POS,
                     lambda at: run(at, (13, normalise_x3), (6, to_pool), (4, normalise), (5, n_hi), (7, tanh), (5, h_hi), (4, square_h), (6, q_hi), (8, exponent), (9, copy_probsT), (13, copy_x3), (14, exp_logits)))

        @block.vector
        def _(dve):
            def combine(t):
                i, j = t.slot % 4, t.slot % 2
                at = t.slot * (2 * B) + t.round * 2
                dve.wait_ge(x1_loaded[i], fours(t) * 16 + 16)
                dve.wait_ge(y0_gathered[i], fours(t) * 16 + 16)
                dve.scalar_tensor_tensor(out=part1[:, j, :], in0=y0[:, i, :], scalar=k.weights[:, bass.ds(at, 1)],
                                         in1=x1[:, i, :], op0=ALU.mult, op1=ALU.add
                                         ).then_inc(q.part1_ready, 1)
                dve.wait_ge(q.part1_ready, t.count)
                dve.wait_ge(y1_gathered[i], fours(t) * 16 + 16)
                dve.scalar_tensor_tensor(out=part2[:, j, :], in0=y1[:, i, :],
                                         scalar=k.weights[:, bass.ds(at + 1, 1)], in1=part1[:, j, :],
                                         op0=ALU.mult, op1=ALU.add).then_inc(q.part2_ready, 1)
                dve.wait_ge(q.part2_ready, t.count)
                dve.wait_ge(ys_loaded[i], fours(t) * 16 + 16)
                if t.after(4):
                    dve.wait_ge(q.base_ready, t.before(4))
                dve.scalar_tensor_tensor(out=x2[:, i, :], in0=ys[:, i, :], scalar=k.tanh_g[:, 1:2],
                                         in1=part2[:, j, :], op0=ALU.mult, op1=ALU.add
                                         ).then_inc(q.x2_ready, 1)
                dve.wait_ge(q.x2_ready, t.count)
                dve.bn_stats(stats[:, t.slot, :], x2[:, i, :]).then_inc(q.stats_ready, 1)
                wait_apart(dve, k, (q.stats_ready, t.count))
                dve.bn_aggr(moments[:, t.slot, :], stats[:, t.slot, :]).then_inc(q.moments_ready, 1)

            def rms_norm(t):
                i = t.slot
                dve.wait_ge(q.rrms_ready, t.count)
                if t.after(2):
                    dve.wait_ge(q.nT_done, t.before(2))
                    dve.wait_ge(q.pooled, t.before(2))
                dve.scalar_tensor_tensor(out=normed[:, i % 2, :], in0=h[:, i, :],
                                         scalar=rrms[:, i:i + 1], in1=w.norm_w[:, :],
                                         op0=ALU.mult, op1=ALU.mult).then_inc(q.normed_ready, 1)

            def difference(t):
                i, j = t.slot, t.slot % 2
                dve.wait_ge(q.probs_ready, t.count)
                dve.reciprocal(rden[:, i:i + 1], den[:, i:i + 1]).then_inc(q.rden_ready, 1)
                dve.wait_ge(q.rden_ready, t.count)
                dve.wait_ge(q.pv_done, t.count)
                dve.scalar_tensor_tensor(out=diff[:, j, :], in0=out_ps[:, 0:D], scalar=rden[:, i:i + 1],
                                         in1=h[:, i, :], op0=ALU.mult, op1=ALU.subtract
                                         ).then_inc(q.diff_ready, 1)
                dve.wait_ge(q.diff_ready, t.count)
                dve.wait_ge(q.tanh_ready, t.count)
                dve.scalar_tensor_tensor(out=mixed[:, j, :], in0=tanh_z[:, i % 4, :], scalar=1.0,
                                         in1=diff[:, j, :], op0=ALU.add, op1=ALU.mult
                                         ).then_inc(q.mixed_ready, 1)
                dve.wait_ge(q.mixed_ready, t.count)
                dve.wait_ge(q.base_ready, t.count)
                if t.after(4):
                    dve.wait_ge(x3_stored[i % 4], fours(t) * 16)
                    dve.wait_ge(q.xn3_ready, t.before(4))
                dve.scalar_tensor_tensor(out=x3[:, i % 4, :], in0=mixed[:, j, :], scalar=w.half_g[:, :],
                                         in1=base[:, i, :], op0=ALU.mult, op1=ALU.add
                                         ).then_inc(q.x3_ready, 1)
                dve.wait_ge(q.x3_ready, t.count)
                dve.bn_stats(stats3[:, i, :], x3[:, i % 4, :]).then_inc(q.stats3_ready, 1)
                wait_apart(dve, k, (q.stats3_ready, t.count))
                dve.bn_aggr(moments3[:, i, :], stats3[:, i, :]).then_inc(q.moments3_ready, 1)

            def h_lo(t):
                j = t.slot % 2
                dve.wait_ge(q.hT_hi, t.count)
                dve.tensor_tensor(hT[1][:, j, :], turn_ps[:, 0:D], hT[0][:, j, :].bitcast(F32),
                                  ALU.subtract).then_inc(q.hT_lo, 1)

            def n_lo(t):
                dve.wait_ge(q.nT_hi, t.count)
                for kk in range(KD):
                    ins = dve.tensor_tensor(keysT[1][:, keys_at(t, kk, t.slot * P, P)],
                                            turn_ps[:, kk * P:(kk + 1) * P],
                                            keysT[0][:, keys_at(t, kk, t.slot * P, P)].bitcast(F32),
                                            ALU.subtract)
                ins.then_inc(q.nT_lo, 1)

            def copy_glogits(t):
                i = t.slot % 4
                dve.wait_ge(q.glogits_done, t.count)
                if t.after(4):
                    dve.wait_ge(q.exp_ready, fours(t))
                dve.tensor_copy(logits[:, i, :], out_ps[:, 0:E]).then_inc(q.glogits_ready, 1)

            def add_gate_b(t):
                dve.wait_ge(q.gate_done, t.count)
                if t.after(2):
                    dve.wait_ge(q.tanh_ready, t.before(2))
                dve.tensor_tensor(z[:, t.slot % 2, :], mm_ps[:, 0:D], w.gate_b[:, :],
                                  ALU.add).then_inc(q.z_ready, 1)

            def q_lo(t):
                j = t.slot % 2
                dve.wait_ge(q.q_hi, t.count)
                dve.tensor_tensor(qT[1][:, j, :], mm_ps[:, 0:D], qT[0][:, j, :].bitcast(F32),
                                  ALU.subtract).then_inc(q.q_lo, 1)

            def row_max(t):
                i = t.slot
                dve.wait_ge(q.logits_done, t.count)
                dve.tensor_reduce(rowmax[:, i:i + 1], logits_ps[:, 0:KEYS + (i + 1) * P], AX.X,
                                  ALU.max).then_inc(q.rowmax_ready, 1)

            def route(t):
                if t.slot % 4 != 3:
                    return
                r = fours(t)
                dve.wait_ge(q.exp_ready, r + 1)
                dve.tensor_scalar(one_plus[:, :, :], exp_l[:, :, :], 1.0, None,
                                  ALU.add).then_inc(q.one_plus_ready, 1)
                dve.wait_ge(q.one_plus_ready, r + 1)
                dve.reciprocal(sigmoid[:, :, :], one_plus[:, :, :]).then_inc(q.sigmoid_ready, 1)
                dve.wait_ge(q.sigmoid_ready, r + 1)
                dve.tensor_scalar(gate_s[:, :, :], sigmoid[:, :, :], w.route_scale[:, :], None,
                                  ALU.mult).then_inc(q.gate_s_ready, 1)
                wait_apart(dve, k, (q.gate_s_ready, r + 1))
                for i in range(4):
                    ins = dve.max(top[:, i, :], gate_s[:, i, :])
                ins.then_inc(q.top_ready, 1)
                wait_apart(dve, k, (q.top_ready, r + 1))
                for i in range(4):
                    ins = dve.max_index(top_at[:, i, :], top[:, i, :], gate_s[:, i, :])
                ins.then_inc(q.top_at_ready, 1)
                dve.tensor_tensor(total[:, :], top[:, :, 0], top[:, :, 1], ALU.add).then_inc(q.total_ready, 1)
                dve.wait_ge(q.total_ready, r + 1)
                dve.reciprocal(rtotal[:, :], total[:, :]).then_inc(q.rtotal_ready, 1)
                dve.wait_ge(q.top_at_ready, r + 1)
                dve.tensor_copy(chosen_at[:, :, :], top_at[:, :, 0:2]).then_inc(q.chosen_at_ready, 1)
                dve.wait_ge(q.rtotal_ready, r + 1)
                for c in range(2):
                    ins = dve.scalar_tensor_tensor(out=chosen_w[:, :, c], in0=top[:, :, c],
                                                   scalar=k.tanh_g[:, 3:4], in1=rtotal[:, :],
                                                   op0=ALU.mult, op1=ALU.mult)
                ins.then_inc(q.chosen_w_ready, 1)
                dve.wait_ge(q.chosen_at_ready, r + 1)
                dve.tensor_tensor(chosen[:, :, :, :].rearrange("p b c e -> p (b c) e"),
                                  k.iota8[:, :].unsqueeze(1).to_broadcast([P, 8, E]),
                                  chosen_at[:, :, :].rearrange("p b c -> p (b c)").unsqueeze(2)
                                  .to_broadcast([P, 8, E]), ALU.is_equal).then_inc(q.chosen_ready, 1)
                dve.wait_ge(q.chosen_ready, r + 1)
                dve.wait_ge(q.chosen_w_ready, r + 1)
                dve.tensor_tensor(weighed[:, :, :, :].rearrange("p b c e -> p (b c) e"),
                                  chosen[:, :, :, :].rearrange("p b c e -> p (b c) e"),
                                  chosen_w[:, :, :].rearrange("p b c -> p (b c)").unsqueeze(2)
                                  .to_broadcast([P, 8, E]), ALU.mult).then_inc(q.weighed_ready, 1)
                dve.wait_ge(q.weighed_ready, r + 1)
                here = k.gates[:, bass.ds(r * (4 * (E + 1)), 4 * (E + 1))].rearrange("p (b e) -> p b e", e=E + 1)
                dve.tensor_tensor(here[:, :, 0:E], weighed[:, :, 0, :], weighed[:, :, 1, :],
                                  ALU.add).then_inc(q.gates_ready, 1)

            dve.tensor_scalar(k.gates[:, E::E + 1], k.ones32[:, :], k.tanh_g[:, 3:4], None,
                              ALU.mult).then_inc(q.weight_ready, 1)
            pipeline(dve, NT, DEPTH, POS,
                     lambda at: run(at, (5, rms_norm), (11, difference), (8, row_max), (6, add_gate_b), (14, copy_glogits), (5, n_lo), (5, h_lo), (2, combine), (6, q_lo), (14, route)))


def dense_experts(nc, a, k, out):
    with Scope(nc, "dense") as s:
        N = BANK
        SUB = N // P
        GROUPS = T // N
        X = E + 1
        UNITS = X + 1
        WIDTH = 2 * UNITS
        W1, W2, b1 = (s.sb(n, sh) for n, sh in (("W1", [P, X, KD, H1]), ("W2", [P, X, D]), ("b1", [P, X])))
        W1_parts = [s.sb(f"W1_{i}", [P, X, KD, H1], F32R) for i in range(2)]
        W2_parts = [s.sb(f"W2_{i}", [P, X, D], F32R) for i in range(2)]
        b2 = s.sb("b2", [X, D])
        xT = s.sb("xT", [P, 2, KD, N])
        xT_parts = [s.sb(f"xT{i}", [P, 2, KD, N], F32R) for i in range(2)]
        x3 = s.sb("x3", [P, 2, SUB, D])
        acc = s.sb("acc", [P, 2, SUB, D])
        h = s.sb("h", [P, 2, N])
        h_parts = [s.sb(f"h{i}", [P, 2, N], F32R) for i in range(2)]
        gates_now = s.sb("gates_now", [P, SUB * X])
        gatesT = s.sb("gatesT", [X, N])
        hid_ps = s.ps("hid_ps", [P, 2, BANK])
        y_ps = s.ps("y_ps", [P, SUB, BANK])
        gates_ps = s.ps("gates_ps", [P, BANK])

        weights_loaded = s.sem("weights_loaded")
        x_loaded = [s.sem(f"x_loaded{i}") for i in range(2)]
        x3_loaded = [s.sem(f"x3_loaded{i}") for i in range(2)]
        stored = [s.sem(f"stored{i}") for i in range(2)]
        q = Named()
        (q.w_hi, q.w_lo, q.x_hi, q.x_lo, q.hid_done, q.h_ready, q.h_hi, q.h_lo) = s.sems(
            "w_hi w_lo x_hi x_lo hid_done h_ready h_hi h_lo")
        (q.y_done, q.added, q.gates_copied, q.gates_turned, q.gatesT_ready) = s.sems(
            "y_done added gates_copied gates_turned gatesT_ready")
        LOAD, SPLIT, HIDDEN, OUT, STORE = 0, 4, 6, 7, 8
        DEPTH = 8
        block = s.block()

        def expert(t):
            return t.slot % UNITS

        def parity(t):
            return t.slot // UNITS

        def group(t, ahead=0):
            return t.round * 2 + (parity(t) + ahead)

        def hidden_count(t, ahead=0):
            return t.round * (2 * X) + (parity(t) * X + expert(t) + 1 + ahead)

        def buffer(t):
            return (parity(t) * X + expert(t)) % 2

        def at_expert(stage, *which):
            return lambda t: stage(t) if expert(t) in which else None

        def many(stage):
            return at_expert(stage, *range(X))

        def tile(t, j):
            return t.round * (2 * SUB) + (parity(t) * SUB + j)

        loads = [
            (W1[:, 0:E, :, :], a["L1_ffn_W1"].rearrange("e (k p) n -> p e k n", p=P)),
            (W1[:, E, :, :], a["L1_ffn_Ws1"].rearrange("(k p) n -> p k n", p=P)),
            (b1[:, :], a["L1_ffn_b1"]),
            (W2[:, 0:E, :], a["L1_ffn_W2"].rearrange("e p n -> p e n")),
            (W2[:, E, :], a["L1_ffn_Ws2"]),
            (b2[:, :], a["L1_ffn_b2"]),
        ]

        @block.sync
        def _(sp):
            def load(t):
                g = parity(t)
                if t.after(WIDTH):
                    sp.wait_ge(q.x_lo, group(t, -1))
                    sp.wait_ge(q.added, t.before(WIDTH) * SUB)
                sp.dma_start(xT[:, g, :, :], k.xn4T.rearrange("(k p) t -> p k t", p=P)
                             [:, :, bass.ds(group(t) * N, N)]).then_inc(x_loaded[g], 16)
                sp.dma_start(x3[:, g, :, :], k.x3[bass.ds(group(t) * N, N), :]
                             .rearrange("(j p) d -> p j d", p=P)).then_inc(x3_loaded[g], 16)

            def store(t):
                g = parity(t)
                sp.wait_ge(q.added, t.count * SUB)
                sp.dma_start(out[bass.ds(group(t) * N, N), :].rearrange("(j p) d -> p j d", p=P),
                             acc[:, g, :, :]).then_inc(stored[g], 16)

            for to, of in loads:
                sp.dma_start(to, of).then_inc(weights_loaded, 16)
            pipeline(sp, GROUPS * UNITS, DEPTH, WIDTH,
                     lambda at: run(at, (LOAD, at_expert(load, 0)), (STORE, at_expert(store, X))))
            for g in range(2):
                sp.wait_ge(stored[g], 16 * (GROUPS // 2))

        @block.gpsimd
        def _(pool):
            def copy_gates(t):
                if t.after(UNITS):
                    pool.wait_ge(q.gates_turned, group(t))
                pool.tensor_copy(gates_now[:, :], k.gates[:, bass.ds(group(t) * (SUB * X), SUB * X)]
                                 ).then_inc(q.gates_copied, 1)

            pipeline(pool, GROUPS * UNITS, DEPTH, WIDTH,
                     lambda at: run(at, (SPLIT, at_expert(copy_gates, X))))

        @block.tensor
        def _(pe):
            def hidden(t):
                i = buffer(t)
                pe.wait_ge(q.x_lo, group(t, 1))
                if t.after(2):
                    pe.wait_ge(q.h_ready, hidden_count(t, -2))
                e = expert(t)
                for c in range(KD):
                    mm = three_passes(pe, hid_ps[:, i, :], [part[:, e, c, :] for part in W1_parts],
                                      [part[:, parity(t), c, :] for part in xT_parts],
                                      start=(c == 0), stop=(c == KD - 1))
                mm.then_inc(q.hid_done, 1)

            def turn_gates(t):
                pe.wait_ge(q.gates_copied, group(t, 1))
                if t.after(UNITS):
                    pe.wait_ge(q.gatesT_ready, group(t))
                for j in range(SUB):
                    mm = pe.transpose(gates_ps[0:X, j * P:(j + 1) * P], gates_now[:, j * X:(j + 1) * X],
                                      k.ident[:, :])
                mm.then_inc(q.gates_turned, 1)

            def bank_free(t, j):
                if t.after(1):
                    pe.wait_ge(q.added, t.before(1) * SUB - (SUB - 1 - j))

            def product(t):
                i, e = buffer(t), expert(t)
                pe.wait_ge(q.h_lo, hidden_count(t))
                for j in range(SUB):
                    bank_free(t, j)
                    three_passes(pe, y_ps[:, j, 0:D], [part[:, i, j * P:(j + 1) * P] for part in h_parts],
                                 [part[:, e, :] for part in W2_parts], start=True, stop=True
                                 ).then_inc(q.y_done, 1)

            def bias(t):
                pe.wait_ge(q.gatesT_ready, group(t, 1))
                for j in range(SUB):
                    bank_free(t, j)
                    pe.matmul(y_ps[:, j, 0:D], gatesT[:, j * P:(j + 1) * P], b2[:, :],
                              start=True, stop=True).then_inc(q.y_done, 1)

            pe.wait_ge(q.w_lo, 2)
            pipeline(pe, GROUPS * UNITS, DEPTH, WIDTH,
                     lambda at: run(at, (HIDDEN, many(hidden)), (HIDDEN, at_expert(turn_gates, X)),
                                    (OUT, many(product)), (OUT, at_expert(bias, X))))

        @block.scalar
        def _(act):
            def split(t):
                g = parity(t)
                act.wait_ge(x_loaded[g], t.round * 16 + 16)
                if t.after(WIDTH):
                    act.wait_ge(q.hid_done, hidden_count(t, -X - 1))
                act.activation(xT_parts[0][:, g, :, :], xT[:, g, :, :], ACT.Copy).then_inc(q.x_hi, 1)

            def gelu(t):
                i, e = buffer(t), expert(t)
                act.wait_ge(q.hid_done, hidden_count(t))
                if t.after(2):
                    act.wait_ge(q.h_lo, hidden_count(t, -2))
                act.activation(h[:, i, :], hid_ps[:, i, :], ACT.Gelu, bias=b1[:, e:e + 1]
                               ).then_inc(q.h_ready, 1)
                act.wait_ge(q.h_ready, hidden_count(t))
                if t.after(2):
                    act.wait_ge(q.y_done, (t.before(3) if e < 2 else t.before(2)) * SUB)
                act.activation(h_parts[0][:, i, :], h[:, i, :], ACT.Copy).then_inc(q.h_hi, 1)

            def copy_gatesT(t):
                act.wait_ge(q.gates_turned, group(t, 1))
                if t.after(UNITS):
                    act.wait_ge(q.y_done, t.before(UNITS) * SUB)
                act.activation(gatesT[:, :], gates_ps[0:X, :], ACT.Copy).then_inc(q.gatesT_ready, 1)

            act.wait_ge(weights_loaded, 16 * len(loads))
            act.activation(W1_parts[0][:, :, :, :], W1[:, :, :, :], ACT.Copy).then_inc(q.w_hi, 1)
            act.activation(W2_parts[0][:, :, :], W2[:, :, :], ACT.Copy).then_inc(q.w_hi, 1)
            pipeline(act, GROUPS * UNITS, DEPTH, WIDTH,
                     lambda at: run(at, (SPLIT, at_expert(split, 0)), (HIDDEN, many(gelu)),
                                    (HIDDEN, at_expert(copy_gatesT, X))))

        @block.vector
        def _(dve):
            def split(t):
                g = parity(t)
                dve.wait_ge(q.x_hi, group(t, 1))
                dve.tensor_tensor(xT_parts[1][:, g, :, :], xT[:, g, :, :],
                                  xT_parts[0][:, g, :, :].bitcast(F32), ALU.subtract).then_inc(q.x_lo, 1)

            def add(t):
                g, e = parity(t), expert(t)
                if e == 0:
                    dve.wait_ge(x3_loaded[g], t.round * 16 + 16)
                    if t.after(WIDTH):
                        dve.wait_ge(stored[g], t.round * 16)
                for j in range(SUB):
                    dve.wait_ge(q.y_done, t.before(1) * SUB + (j + 1))
                    if e == 0:
                        so_far = x3[:, g, j, :]
                    else:
                        so_far = acc[:, g, j, :]
                        dve.wait_ge(q.added, t.before(1) * SUB - (SUB - 1 - j))
                    if e < X:
                        ins = dve.scalar_tensor_tensor(out=acc[:, g, j, :], in0=y_ps[:, j, 0:D],
                                                       scalar=k.gates[:, bass.ds(tile(t, j) * X + e, 1)],
                                                       in1=so_far, op0=ALU.mult, op1=ALU.add)
                    else:
                        ins = dve.tensor_tensor(acc[:, g, j, :], y_ps[:, j, 0:D], so_far, ALU.add)
                    ins.then_inc(q.added, 1)

            def h_lo(t):
                i = buffer(t)
                dve.wait_ge(q.h_hi, hidden_count(t))
                dve.tensor_tensor(h_parts[1][:, i, :], h[:, i, :], h_parts[0][:, i, :].bitcast(F32),
                                  ALU.subtract).then_inc(q.h_lo, 1)

            dve.wait_ge(q.w_hi, 2)
            dve.tensor_tensor(W1_parts[1][:, :, :, :], W1[:, :, :, :], W1_parts[0][:, :, :, :].bitcast(F32),
                              ALU.subtract).then_inc(q.w_lo, 1)
            dve.tensor_tensor(W2_parts[1][:, :, :], W2[:, :, :], W2_parts[0][:, :, :].bitcast(F32),
                              ALU.subtract).then_inc(q.w_lo, 1)
            pipeline(dve, GROUPS * UNITS, DEPTH, WIDTH,
                     lambda at: run(at, (SPLIT, at_expert(split, 0)), (OUT, add), (HIDDEN, many(h_lo))))


def flamingo(nc, a, out):
    with Scope(nc, "kept") as s:
        k = allocate_kept(nc, s)
        cross_attention(nc, a, k)
        plan_tiles(nc, k)
        expert_tiles(nc, a, k)
        causal_attention(nc, a, k)
        dense_experts(nc, a, k, out)


def constants():
    c = {}
    c["c_ident"] = np.eye(P, dtype=np.float32)
    c["c_upper"] = np.triu(np.ones((P, P), np.float32), 1)
    c["c_iota8"] = np.tile(np.arange(E, dtype=np.float32), (P, 1))
    c["c_region"] = np.tile(np.arange(E, dtype=np.float32) * T, (P, 1))
    c["c_above"] = np.triu(np.full((P, P), -1e30, np.float32), 1)
    c["c_order"] = np.arange(T, dtype=np.int32)
    token = np.arange(P)[:, None, None] + P * np.arange(POS)[None, :, None] + S * np.arange(B)[None, None, :]
    c["c_token"] = token.reshape(P, NT).astype(np.int32)
    c["c_head_mask"] = (np.arange(P)[:, None] // HEAD == np.arange(HEADS // KD)[None, :]).astype(np.float32)
    v = np.zeros((P, PCH, MAXH * VW), np.float32)
    for r in range(HEADS * KEYS):
        v[r % P, r // P, (r // KEYS - chunk_heads(r // P)[0]) * VW + HEAD] = 1.0
    c["c_values"] = v
    return c


def laid_out(x):
    a = {n: np.ascontiguousarray(v) for n, v in x.items()}
    t = {"x": a["x"].reshape(T, D), "mask": a["mask_1x1xSxS2_ik1"].reshape(S, KEYS),
         "ctx": a["ctx_1024"], "ctxT": a["ctx_1024"].transpose(2, 0, 1)}
    t["gates"] = np.stack([a["g_xattn"], a["g_ffn"]], 1).reshape(4)
    for n in ("L0_xattn_bq", "L0_xattn_bk"):
        t[n] = a[n].reshape(KD, P).T
    for n in ("L0_xattn_bv", "L0_xattn_bo",
              "L0_ffn_gate_w", "L0_ffn_ew1", "L0_ffn_ew2", "L0_ffn_ew3", "L0_ffn_sw1", "L0_ffn_sw2",
              "L0_ffn_sw3", "L1_xattn_q_w", "L1_xattn_k_w", "L1_xattn_norm_w", "L1_xattn_gate_b",
              "L1_ffn_gate_W", "L1_ffn_W1", "L1_ffn_W2", "L1_ffn_Ws1", "L1_ffn_Ws2"):
        t[n] = a[n]
    t["L1_ffn_b1"] = np.concatenate([a["L1_ffn_b1"], a["L1_ffn_bs1"].reshape(1, H1)]).T
    t["L1_ffn_b2"] = np.concatenate([a["L1_ffn_b2"], a["L1_ffn_bs2"].reshape(1, D)])
    t["L1_ffn_route_scale"] = a["L1_ffn_route_scale"].reshape(1)
    for n in ("L0_xattn_wq", "L0_xattn_wk", "L0_xattn_wv", "L0_xattn_wo", "L1_xattn_gate_w"):
        t[n] = a[n].T
    return {n: np.ascontiguousarray(v) for n, v in {**t, **constants()}.items()}


def kernel(**inputs):
    from concourse import bacc
    from concourse.bass_utils import run_bass_kernel_spmd

    nc = bacc.Bacc("TRN2", target_bir_lowering=False, num_devices=1)
    arrays = {f"in_{n}": v for n, v in laid_out({n: np.asarray(v) for n, v in inputs.items()}).items()}
    a = {n[3:]: nc.dram_tensor(n, v.shape, mybir.dt.from_np(v.dtype), kind="ExternalInput").ap()
         for n, v in arrays.items()}
    out = nc.dram_tensor("out_0", (B, S, D), F32, kind="ExternalOutput").ap()
    flamingo(nc, a, out.rearrange("b s d -> (b s) d"))
    result = run_bass_kernel_spmd(nc, [arrays], core_ids=[0])
    return result.results[0]["out_0"]
```

```python
from contextlib import ExitStack

import numpy as np

import concourse.bass as bass
from concourse import mybir

F32 = mybir.dt.float32
F32R = mybir.dt.float32r
I32 = mybir.dt.int32
U32 = mybir.dt.uint32
ACT = mybir.ActivationFunctionType
ALU = mybir.AluOpType
AX = mybir.AxisListType

P = 128
B, S, D = 4, 1024, 256
KEYS = 77
HEADS, HEAD = 16, 16
KD = D // P
POS = S // P
NT = B * POS
E = 8
H0 = 512
H1 = 128
EPS_LN = 1e-5
EPS_RMS = 1e-6
MASKED = -10000.0
BANK = 512

PER_BANK = 6
GROUP = PER_BANK * KEYS
EVEN = KEYS + KEYS % 2
PCH = -(-HEADS * KEYS // P)
VW = HEAD + 1
MAXH = 3

T = B * S
SPARE_ROWS = 1024
ROWS = E * T + SPARE_ROWS
PAD = 16
TILES = 2 * T // P + E


def chunk_heads(c):
    first = c * P // KEYS
    return first, min((c * P + P - 1) // KEYS, HEADS - 1) - first + 1


class Step:

    def __init__(self, round_, slot, width):
        self.round, self.slot, self.width = round_, slot, width

    @property
    def index(self):
        return self.round * self.width + self.slot

    @property
    def count(self):
        return self.round * self.width + (self.slot + 1)

    def before(self, back):
        return self.round * self.width + (self.slot + 1 - back)

    def after(self, back):
        return not isinstance(self.round, int) or self.index >= back


def pipeline(eng, tiles, depth, width, body, pause=None):
    first = -(-depth // width) * width
    last = tiles // width * width

    def fixed(s):
        def at(lag):
            t = s - lag
            return Step(t // width, t % width, width) if 0 <= t < tiles else None
        return at

    for s in range(first):
        body(fixed(s))
    cuts = [first, last]
    if pause:
        cuts.insert(1, pause[0])
    for n, (start, end) in enumerate(zip(cuts, cuts[1:])):
        if n:
            pause[1]()
        with eng.Fori(start // width, end // width) as i:
            for p in range(width):
                body(lambda lag: Step(i + (p - lag) // width, (p - lag) % width, width))
    for s in range(last, tiles + depth):
        body(fixed(s))


def three_passes(pe, out, left, right, start, stop):
    pe.matmul(out, left[0], right[0], start=start, stop=False, skip_group_check=True)
    pe.matmul(out, left[0], right[1], start=False, stop=False, skip_group_check=True)
    return pe.matmul(out, left[1], right[0], start=False, stop=stop, skip_group_check=True)


def wait_apart(eng, k, *waits):
    waits = [(sem, value if isinstance(value, int) else eng.to_reg(value)) for sem, value in waits]
    eng.wait_ge(k.started, 1)
    for sem, value in waits:
        eng.wait_ge(sem, value)


def run(at, *stages):
    for lag, stage in stages:
        t = at(lag)
        if t:
            stage(t)


class Bank:

    def __init__(self, tiles, users):
        self.tiles, self.users = tiles, users

    def last(self, name, t, lag=None):
        names = [u[0] for u in self.users]
        at = names.index(name) if name in names else len(names)
        lag = self.users[at][1] if lag is None else lag
        for back in range(3 * len(names)):
            i = at - 1 - back
            _, other, sem = self.users[i % len(names)]
            shift = lag - other + i // len(names)
            if isinstance(t.round, int):
                if not 0 <= t.index + shift < self.tiles:
                    continue
            return sem, t.before(-shift)
        return None

    def used(self, name, t):
        return self.last(name, t) is not None

    def freed(self, name, t, lag=None):
        return self.last(name, t, lag)


class Named:
    pass


class Scope:

    def __init__(self, nc, prefix):
        self.nc, self.prefix, self.stack = nc, prefix, ExitStack()
        self.held = []

    def __enter__(self):
        return self

    def __exit__(self, *a):
        done = self.stack.__exit__(*a)
        if self.held:
            self.nc.clear_and_free_semaphores(self.held)
            self.nc.all_engine_barrier()
        return done

    def sb(self, name, shape, dt=F32):
        return self.stack.enter_context(self.nc.sbuf_tensor(f"{self.prefix}_{name}", shape, dt))

    def ps(self, name, shape, dt=F32):
        return self.stack.enter_context(self.nc.psum_tensor(f"{self.prefix}_{name}", shape, dt))

    def sem(self, name):
        self.held.append(self.nc.alloc_semaphore(f"{self.prefix}_{name}"))
        return self.held[-1]

    def sems(self, names):
        return [self.sem(name) for name in names.split()]

    def block(self):
        return self.stack.enter_context(self.nc.Block())




def allocate_kept(nc, s):
    k = Named()
    k.ident = s.sb("ident", [P, P])
    k.neghalf = s.sb("neghalf", [P, 1])
    k.iota8 = s.sb("iota8", [P, E])
    k.tanh_g = s.sb("tanh_g", [P, 4])
    k.count = s.sb("count", [P, 5, E])
    k.slots = s.sb("slots", [P, POS * 2 * B], I32)
    k.weights = s.sb("weights", [P, POS * 2 * B])
    k.plan = s.sb("plan", [1, 2, PAD + TILES + PAD], I32)
    k.gates = s.sb("gates", [P, NT * (E + 1)])
    k.ones32 = s.sb("ones32", [P, NT])
    k.eps = s.sb("eps", [P, 2])
    k.started = s.sem("started")
    k.x1 = nc.dram_tensor("x1_scratch", (T, D), F32, kind="Internal").ap()
    k.xn1T = nc.dram_tensor("xn1T_scratch", (D, T), F32, kind="Internal").ap()
    k.x1s = nc.dram_tensor("x1s_scratch", (T, D), F32, kind="Internal").ap()
    k.xn = nc.dram_tensor("xn_scratch", (T, D), F32, kind="Internal").ap()
    k.table = nc.dram_tensor("table_scratch", (ROWS, 1), I32, kind="Internal").ap()
    k.y = nc.dram_tensor("y_scratch", (TILES * P, D), F32, kind="Internal").ap()
    k.x3 = nc.dram_tensor("x3_scratch", (T, D), F32, kind="Internal").ap()
    k.xn4T = nc.dram_tensor("xn4T_scratch", (D, T), F32, kind="Internal").ap()
    return k


def prepare_cross(nc, a, k, w):
    with Scope(nc, "prep") as s:
        wkT = s.sb("wkT", [P, KD, D])
        wvT = s.sb("wvT", [P, KD, D])
        wq_raw = s.sb("wq_raw", [P, KD, D])
        wo_raw = s.sb("wo_raw", [P, KD, D])
        wo_scaled = s.sb("wo_scaled", [P, KD, D])
        ctxT = s.sb("ctxT", [P, KD, B, KEYS])
        bk = s.sb("bk", [P, KD])
        bv = s.sb("bv", [P, D])
        bo = s.sb("bo", [P, D])
        g = s.sb("g", [P, 4])
        head_mask = s.sb("head_mask", [P, HEADS // KD])
        keysT = s.sb("keysT", [P, KD, B * KEYS])
        keysT_hi = s.sb("keysT_hi", [P, KD, B * KEYS], F32R)
        keysT_lo = s.sb("keysT_lo", [P, KD, B * KEYS], F32R)
        values = s.sb("values", [KEYS, B, D])
        zeros = s.sb("zeros", [P, ROWS // P], I32)
        k_ps = s.ps("k_ps", [P, KD, BANK])
        v_ps = s.ps("v_ps", [P, B, D])

        loaded = s.sem("loaded")
        pattern_loaded = s.sem("pattern_loaded")
        zeros_set = s.sem("zeros_set")
        table_cleared = s.sem("table_cleared")
        tanh_ready = s.sem("tanh_ready")
        keys_done = s.sem("keys_done")
        values_done = s.sem("values_done")
        keysT_ready = s.sem("keysT_ready")
        keys_hi_ready = s.sem("keys_hi_ready")
        keys_lo_ready = s.sem("keys_lo_ready")
        values_ready = s.sem("values_ready")
        values_placed = s.sem("values_placed")
        wo_scaled_ready = s.sem("wo_scaled_ready")
        w_hi_ready = s.sem("w_hi_ready")
        const_set = s.sem("const_set")
        prepared = s.sem("prepared")

        loads = [
            (ctxT[:, :, :, :], a["ctxT"].rearrange("(k p) b n -> p k b n", p=P)),
            (wkT[:, :, :], a["L0_xattn_wk"].rearrange("(k p) n -> p k n", p=P)),
            (wvT[:, :, :], a["L0_xattn_wv"].rearrange("(k p) n -> p k n", p=P)),
            (bk[:, :], a["L0_xattn_bk"]),
            (bv[:, :], a["L0_xattn_bv"].partition_broadcast(P)),
            (head_mask[:, :], a["c_head_mask"]),
            (wq_raw[:, :, :], a["L0_xattn_wq"].rearrange("(k p) n -> p k n", p=P)),
            (wo_raw[:, :, :], a["L0_xattn_wo"].rearrange("(k p) n -> p k n", p=P)),
            (bo[:, :], a["L0_xattn_bo"].partition_broadcast(P)),
            (g[:, :], a["gates"].partition_broadcast(P)),
            (w.bq[:, :], a["L0_xattn_bq"]),
            (w.mask[:, :].rearrange("p (t n) -> p t n", n=KEYS), a["mask"].rearrange("(t p) n -> p t n", p=P)),
            (w.gate[:, :, :], a["L0_ffn_gate_w"].rearrange("(k p) n -> p k n", p=P)),
            (w.token[:, :], a["c_token"]),
            (w.upper[:, :], a["c_upper"]),
            (k.ident[:, :], a["c_ident"]),
            (k.iota8[:, :], a["c_iota8"]),
            (k.count[:, B, :], a["c_region"]),
        ]
        block = s.block()

        @block.sync
        def _(sp):
            for to, of in loads:
                sp.dma_start(to, of).then_inc(loaded, 16)
            for b in range(B):
                sp.dma_start(w.values[:, b, :, :], a["c_values"]).then_inc(pattern_loaded, 16)
            sp.wait_ge(pattern_loaded, 16 * B)
            sp.wait_ge(values_ready, 1)
            placed = 0
            for h in range(HEADS):
                r = h * KEYS
                while r < (h + 1) * KEYS:
                    c = r // P
                    n = min((h + 1) * KEYS, (c + 1) * P) - r
                    col = (h - chunk_heads(c)[0]) * VW
                    sp.dma_start(w.values[r - c * P:r - c * P + n, :, c, col:col + HEAD],
                                 values[r - h * KEYS:r - h * KEYS + n, :, h * HEAD:(h + 1) * HEAD]
                                 ).then_inc(values_placed, 16)
                    placed += 1
                    r += n
            sp.wait_ge(values_placed, 16 * placed)

        @block.gpsimd
        def _(pool):
            pool.memset(zeros[:, :], 0).then_inc(zeros_set, 1)
            pool.memset(w.masked[:, :, :], MASKED * HEAD ** 0.5).then_inc(const_set, 1)
            pool.memset(w.shifted[:, :, HEADS * KEYS:], 0.0).then_inc(const_set, 1)
            pool.memset(k.ones32[:, :], 1.0).then_inc(k.started, 1)
            pool.memset(k.neghalf[:, :], -0.5).then_inc(const_set, 1)
            pool.memset(k.eps[:, 0:1], EPS_LN).then_inc(const_set, 1)
            pool.memset(k.eps[:, 1:2], EPS_RMS).then_inc(const_set, 1)
            pool.memset(w.ones[:, :], 1.0).then_inc(const_set, 1)
            pool.wait_ge(zeros_set, 1)
            pool.dma_start(k.table.rearrange("(p n) o -> p (n o)", p=P),
                           zeros[:, :]).then_inc(table_cleared, 16)
            pool.wait_ge(loaded, 16 * len(loads))
            pool.tensor_copy(w.wq[0][:, :, :], wq_raw[:, :, :]).then_inc(w_hi_ready, 1)
            pool.wait_ge(wo_scaled_ready, 1)
            pool.tensor_copy(w.wo[0][:, :, :], wo_scaled[:, :, :]).then_inc(w_hi_ready, 1)
            pool.wait_ge(table_cleared, 16)

        @block.tensor
        def _(pe):
            pe.wait_ge(loaded, 16 * len(loads))
            for c in range(KD):
                for kk in range(KD):
                    mm = pe.matmul(k_ps[:, c, 0:B * KEYS], wkT[:, kk, c * P:(c + 1) * P],
                                   ctxT[:, kk, :, :].rearrange("p b n -> p (b n)"),
                                   start=(kk == 0), stop=(kk == KD - 1))
            mm.then_inc(keys_done, 1)
            for b in range(B):
                for kk in range(KD):
                    mm = pe.matmul(v_ps[0:KEYS, b, :], ctxT[:, kk, b, :], wvT[:, kk, :],
                                   start=(kk == 0 and b % 2 == 0), stop=(kk == KD - 1),
                                   skip_group_check=True)
            mm.then_inc(values_done, 1)

        @block.scalar
        def _(act):
            act.wait_ge(loaded, 16 * len(loads))
            act.activation(k.tanh_g[:, :], g[:, :], ACT.Tanh).then_inc(tanh_ready, 1)
            act.wait_ge(keys_done, 1)
            for c in range(KD):
                act.activation(keysT[:, c, :], k_ps[:, c, 0:B * KEYS], ACT.Identity,
                               bias=bk[:, c:c + 1]).then_inc(keysT_ready, 1)
            act.wait_ge(keysT_ready, KD)
            act.activation(keysT_hi[:, :, :], keysT[:, :, :], ACT.Copy).then_inc(keys_hi_ready, 1)

        @block.vector
        def _(dve):
            dve.wait_ge(tanh_ready, 1)
            dve.tensor_scalar(wo_scaled[:, :, :], wo_raw[:, :, :], k.tanh_g[:, 0:1], None,
                              ALU.mult).then_inc(wo_scaled_ready, 1)
            dve.tensor_scalar(w.bo[:, :], bo[:, :], k.tanh_g[:, 0:1], None, ALU.mult).then_inc(prepared, 1)
            dve.wait_ge(values_done, 1)
            dve.tensor_tensor(values[:, :, :], v_ps[0:KEYS, :, :],
                              bv[0:KEYS, :].unsqueeze(1).to_broadcast([KEYS, B, D]),
                              ALU.add).then_inc(values_ready, 1)
            dve.wait_ge(keys_hi_ready, 1)
            dve.tensor_tensor(keysT_lo[:, :, :], keysT[:, :, :], keysT_hi[:, :, :].bitcast(F32),
                              ALU.subtract).then_inc(keys_lo_ready, 1)
            dve.wait_ge(keys_lo_ready, 1)
            for c in range(KD):
                for b in range(B):
                    for part, of in ((0, keysT_hi), (1, keysT_lo)):
                        src = of[:, c, b * KEYS:(b + 1) * KEYS].bitcast(F32)
                        dve.tensor_tensor(
                            w.keys[part][:, b, c, :].rearrange("p (h n) -> p h n", n=KEYS),
                            src.unsqueeze(1).to_broadcast([P, HEADS // KD, KEYS]),
                            head_mask[:, :].unsqueeze(2).to_broadcast([P, HEADS // KD, KEYS]),
                            ALU.mult).then_inc(prepared, 1)
            dve.wait_ge(w_hi_ready, 2)
            dve.tensor_tensor(w.wq[1][:, :, :], wq_raw[:, :, :], w.wq[0][:, :, :].bitcast(F32),
                              ALU.subtract).then_inc(prepared, 1)
            dve.tensor_tensor(w.wo[1][:, :, :], wo_scaled[:, :, :], w.wo[0][:, :, :].bitcast(F32),
                              ALU.subtract).then_inc(prepared, 1)


def cross_attention(nc, a, k):
    with Scope(nc, "cross") as s:
        w = Named()
        w.wq = [s.sb(f"wq{i}", [P, KD, D], F32R) for i in range(2)]
        w.wo = [s.sb(f"wo{i}", [P, KD, D], F32R) for i in range(2)]
        w.keys = [s.sb(f"keys{i}", [P, B, KD, HEADS // KD * KEYS], F32R) for i in range(2)]
        w.values = s.sb("values", [P, B, PCH, MAXH * VW])
        w.bq = s.sb("bq", [P, KD])
        w.bo = s.sb("bo", [P, D])
        w.gate = s.sb("gate", [P, KD, E])
        w.mask = s.sb("mask", [P, POS * KEYS], I32)
        w.token = s.sb("token", [P, POS * B], I32)
        w.upper = s.sb("upper", [P, P])
        w.ones = s.sb("ones", [P, P])
        w.masked = s.sb("masked", [P, 2, HEADS * KEYS])
        scores = s.ps("scores", [P, 3, BANK])
        w.shifted = shifted = s.sb("shifted", [P, 2, PCH * P])
        prepare_cross(nc, a, k, w)

        mask_now = s.sb("mask_now", [P, KEYS], I32)
        x = s.sb("x", [P, 4, D])
        x_again = s.sb("x_again", [P, 4, D])
        stats = s.sb("stats", [P, 4, 6])
        moments = s.sb("moments", [P, 4, 2])
        var_eps = s.sb("var_eps", [P, 4])
        rstd = s.sb("rstd", [P, 4])
        shift_x = s.sb("shift_x", [P, 4])
        shift_x1 = s.sb("shift_x1", [P, 4])
        xn = s.sb("xn", [P, 2, D])
        xT = [s.sb(f"xT{i}", [P, 2, KD * P], F32R) for i in range(2)]
        qT = [s.sb(f"qT{i}", [P, 2, KD * P], F32R) for i in range(2)]
        rowmax = s.sb("rowmax", [P, 2, HEADS])
        probs = s.sb("probs", [P, 2, PCH * P])
        probsT = s.sb("probsT", [P, 2, PCH * P])
        rden = s.sb("rden", [P, 2, HEADS])
        att = s.sb("att", [P, 2, D])
        attT = [s.sb(f"attT{i}", [P, 2, KD * P], F32R) for i in range(2)]
        base = s.sb("base", [P, 2, D])
        x1 = s.sb("x1", [P, 4, D])
        stats1 = s.sb("stats1", [P, 4, 6])
        moments1 = s.sb("moments1", [P, 4, 2])
        var_eps1 = s.sb("var_eps1", [P, 4])
        rstd1 = s.sb("rstd1", [P, 4])
        xn1 = s.sb("xn1", [P, 4, D])
        xn1T = s.sb("xn1T", [P, 2, KD * P])
        logits = s.sb("logits", [P, 4, E])
        top = s.sb("top", [P, 4, 8])
        top_at = s.sb("top_at", [P, 4, 8], U32)
        gap = s.sb("gap", [P, 4])
        gap_exp = s.sb("gap_exp", [P, 4])
        total = s.sb("total", [P, 4])
        rtotal = s.sb("rtotal", [P, 4])
        chosen_at = s.sb("chosen_at", [P, 4, 2])
        chosen = s.sb("chosen", [P, 4, 2, E])
        either = s.sb("either", [P, 4, E])
        rank = s.sb("rank", [P, 4, E])
        ranked = s.sb("ranked", [P, 4, 2, E])
        slot_f = s.sb("slot_f", [P, 4, 2])
        slot = s.sb("slot", [P, 2 * B], I32)
        token = s.sb("token_now", [P, 4], I32)

        turn_ps = s.ps("turn_ps", [P, BANK])
        q_ps = s.ps("q_ps", [P, BANK])
        pT_ps = s.ps("pT_ps", [P, 2, BANK])
        pv_ps = s.ps("pv_ps", [P, BANK])

        q = Named()
        (q.shift_ready, q.shift1_ready) = s.sems("shift_ready shift1_ready")
        (q.stats_ready, q.moments_ready, q.var_ready, q.rstd_ready, q.xn_ready) = s.sems(
            "stats_ready moments_ready var_ready rstd_ready xn_ready")
        (q.xT_done, q.xT_hi, q.xT_lo, q.q_done, q.q_hi, q.q_lo, q.scores_done) = s.sems(
            "xT_done xT_hi xT_lo q_done q_hi q_lo scores_done")
        (q.masked_ready, q.rowmax_ready, q.shifted_ready, q.refilled, q.probs_ready) = s.sems(
            "masked_ready rowmax_ready shifted_ready refilled probs_ready")
        (q.pT_done, q.pT_ready, q.pv_done, q.rden_ready, q.att_ready, q.attT_done) = s.sems(
            "pT_done pT_ready pv_done rden_ready att_ready attT_done")
        (q.attT_hi, q.attT_lo, q.proj_done, q.base_ready, q.x1_ready, q.stats1_ready) = s.sems(
            "attT_hi attT_lo proj_done base_ready x1_ready stats1_ready")
        (q.moments1_ready, q.var1_ready, q.rstd1_ready, q.xn1_ready, q.xn1T_done) = s.sems(
            "moments1_ready var1_ready rstd1_ready xn1_ready xn1T_done")
        (q.xn1T_ready, q.logits_done, q.logits_ready, q.top_ready, q.top_at_ready) = s.sems(
            "xn1T_ready logits_done logits_ready top_ready top_at_ready")
        (q.gap_ready, q.gap_exp_ready, q.total_ready, q.rtotal_ready, q.weight_ready) = s.sems(
            "gap_ready gap_exp_ready total_ready rtotal_ready weight_ready")
        (q.weights_ready, q.chosen_at_ready, q.chosen_ready, q.either_ready) = s.sems(
            "weights_ready chosen_at_ready chosen_ready either_ready")
        (q.ranks_done, q.count_ready, q.rank_ready, q.ranked_ready, q.slot_f_ready) = s.sems(
            "ranks_done count_ready rank_ready ranked_ready slot_f_ready")
        (q.slot_ready, q.token_ready, q.table_written, q.slots_kept, q.counts_ready) = s.sems(
            "slot_ready token_ready table_written slots_kept counts_ready")
        q.mask_copied = s.sem("mask_copied")
        x_loaded = [s.sem(f"x_loaded{i}") for i in range(4)]
        x_reloaded = [s.sem(f"x_reloaded{i}") for i in range(4)]
        x1_stored = [s.sem(f"x1_stored{i}") for i in range(4)]
        xn1T_stored = [s.sem(f"xn1T_stored{i}") for i in range(2)]
        xn1_stored = [s.sem(f"xn1_stored{i}") for i in range(4)]

        def rows(t):
            return bass.ds(t.round * P + t.slot * S, P)

        DEPTH = 22
        turn_bank = Bank(NT, [("att", 12, q.attT_lo), ("xn", 5, q.xT_lo), ("xn1", 16, q.xn1T_ready)])
        q_bank = Bank(NT, [("queries", 7, q.q_lo), ("proj", 13, q.x1_ready)])
        pv_bank = Bank(NT, [("attend", 11, q.att_ready), ("logits", 18, q.logits_ready)])
        HALF = HEADS // KD
        block = s.block()

        @block.sync
        def _(sp):
            def load(t):
                if t.after(4):
                    sp.wait_ge(q.xn_ready, t.before(4))
                sp.dma_start(x[:, t.slot, :], a["x"][rows(t), :]).then_inc(x_loaded[t.slot], 16)

            def load_again(t):
                if t.after(4):
                    sp.wait_ge(q.base_ready, t.before(4))
                sp.dma_start(x_again[:, t.slot, :], a["x"][rows(t), :]).then_inc(x_reloaded[t.slot], 16)

            def store_x1(t):
                sp.wait_ge(q.x1_ready, t.count)
                sp.dma_start(k.x1[rows(t), :], x1[:, t.slot, :]).then_inc(x1_stored[t.slot], 16)

            def store_xn1T(t):
                wait_apart(sp, k, (q.xn1T_ready, t.count))
                sp.dma_start(k.xn1T.rearrange("(k p) t -> p k t", p=P)[:, :, rows(t)],
                             xn1T[:, t.slot % 2, :].rearrange("p (k t) -> p k t", k=KD)
                             ).then_inc(xn1T_stored[t.slot % 2], 16)

            def store_xn1(t):
                sp.wait_ge(q.xn1_ready, t.count)
                sp.dma_start(k.xn[rows(t), :], xn1[:, t.slot, :]).then_inc(xn1_stored[t.slot], 16)

            def body(at):
                run(at, (15, store_xn1), (13, store_x1), (17, store_xn1T), (7, load_again), (0, load))

            pipeline(sp, NT, DEPTH, 4, body)
            for i in range(4):
                sp.wait_ge(x1_stored[i], 16 * POS)
                sp.wait_ge(xn1_stored[i], 16 * POS)
            for i in range(2):
                sp.wait_ge(xn1T_stored[i], 16 * (NT // 2))

        @block.gpsimd
        def _(pool):
            def shift(t):
                i = t.slot % 2
                pool.wait_ge(q.rowmax_ready, t.count)
                if t.after(2):
                    pool.wait_ge(q.probs_ready, t.before(2))
                pool.tensor_tensor(
                    shifted[:, i, 0:HEADS * KEYS].rearrange("p (h n) -> p h n", n=KEYS),
                    w.masked[:, i, :].rearrange("p (h n) -> p h n", n=KEYS),
                    rowmax[:, i, :].unsqueeze(2).to_broadcast([P, HEADS, KEYS]),
                    ALU.subtract).then_inc(q.shifted_ready, 1)
                if t.slot >= 2:
                    wait_apart(pool, k, (q.shifted_ready, t.count))
                    pool.memset(w.masked[:, i, :], MASKED * HEAD ** 0.5).then_inc(q.refilled, 1)

            def residual(t):
                pool.wait_ge(x_reloaded[t.slot], t.round * 16 + 16)
                if t.after(2):
                    pool.wait_ge(q.x1_ready, t.before(2))
                pool.tensor_tensor(base[:, t.slot % 2, :], x_again[:, t.slot, :], w.bo[:, :],
                                   ALU.add).then_inc(q.base_ready, 1)

            def reciprocal_std(t, moments, var, std, shift, moments_ready, var_ready, rstd_ready, shift_ready):
                i = t.slot
                pool.wait_ge(moments_ready, t.count)
                pool.tensor_tensor(var[:, i:i + 1], moments[:, i, 1:2], k.eps[:, 0:1],
                                   ALU.add).then_inc(var_ready, 1)
                pool.wait_ge(var_ready, t.count)
                pool.tensor_tensor(std[:, i:i + 1], var[:, i:i + 1], k.neghalf[:, :],
                                   ALU.pow).then_inc(rstd_ready, 1)
                wait_apart(pool, k, (rstd_ready, t.count))
                pool.tensor_scalar(shift[:, i:i + 1], moments[:, i, 0:1], std[:, i:i + 1], -1.0,
                                   ALU.mult, ALU.mult).then_inc(shift_ready, 1)

            def rstd_x(t):
                reciprocal_std(t, moments, var_eps, rstd, shift_x, q.moments_ready, q.var_ready, q.rstd_ready,
                               q.shift_ready)

            def rstd_x1(t):
                reciprocal_std(t, moments1, var_eps1, rstd1, shift_x1, q.moments1_ready, q.var1_ready,
                               q.rstd1_ready, q.shift1_ready)

            def scatter(t):
                r, b = t.round, t.slot
                if b == 0:
                    if t.after(4):
                        pool.wait_ge(q.table_written, r * (16 * 2 * B))
                    pool.tensor_copy(token[:, :], w.token[:, bass.ds(r * B, B)]).then_inc(q.token_ready, 1)
                wait_apart(pool, k, (q.token_ready, r + 1), (q.slot_ready, r + 1))
                for c in range(2):
                    pool.indirect_dma_start(
                        out=k.table[:, :],
                        out_offset=bass.IndirectOffsetOnAxis(ap=slot[:, 2 * b + c:2 * b + c + 1], axis=0),
                        in_=token[:, b:b + 1], in_offset=None).then_inc(q.table_written, 16)

            def body(at):
                run(at, (14, rstd_x1), (9, shift), (2, rstd_x), (11, residual), (22, scatter))

            pipeline(pool, NT, DEPTH, 4, body)
            pool.wait_ge(q.table_written, NT * 2 * 16)

        @block.tensor
        def _(pe):
            def turn(of, done):
                for c in range(KD):
                    mm = pe.transpose(turn_ps[:, c * P:(c + 1) * P], of[:, c * P:(c + 1) * P], k.ident[:, :])
                mm.then_inc(done, 1)

            def turn_att(t):
                pe.wait_ge(q.att_ready, t.count)
                if turn_bank.used("att", t):
                    pe.wait_ge(*turn_bank.freed("att", t))
                turn(att[:, t.slot % 2, :], q.attT_done)

            def turn_xn(t):
                pe.wait_ge(q.xn_ready, t.count)
                if turn_bank.used("xn", t):
                    pe.wait_ge(*turn_bank.freed("xn", t))
                turn(xn[:, t.slot % 2, :], q.xT_done)

            def turn_xn1(t):
                pe.wait_ge(q.xn1_ready, t.count)
                if turn_bank.used("xn1", t):
                    pe.wait_ge(*turn_bank.freed("xn1", t))
                turn(xn1[:, t.slot, :], q.xn1T_done)

            def turn_probs(t):
                i = t.slot % 2
                pe.wait_ge(q.probs_ready, t.count)
                for group in range(3):
                    if group == 0 and t.after(1):
                        pe.wait_ge(q.pT_ready, t.index * 3)
                    if group == 2:
                        pe.wait_ge(q.pT_ready, t.index * 3 + 1)
                    for c in range(4 * group, min(4 * group + 4, PCH)):
                        mm = pe.transpose(pT_ps[:, group % 2, (c % 4) * P:(c % 4 + 1) * P],
                                          probs[:, i, c * P:(c + 1) * P], k.ident[:, :])
                    mm.then_inc(q.pT_done, 1)

            def queries(t):
                i = t.slot % 2
                pe.wait_ge(q.xT_lo, t.count)
                if q_bank.used("queries", t):
                    pe.wait_ge(*q_bank.freed("queries", t))
                for c in range(KD):
                    for kk in range(KD):
                        mm = three_passes(
                            pe, q_ps[:, c * P:(c + 1) * P],
                            [part[:, kk, c * P:(c + 1) * P] for part in w.wq],
                            [part[:, i, kk * P:(kk + 1) * P] for part in xT],
                            start=(kk == 0 and c == 0), stop=(kk == KD - 1))
                mm.then_inc(q.q_done, 1)

            def attend(t):
                i = t.slot % 2
                pe.wait_ge(q.pT_ready, t.index * 3 + 3)
                if pv_bank.used("attend", t):
                    pe.wait_ge(*pv_bank.freed("attend", t))
                wait_ranks(t, -8)
                for c in range(PCH):
                    h, n = chunk_heads(c)
                    mm = pe.matmul(pv_ps[:, h * VW:(h + n) * VW], probsT[:, i, c * P:(c + 1) * P],
                                   w.values[:, t.slot, c, 0:n * VW], start=(c == 0), stop=(c == PCH - 1),
                                   skip_group_check=True)
                mm.then_inc(q.pv_done, 1)

            def project(t):
                i = t.slot % 2
                pe.wait_ge(q.attT_lo, t.count)
                if q_bank.used("proj", t):
                    pe.wait_ge(*q_bank.freed("proj", t))
                for kk in range(KD):
                    mm = three_passes(pe, q_ps[:, 0:D],
                                      [part[:, i, kk * P:(kk + 1) * P] for part in attT],
                                      [part[:, kk, :] for part in w.wo],
                                      start=(kk == 0), stop=(kk == KD - 1))
                mm.then_inc(q.proj_done, 1)

            def score(t):
                i = t.slot % 2
                pe.wait_ge(q.q_lo, t.count)
                if t.after(1):
                    pe.wait_ge(q.masked_ready, t.before(1))
                for bank in range(3):
                    for c in range(KD):
                        h0 = max(bank * PER_BANK, c * HALF)
                        h1 = min((bank + 1) * PER_BANK, (c + 1) * HALF)
                        if h0 < h1:
                            o = (h0 - bank * PER_BANK) * KEYS
                            r = (h0 - c * HALF) * KEYS
                            n = (h1 - h0) * KEYS
                            mm = three_passes(
                                pe, scores[:, bank, o:o + n],
                                [part[:, i, c * P:(c + 1) * P] for part in qT],
                                [part[:, t.slot, c, r:r + n] for part in w.keys],
                                start=(o == 0), stop=True)
                mm.then_inc(q.scores_done, 1)

            def wait_ranks(t, ahead):
                rounds = t.round + (t.slot + ahead) // 4
                if not isinstance(rounds, int) or rounds > 0:
                    pe.wait_ge(q.count_ready, rounds)

            def gate_logits(t):
                i = t.slot % 2
                pe.wait_ge(q.xn1T_ready, t.count)
                if pv_bank.used("logits", t):
                    pe.wait_ge(*pv_bank.freed("logits", t))
                wait_ranks(t, -1)
                for kk in range(KD):
                    mm = pe.matmul(pv_ps[:, 0:E], xn1T[:, i, kk * P:(kk + 1) * P], w.gate[:, kk, :],
                                   start=(kk == 0), stop=(kk == KD - 1))
                mm.then_inc(q.logits_done, 1)

            def ranks(t):
                if t.slot != 3:
                    return
                pe.wait_ge(q.either_ready, t.round + 1)
                pe.wait_ge(*pv_bank.freed("end", t, 19))
                mask = either[:, :, :].rearrange("p b e -> p (b e)")
                pe.matmul(pv_ps[:, 0:4 * E], w.upper[:, :], mask, start=True, stop=True,
                          skip_group_check=True)
                pe.matmul(pv_ps[:, 4 * E:8 * E], w.ones[:, :], mask, start=False, stop=True,
                          skip_group_check=True).then_inc(q.ranks_done, 1)

            def body(at):
                run(at, (11, attend), (12, turn_att), (7, queries), (5, turn_xn), (10, turn_probs),
                    (13, project), (18, gate_logits), (8, score), (19, ranks), (16, turn_xn1))

            pipeline(pe, NT, DEPTH, 4, body)

        @block.scalar
        def _(act):
            def normalise_x(t):
                act.wait_ge(q.shift_ready, t.count)
                if t.after(2):
                    act.wait_ge(q.xT_done, t.before(2))
                act.activation(xn[:, t.slot % 2, :], x[:, t.slot, :], ACT.Identity,
                               scale=rstd[:, t.slot:t.slot + 1], bias=shift_x[:, t.slot:t.slot + 1]).then_inc(q.xn_ready, 1)

            def normalise_x1(t):
                i = t.slot
                act.wait_ge(q.shift1_ready, t.count)
                if t.after(4):
                    act.wait_ge(xn1_stored[i], t.round * 16)
                    act.wait_ge(q.xn1T_done, t.before(4))
                act.activation(xn1[:, i, :], x1[:, i, :], ACT.Identity, scale=rstd1[:, i:i + 1],
                               bias=shift_x1[:, i:i + 1]).then_inc(q.xn1_ready, 1)

            def att_hi(t):
                if t.after(2):
                    act.wait_ge(q.proj_done, t.before(2))
                act.wait_ge(q.attT_done, t.count)
                act.activation(attT[0][:, t.slot % 2, :], turn_ps[:, 0:D], ACT.Copy).then_inc(q.attT_hi, 1)

            def xn_hi(t):
                if t.after(2):
                    act.wait_ge(q.q_done, t.before(2))
                act.wait_ge(q.xT_done, t.count)
                act.activation(xT[0][:, t.slot % 2, :], turn_ps[:, 0:D], ACT.Copy).then_inc(q.xT_hi, 1)

            def exponent(t):
                i = t.slot % 2
                act.wait_ge(q.shifted_ready, t.count)
                if t.after(2):
                    act.wait_ge(q.pT_done, t.index * 3 - 3)
                act.activation(probs[:, i, :], shifted[:, i, 0:PCH * P], ACT.Exp,
                               scale=HEAD ** -0.5).then_inc(q.probs_ready, 1)

            def copy_probsT(t):
                i = t.slot % 2
                if t.after(2):
                    act.wait_ge(q.pv_done, t.before(2))
                for group in range(3):
                    n = min(4, PCH - 4 * group) * P
                    act.wait_ge(q.pT_done, t.index * 3 + group + 1)
                    act.activation(probsT[:, i, group * BANK:group * BANK + n], pT_ps[:, group % 2, 0:n],
                                   ACT.Copy).then_inc(q.pT_ready, 1)

            def q_hi(t):
                i = t.slot % 2
                if t.after(2):
                    act.wait_ge(q.scores_done, t.before(2))
                act.wait_ge(q.q_done, t.count)
                for c in range(KD):
                    cols = slice(c * P, (c + 1) * P)
                    ins = act.activation(qT[0][:, i, cols], q_ps[:, cols], ACT.Identity,
                                         bias=w.bq[:, c:c + 1])
                ins.then_inc(q.q_hi, 1)

            def copy_xn1T(t):
                if t.after(2):
                    act.wait_ge(q.logits_done, t.before(2))
                    act.wait_ge(xn1T_stored[t.slot % 2], t.round * 32 + (t.slot // 2) * 16)
                act.wait_ge(q.xn1T_done, t.count)
                act.activation(xn1T[:, t.slot % 2, :], turn_ps[:, 0:D], ACT.Copy).then_inc(q.xn1T_ready, 1)

            def gap_exponent(t):
                if t.slot == 3:
                    act.wait_ge(q.gap_ready, t.round + 1)
                    act.activation(gap_exp[:, :], gap[:, :], ACT.Exp).then_inc(q.gap_exp_ready, 1)

            def body(at):
                run(at, (10, exponent), (12, att_hi), (7, q_hi), (5, xn_hi), (10, copy_probsT),
                    (3, normalise_x), (16, copy_xn1T), (18, gap_exponent), (14, normalise_x1))

            pipeline(act, NT, DEPTH, 4, body)

        @block.vector
        def _(dve):
            def normalise_att(t):
                i = t.slot % 2
                dve.wait_ge(q.pv_done, t.count)
                pv = pv_ps[:, 0:HEADS * VW].rearrange("p (h n) -> p h n", n=VW)
                dve.reciprocal(rden[:, i, :], pv[:, :, HEAD]).then_inc(q.rden_ready, 1)
                dve.wait_ge(q.rden_ready, t.count)
                if t.after(2):
                    dve.wait_ge(q.attT_done, t.before(2))
                dve.tensor_tensor(att[:, i, :].rearrange("p (h n) -> p h n", n=HEAD), pv[:, :, 0:HEAD],
                                  rden[:, i, :].unsqueeze(2).to_broadcast([P, HEADS, HEAD]),
                                  ALU.mult).then_inc(q.att_ready, 1)

            def att_lo(t):
                i = t.slot % 2
                dve.wait_ge(q.attT_hi, t.count)
                dve.tensor_tensor(attT[1][:, i, :], turn_ps[:, 0:D], attT[0][:, i, :].bitcast(F32),
                                  ALU.subtract).then_inc(q.attT_lo, 1)

            def xn_lo(t):
                i = t.slot % 2
                dve.wait_ge(q.xT_hi, t.count)
                dve.tensor_tensor(xT[1][:, i, :], turn_ps[:, 0:D], xT[0][:, i, :].bitcast(F32),
                                  ALU.subtract).then_inc(q.xT_lo, 1)

            def q_lo(t):
                i = t.slot % 2
                dve.wait_ge(q.q_hi, t.count)
                for c in range(KD):
                    cols = slice(c * P, (c + 1) * P)
                    ins = dve.scalar_tensor_tensor(out=qT[1][:, i, cols], in0=q_ps[:, cols],
                                                   scalar=w.bq[:, c:c + 1],
                                                   in1=qT[0][:, i, cols].bitcast(F32),
                                                   op0=ALU.add, op1=ALU.subtract)
                ins.then_inc(q.q_lo, 1)

            def add_residual(t):
                i = t.slot
                dve.wait_ge(q.proj_done, t.count)
                dve.wait_ge(q.base_ready, t.count)
                if t.after(4):
                    dve.wait_ge(x1_stored[i], t.round * 16)
                    dve.wait_ge(q.xn1_ready, t.before(4))
                dve.tensor_tensor(x1[:, i, :], q_ps[:, 0:D], base[:, i % 2, :],
                                  ALU.add).then_inc(q.x1_ready, 1)

            def x1_moments(t):
                i = t.slot
                dve.wait_ge(q.x1_ready, t.count)
                dve.bn_stats(stats1[:, i, :], x1[:, i, :]).then_inc(q.stats1_ready, 1)
                wait_apart(dve, k, (q.stats1_ready, t.count))
                dve.bn_aggr(moments1[:, i, :], stats1[:, i, :]).then_inc(q.moments1_ready, 1)

            def mask_scores(t):
                i = t.slot % 2
                if t.slot == 0:
                    dve.tensor_copy(mask_now[:, :], w.mask[:, bass.ds(t.round * KEYS, KEYS)]
                                    ).then_inc(q.mask_copied, 1)
                waits = [(q.scores_done, t.count), (q.mask_copied, t.round + 1)]
                if t.after(2) and t.slot >= 2:
                    waits.append((q.shifted_ready, t.before(2)))
                elif t.after(4):
                    waits.append((q.refilled, t.round * 2 - (1 - t.slot)))
                wait_apart(dve, k, *waits)
                for bank in range(3):
                    n = min(PER_BANK, HEADS - bank * PER_BANK)
                    ins = dve.copy_predicated(
                        w.masked[:, i, bank * GROUP:bank * GROUP + n * KEYS].rearrange("p (h n) -> p h n", n=KEYS),
                        mask_now[:, :].unsqueeze(1).to_broadcast([P, n, KEYS]),
                        scores[:, bank, 0:n * KEYS].rearrange("p (h n) -> p h n", n=KEYS))
                ins.then_inc(q.masked_ready, 1)

            def row_maxima(t):
                i = t.slot % 2
                dve.wait_ge(q.masked_ready, t.count)
                if t.after(2):
                    dve.wait_ge(q.shifted_ready, t.before(2))
                dve.tensor_reduce(rowmax[:, i, :], w.masked[:, i, :].rearrange("p (h n) -> p h n", n=KEYS),
                                  AX.X, ALU.max).then_inc(q.rowmax_ready, 1)

            def x_moments(t):
                i = t.slot
                dve.wait_ge(x_loaded[i], t.round * 16 + 16)
                dve.bn_stats(stats[:, i, :], x[:, i, :]).then_inc(q.stats_ready, 1)
                wait_apart(dve, k, (q.stats_ready, t.count))
                dve.bn_aggr(moments[:, i, :], stats[:, i, :]).then_inc(q.moments_ready, 1)

            def top_two(t):
                i = t.slot
                dve.wait_ge(q.logits_done, t.count)
                dve.tensor_copy(logits[:, i, :], pv_ps[:, 0:E]).then_inc(q.logits_ready, 1)
                wait_apart(dve, k, (q.logits_ready, t.count))
                dve.max(top[:, i, :], logits[:, i, :]).then_inc(q.top_ready, 1)
                wait_apart(dve, k, (q.top_ready, t.count))
                dve.max_index(top_at[:, i, :], top[:, i, :], logits[:, i, :]).then_inc(q.top_at_ready, 1)

            def route(t):
                if t.slot != 3:
                    return
                r = t.round
                dve.wait_ge(q.top_at_ready, t.count)
                if t.after(4):
                    dve.wait_ge(q.gap_exp_ready, r)
                dve.tensor_tensor(gap[:, :], top[:, :, 1], top[:, :, 0], ALU.subtract).then_inc(q.gap_ready, 1)
                dve.tensor_copy(chosen_at[:, :, :], top_at[:, :, 0:2]).then_inc(q.chosen_at_ready, 1)
                dve.wait_ge(q.chosen_at_ready, r + 1)
                dve.tensor_tensor(chosen[:, :, :, :].rearrange("p b c e -> p (b c) e"),
                                  k.iota8[:, :].unsqueeze(1).to_broadcast([P, 2 * B, E]),
                                  chosen_at[:, :, :].rearrange("p b c -> p (b c)").unsqueeze(2)
                                  .to_broadcast([P, 2 * B, E]), ALU.is_equal).then_inc(q.chosen_ready, 1)
                dve.wait_ge(q.chosen_ready, r + 1)
                if t.after(4):
                    dve.wait_ge(q.ranks_done, r)
                dve.tensor_tensor(either[:, :, :], chosen[:, :, 0, :], chosen[:, :, 1, :],
                                  ALU.add).then_inc(q.either_ready, 1)
                dve.wait_ge(q.gap_exp_ready, r + 1)
                dve.tensor_scalar(total[:, :], gap_exp[:, :], 1.0, None, ALU.add).then_inc(q.total_ready, 1)
                dve.wait_ge(q.total_ready, r + 1)
                dve.reciprocal(rtotal[:, :], total[:, :]).then_inc(q.rtotal_ready, 1)
                dve.wait_ge(q.rtotal_ready, r + 1)
                here = k.weights[:, bass.ds(r * (2 * B), 2 * B)].rearrange("p (b c) -> p b c", c=2)
                dve.tensor_scalar(here[:, :, 0], rtotal[:, :], k.tanh_g[:, 1:2], None,
                                  ALU.mult).then_inc(q.weight_ready, 1)
                dve.scalar_tensor_tensor(out=here[:, :, 1], in0=gap_exp[:, :], scalar=k.tanh_g[:, 1:2],
                                         in1=rtotal[:, :], op0=ALU.mult, op1=ALU.mult
                                         ).then_inc(q.weights_ready, 1)

            def place(t):
                if t.slot != 3:
                    return
                r = t.round
                dve.tensor_copy(k.count[:, 0, :], k.count[:, B, :]).then_inc(q.counts_ready, 1)
                dve.wait_ge(q.ranks_done, r + 1)
                for b in range(B):
                    dve.wait_ge(q.counts_ready, r * (B + 1) + (b + 1))
                    dve.tensor_tensor(k.count[:, b + 1, :], k.count[:, b, :],
                                      pv_ps[:, (4 + b) * E:(5 + b) * E], ALU.add).then_inc(q.counts_ready, 1)
                dve.wait_ge(q.counts_ready, (r + 1) * (B + 1))
                dve.tensor_tensor(rank[:, :, :], k.count[:, 0:B, :],
                                  pv_ps[:, 0:4 * E].rearrange("p (b e) -> p b e", e=E),
                                  ALU.add).then_inc(q.count_ready, 1)
                dve.wait_ge(q.count_ready, r + 1)
                dve.tensor_tensor(ranked[:, :, :, :], chosen[:, :, :, :],
                                  rank[:, :, :].unsqueeze(2).to_broadcast([P, B, 2, E]),
                                  ALU.mult).then_inc(q.ranked_ready, 1)
                dve.wait_ge(q.ranked_ready, r + 1)
                dve.tensor_reduce(slot_f[:, :, :], ranked[:, :, :, :], AX.X, ALU.add
                                  ).then_inc(q.slot_f_ready, 1)
                dve.wait_ge(q.slot_f_ready, r + 1)
                if t.after(4):
                    dve.wait_ge(q.table_written, r * (16 * 2 * B))
                dve.tensor_copy(slot[:, :], slot_f[:, :, :].rearrange("p b c -> p (b c)")
                                ).then_inc(q.slot_ready, 1)
                dve.tensor_copy(k.slots[:, bass.ds(r * (2 * B), 2 * B)],
                                slot_f[:, :, :].rearrange("p b c -> p (b c)")).then_inc(q.slots_kept, 1)

            def body(at):
                run(at, (9, mask_scores), (12, att_lo), (9, row_maxima), (7, q_lo), (11, normalise_att),
                    (5, xn_lo), (13, add_residual), (1, x_moments), (18, top_two), (19, place),
                    (13, x1_moments), (18, route))

            pipeline(dve, NT, DEPTH, 4, body)


class Plan:

    def __init__(self, k, s):
        self.k = k
        self.W = W = POS * 2 * B
        self.counts = s.sb("counts", [P, E])
        self.upped = s.sb("upped", [P, E], I32)
        self.filled_i = s.sb("filled_i", [P, E], I32)
        self.sizes = s.sb("sizes", [P, E])
        self.ends = s.sb("ends", [P, E])
        self.tile = s.sb("tile", [1, TILES])
        self.passed = s.sb("passed", [1, TILES, E])
        self.passed_sizes = s.sb("passed_sizes", [1, TILES, E])
        self.expert = s.sb("expert", [1, TILES])
        self.start = s.sb("start", [1, TILES])
        self.local = s.sb("local", [1, TILES])
        self.row = s.sb("row", [1, TILES])
        self.region = s.sb("region", [P, E])
        self.step = s.sb("step", [P, E])
        self.at_least = s.sb("at_least", [P, W, E])
        self.steps = s.sb("steps", [P, W, E])
        self.moved = s.sb("moved", [P, W])
        self.table_rows = s.sb("table_rows", [P, W])
        self.numbered = s.sem("numbered")
        self.chain = s.sem("chain")

    def number(self, pool):
        pool.iota(self.tile[:, :], [[1, TILES]], base=0, channel_multiplier=0,
                  allow_small_or_imprecise_dtypes=True).then_inc(self.numbered, 1)

    def make(self, dve):
        k, W, chain = self.k, self.W, self.chain
        counts, sizes, ends, step, tile, passed = (self.counts, self.sizes, self.ends, self.step, self.tile,
                                                   self.passed)
        expert, row, table_rows = self.expert, self.row, self.table_rows
        dve.scalar_tensor_tensor(out=counts[:, :], in0=k.iota8[:, :], scalar=-float(T),
                                 in1=k.count[:, B, :], op0=ALU.mult, op1=ALU.add).then_inc(chain, 1)
        dve.wait_ge(chain, 1)
        dve.tensor_scalar(self.upped[:, :], counts[:, :], float(P - 1), None, ALU.add).then_inc(chain, 1)
        dve.wait_ge(chain, 2)
        dve.tensor_scalar(self.filled_i[:, :], self.upped[:, :], 7, None,
                          ALU.logical_shift_right).then_inc(chain, 1)
        dve.wait_ge(chain, 3)
        dve.tensor_copy(sizes[:, :], self.filled_i[:, :]).then_inc(chain, 1)
        dve.wait_ge(chain, 4)
        dve.tensor_copy(ends[:, 0:1], sizes[:, 0:1]).then_inc(chain, 1)
        for e in range(1, E):
            dve.wait_ge(chain, 4 + e)
            dve.tensor_tensor(ends[:, e:e + 1], ends[:, e - 1:e], sizes[:, e:e + 1], ALU.add
                              ).then_inc(chain, 1)
        n = 4 + E
        dve.wait_ge(chain, n)
        dve.wait_ge(self.numbered, 1)
        dve.tensor_tensor(passed[:, :, :], ends[0:1, :].unsqueeze(1).to_broadcast([1, TILES, E]),
                          tile[:, :].unsqueeze(2).to_broadcast([1, TILES, E]), ALU.is_le).then_inc(chain, 1)
        dve.tensor_scalar(self.region[:, :], k.iota8[:, :], float(T), None, ALU.mult).then_inc(chain, 1)
        dve.memset(step[:, 0:1], 0.0).then_inc(chain, 1)
        dve.memset(k.plan[:, :, :], 0).then_inc(chain, 1)
        dve.tensor_scalar(step[:, 1:E], sizes[:, 0:E - 1], float(P), -float(T), ALU.mult,
                          ALU.add).then_inc(chain, 1)
        dve.tensor_copy(table_rows[:, :], k.slots[:, :]).then_inc(chain, 1)
        dve.wait_ge(chain, n + 6)
        dve.tensor_reduce(expert[:, :], passed[:, :, :], AX.X, ALU.add).then_inc(chain, 1)
        dve.tensor_tensor(self.passed_sizes[:, :, :], passed[:, :, :],
                          sizes[0:1, :].unsqueeze(1).to_broadcast([1, TILES, E]), ALU.mult).then_inc(chain, 1)
        dve.tensor_tensor(self.at_least[:, :, :], table_rows[:, :].unsqueeze(2).to_broadcast([P, W, E]),
                          self.region[:, :].unsqueeze(1).to_broadcast([P, W, E]),
                          ALU.is_ge).then_inc(chain, 1)
        dve.wait_ge(chain, n + 9)
        dve.tensor_reduce(self.start[:, :], self.passed_sizes[:, :, :], AX.X, ALU.add).then_inc(chain, 1)
        dve.tensor_tensor(self.steps[:, :, :], self.at_least[:, :, :],
                          step[:, :].unsqueeze(1).to_broadcast([P, W, E]), ALU.mult).then_inc(chain, 1)
        dve.wait_ge(chain, n + 11)
        dve.tensor_tensor(self.local[:, :], tile[:, :], self.start[:, :], ALU.subtract).then_inc(chain, 1)
        dve.tensor_scalar(row[:, :], expert[:, :], float(T), None, ALU.mult).then_inc(chain, 1)
        dve.tensor_reduce(self.moved[:, :], self.steps[:, :, :], AX.X, ALU.add).then_inc(chain, 1)
        dve.wait_ge(chain, n + 14)
        dve.scalar_tensor_tensor(out=k.plan[:, 0, PAD:PAD + TILES], in0=self.local[:, :], scalar=float(P), in1=row[:, :],
                                 op0=ALU.mult, op1=ALU.add).then_inc(chain, 1)
        dve.tensor_tensor(k.slots[:, :], table_rows[:, :], self.moved[:, :], ALU.add).then_inc(chain, 1)
        dve.tensor_scalar(k.plan[:, 1, PAD:PAD + TILES], expert[:, :], float(E - 1), None, ALU.min).then_inc(chain, 1)


def shared_expert(nc, a, k, start_loading):
    with Scope(nc, "shared") as s:
        N = BANK
        SUB = N // P
        GROUPS = T // N
        CH = H0 // P
        plan = Plan(k, s)
        raw = [s.sb("w1", [P, KD, H0]), s.sb("w2", [P, KD, H0]), s.sb("w3", [P, CH, D])]
        w1 = [s.sb(f"w1_{i}", [P, KD, H0], F32R) for i in range(2)]
        w2 = [s.sb(f"w2_{i}", [P, KD, H0], F32R) for i in range(2)]
        w3 = [s.sb(f"w3_{i}", [P, CH, D], F32R) for i in range(2)]
        xT = s.sb("xT", [P, KD, N])
        xT_parts = [s.sb(f"xT{i}", [P, 2, KD, N], F32R) for i in range(2)]
        x1 = s.sb("x1", [P, SUB, D])
        x1s = s.sb("x1s", [P, SUB, D])
        act_h = s.sb("act_h", [P, 2, N])
        gated = s.sb("gated", [P, 2, N])
        gated_parts = [s.sb(f"gated{i}", [P, 2, N], F32R) for i in range(2)]
        h1_ps = s.ps("h1_ps", [P, 2, BANK])
        h2_ps = s.ps("h2_ps", [P, 2, BANK])
        y_ps = s.ps("y_ps", [P, SUB, BANK])
        weights_loaded = [s.sem(f"weights_loaded{i}") for i in range(3)]
        x_loaded = s.sem("x_loaded")
        x1_loaded = s.sem("x1_loaded")
        stored = s.sem("stored")
        q = Named()
        (q.w_hi, q.w_lo, q.x_hi, q.x_lo, q.h1_done, q.h2_done, q.act_ready) = s.sems(
            "w_hi w_lo x_hi x_lo h1_done h2_done act_ready")
        (q.gated_ready, q.g_hi, q.g_lo, q.y_done, q.added) = s.sems("gated_ready g_hi g_lo y_done added")
        LOAD, SPLIT, HIDDEN, OUT, STORE = 0, 3, 5, 6, 7
        DEPTH = 7
        UNITS = GROUPS * CH
        WIDTH = 2 * CH
        block = s.block()

        def group(t, ahead=0):
            return t.round * 2 + (t.slot // CH + ahead)

        def at_chunk(stage, chunk):
            return lambda t: stage(t) if t.slot % CH == chunk else None

        @block.sync
        def _(sp):
            def load(t):
                if t.after(CH):
                    sp.wait_ge(q.x_lo, group(t))
                sp.dma_start(xT[:, :, :], k.xn1T.rearrange("(k p) t -> p k t", p=P)
                             [:, :, bass.ds(group(t) * N, N)]).then_inc(x_loaded, 16)

            def load_x1(t):
                if t.after(CH):
                    sp.wait_ge(q.added, group(t) * SUB)
                sp.dma_start(x1[:, :, :], k.x1[bass.ds(group(t) * N, N), :]
                             .rearrange("(j p) d -> p j d", p=P)).then_inc(x1_loaded, 16)

            def store(t):
                sp.wait_ge(q.added, group(t, 1) * SUB)
                sp.dma_start(k.x1s[bass.ds(group(t) * N, N), :].rearrange("(j p) d -> p j d", p=P),
                             x1s[:, :, :]).then_inc(stored, 16)

            for i, name in enumerate(("L0_ffn_sw1", "L0_ffn_sw2", "L0_ffn_sw3")):
                sp.dma_start(raw[i][:, :, :], a[name].rearrange("(c p) n -> p c n", p=P)
                             ).then_inc(weights_loaded[i], 16)
            pipeline(sp, UNITS, DEPTH, WIDTH,
                     lambda at: run(at, (LOAD, at_chunk(load, 0)), (STORE, at_chunk(store, CH - 1)),
                                    (HIDDEN, at_chunk(load_x1, 1))))
            sp.wait_ge(stored, 16 * GROUPS)

        @block.gpsimd
        def _(pool):
            plan.number(pool)
            start_loading(pool)

        @block.tensor
        def _(pe):
            def hidden(t):
                i, c, g = t.slot % 2, t.slot % CH, t.slot // CH
                pe.wait_ge(q.x_lo, group(t, 1))
                for w, out, done, free in ((w1, h1_ps, q.h1_done, q.act_ready),
                                           (w2, h2_ps, q.h2_done, q.gated_ready)):
                    if t.after(2):
                        pe.wait_ge(free, t.before(2))
                    for kk in range(KD):
                        mm = three_passes(pe, out[:, i, :], [part[:, kk, c * P:(c + 1) * P] for part in w],
                                          [part[:, g, kk, :] for part in xT_parts],
                                          start=(kk == 0), stop=(kk == KD - 1))
                    mm.then_inc(done, 1)

            def product(t):
                i, c = t.slot % 2, t.slot % CH
                pe.wait_ge(q.g_lo, t.count)
                for j in range(SUB):
                    if c == 0 and t.after(CH):
                        pe.wait_ge(q.added, group(t) * SUB - (SUB - 1 - j))
                    three_passes(pe, y_ps[:, j, 0:D], [part[:, i, j * P:(j + 1) * P] for part in gated_parts],
                                 [part[:, c, :] for part in w3], start=(c == 0), stop=(c == CH - 1)
                                 ).then_inc(q.y_done, 1)

            pe.wait_ge(q.w_lo, 3)
            pipeline(pe, UNITS, DEPTH, WIDTH, lambda at: run(at, (HIDDEN, hidden), (OUT, product)))

        @block.scalar
        def _(act):
            def split(t):
                g = t.slot // CH
                act.wait_ge(x_loaded, group(t, 1) * 16)
                if t.after(WIDTH):
                    act.wait_ge(q.h2_done, t.before(CH + 1))
                act.activation(xT_parts[0][:, g, :, :], xT[:, :, :], ACT.Copy).then_inc(q.x_hi, 1)

            def silu(t):
                i = t.slot % 2
                act.wait_ge(q.h1_done, t.count)
                if t.after(2):
                    act.wait_ge(q.gated_ready, t.before(2))
                act.activation(act_h[:, i, :], h1_ps[:, i, :], ACT.Silu).then_inc(q.act_ready, 1)

            def gated_hi(t):
                i = t.slot % 2
                act.wait_ge(q.gated_ready, t.count)
                if t.after(2):
                    act.wait_ge(q.y_done, t.before(2) * SUB)
                act.activation(gated_parts[0][:, i, :], gated[:, i, :], ACT.Copy).then_inc(q.g_hi, 1)

            for i in range(3):
                act.wait_ge(weights_loaded[i], 16)
                act.activation((w1, w2, w3)[i][0][:, :, :], raw[i][:, :, :], ACT.Copy).then_inc(q.w_hi, 1)
            pipeline(act, UNITS, DEPTH, WIDTH,
                     lambda at: run(at, (SPLIT, at_chunk(split, 0)), (HIDDEN, silu), (HIDDEN, gated_hi)))

        @block.vector
        def _(dve):
            def split(t):
                g = t.slot // CH
                dve.wait_ge(q.x_hi, group(t, 1))
                dve.tensor_tensor(xT_parts[1][:, g, :, :], xT[:, :, :],
                                  xT_parts[0][:, g, :, :].bitcast(F32), ALU.subtract).then_inc(q.x_lo, 1)

            def gate(t):
                i = t.slot % 2
                dve.wait_ge(q.h2_done, t.count)
                dve.wait_ge(q.act_ready, t.count)
                if t.after(2):
                    dve.wait_ge(q.g_lo, t.before(2))
                dve.tensor_tensor(gated[:, i, :], h2_ps[:, i, :], act_h[:, i, :],
                                  ALU.mult).then_inc(q.gated_ready, 1)

            def gated_lo(t):
                i = t.slot % 2
                dve.wait_ge(q.g_hi, t.count)
                dve.tensor_tensor(gated_parts[1][:, i, :], gated[:, i, :], gated_parts[0][:, i, :].bitcast(F32),
                                  ALU.subtract).then_inc(q.g_lo, 1)

            def add(t):
                dve.wait_ge(x1_loaded, group(t, 1) * 16)
                if t.after(2 * CH - 1):
                    dve.wait_ge(stored, group(t) * 16)
                for j in range(SUB):
                    dve.wait_ge(q.y_done, t.before(1) * SUB + (j + 1))
                    dve.scalar_tensor_tensor(out=x1s[:, j, :], in0=y_ps[:, j, 0:D], scalar=k.tanh_g[:, 1:2],
                                             in1=x1[:, j, :], op0=ALU.mult, op1=ALU.add).then_inc(q.added, 1)

            plan.make(dve)
            for i in range(3):
                dve.wait_ge(q.w_hi, i + 1)
                w = (w1, w2, w3)[i]
                dve.tensor_tensor(w[1][:, :, :], raw[i][:, :, :], w[0][:, :, :].bitcast(F32),
                                  ALU.subtract).then_inc(q.w_lo, 1)
            pipeline(dve, UNITS, DEPTH, WIDTH,
                     lambda at: run(at, (SPLIT, at_chunk(split, 0)), (HIDDEN, gate),
                                    (OUT, at_chunk(add, CH - 1)), (HIDDEN, gated_lo)))


def expert_tiles(nc, a, k):
    with Scope(nc, "expert") as s:
        w1_lo, w2_lo = (s.sb(f"{n}_lo", [P, E, KD * H0], F32R) for n in ("w1", "w2"))
        w3 = s.sb("w3", [P, E * (H0 // P) * D])
        experts_loaded = s.sem("experts_loaded")

        def start_loading(pool):
            for e in range(E):
                for to, of, chunks in ((w1_lo[:, e, :].bitcast(F32), a["L0_ffn_ew1"], KD),
                                       (w2_lo[:, e, :].bitcast(F32), a["L0_ffn_ew2"], KD),
                                       (w3[:, e * (H0 // P * D):(e + 1) * (H0 // P * D)], a["L0_ffn_ew3"],
                                        H0 // P)):
                    pool.dma_start(to.rearrange("p (c n) -> p c n", c=chunks),
                                   of[e].rearrange("(c p) n -> p c n", p=P)).then_inc(experts_loaded, 16)

        shared_expert(nc, a, k, start_loading)

        w1_hi, w2_hi = (s.sb(f"{n}_hi", [P, E, KD * H0], F32R) for n in ("w1", "w2"))
        w1, w2 = (w1_hi, w1_lo), (w2_hi, w2_lo)
        ids = s.sb("ids", [P, 4], I32)
        x = s.sb("x", [P, 4, D])
        xT = [s.sb(f"xT{i}", [P, 2, D], F32R) for i in range(2)]
        act_h = s.sb("act_h", [P, 2, H0])
        gated = s.sb("gated", [P, 2, H0])
        gatedT = s.sb("gatedT", [P, 2, H0])
        y = s.sb("y", [P, 4, D])
        x_ps = s.ps("x_ps", [P, BANK])
        h1_ps = s.ps("h1_ps", [P, 2, BANK])
        h2_ps = s.ps("h2_ps", [P, 2, BANK])
        g_ps = s.ps("g_ps", [P, BANK])
        y_ps = s.ps("y_ps", [P, 2, BANK])
        ids_loaded = [s.sem(f"ids_loaded{i}") for i in range(4)]
        x_gathered = [s.sem(f"x_gathered{i}") for i in range(4)]
        y_stored = [s.sem(f"y_stored{i}") for i in range(4)]
        q = Named()
        (q.w_hi, q.w_lo, q.x_hi, q.x_lo) = s.sems("w_hi w_lo x_hi x_lo")
        (q.turned, q.h1_done, q.h2_done, q.act_ready, q.gated_ready) = s.sems(
            "turned h1_done h2_done act_ready gated_ready")
        (q.g_turned, q.g_copied, q.y_done, q.y_ready) = s.sems(
            "g_turned g_copied y_done y_ready")
        HIDDEN, OUT = 7, 9
        DEPTH = 11
        block = s.block()

        def plan_at(eng, which, t, top):
            return eng.value_load(k.plan[0:1, which, bass.ds(t.index + PAD, 1)], min_val=0, max_val=top)

        @block.sync
        def _(sp):
            def load_ids(t):
                row = plan_at(sp, 0, t, ROWS - P)
                if t.after(4):
                    wait_apart(sp, k, (x_gathered[t.slot], t.round * 16))
                sp.dma_start(ids[:, t.slot:t.slot + 1], k.table[bass.ds(row, P), :]
                             ).then_inc(ids_loaded[t.slot], 16)

            def store(t):
                sp.wait_ge(q.y_ready, t.count)
                sp.dma_start(k.y[bass.ds(t.index * P, P), :], y[:, t.slot, :]).then_inc(y_stored[t.slot], 16)

            pipeline(sp, TILES, DEPTH, 4, lambda at: run(at, (11, store), (3, load_ids)))
            for i in range(4):
                sp.wait_ge(y_stored[i], 16 * (TILES // 4))

        @block.gpsimd
        def _(pool):
            def gather(t):
                i = t.slot
                waits = [(ids_loaded[i], t.round * 16 + 16)]
                if t.after(4):
                    waits.append((q.turned, t.before(4)))
                wait_apart(pool, k, *waits)
                pool.indirect_dma_start(
                    out=x[:, i, :], out_offset=None, in_=k.xn[:, :],
                    in_offset=bass.IndirectOffsetOnAxis(ap=ids[:, i:i + 1], axis=0)
                    ).then_inc(x_gathered[i], 16)

            pipeline(pool, TILES, DEPTH, 4, lambda at: run(at, (7, gather)))

        @block.tensor
        def _(pe):
            pe.wait_ge(q.w_lo, 2 * E)

            def turn_x(t):
                pe.wait_ge(x_gathered[t.slot], t.round * 16 + 16)
                if t.after(1):
                    pe.wait_ge(q.x_lo, t.before(1))
                for c in range(KD):
                    mm = pe.transpose(x_ps[:, c * P:(c + 1) * P], x[:, t.slot, c * P:(c + 1) * P],
                                      k.ident[:, :])
                mm.then_inc(q.turned, 1)

            def hidden(t):
                i = t.slot % 2
                pe.wait_ge(q.x_lo, t.count)
                expert = experts[(t.slot + HIDDEN) % 4 + BEHIND]
                for w, out, done, free in ((w1, h1_ps, q.h1_done, q.act_ready),
                                           (w2, h2_ps, q.h2_done, q.gated_ready)):
                    if t.after(2):
                        pe.wait_ge(free, t.before(2))
                    for c in range(KD):
                        mm = three_passes(pe, out[:, i, :], [part[:, i, c * P:(c + 1) * P] for part in xT],
                                          [part.rearrange("p e n -> p (e n)")
                                           [:, bass.ds(expert * (KD * H0) + c * H0, H0)] for part in w],
                                          start=(c == 0), stop=(c == KD - 1))
                    mm.then_inc(done, 1)

            def turn_gated(t):
                i = t.slot % 2
                pe.wait_ge(q.gated_ready, t.count)
                if t.after(1):
                    pe.wait_ge(q.g_copied, t.before(1))
                for c in range(H0 // P):
                    mm = pe.transpose(g_ps[:, c * P:(c + 1) * P], gated[:, i, c * P:(c + 1) * P],
                                      k.ident[:, :])
                mm.then_inc(q.g_turned, 1)

            def out(t):
                i = t.slot % 2
                expert = experts[(t.slot + OUT) % 4]
                pe.wait_ge(q.g_copied, t.count)
                if t.after(2):
                    pe.wait_ge(q.y_ready, t.before(2))
                for c in range(H0 // P):
                    mm = pe.matmul(y_ps[:, i, 0:D], gatedT[:, i, c * P:(c + 1) * P],
                                   w3[:, bass.ds(expert * (H0 // P * D) + c * D, D)],
                                   start=(c == 0), stop=(c == H0 // P - 1))
                mm.then_inc(q.y_done, 1)

            BEHIND = OUT - HIDDEN
            experts = []

            def body(at):
                for lag in (HIDDEN, OUT):
                    t = at(lag)
                    if t and (not experts or (t.slot + lag) % 4 == 0):
                        first = (t.round + (t.slot + lag) // 4) * 4 + (PAD - OUT)
                        _, experts[:] = nc.values_load_multi_w_load_instructions(
                            k.plan[0:1, 1, bass.ds(first, 4 + BEHIND)], engines=[mybir.EngineType.PE],
                            min_val=0, max_val=E - 1)
                    if t:
                        break
                run(at, (6, turn_x), (7, hidden), (8, turn_gated), (9, out))

            pipeline(pe, TILES, DEPTH, 4, body)

        @block.scalar
        def _(act):
            def x_hi(t):
                act.wait_ge(q.turned, t.count)
                if t.after(2):
                    act.wait_ge(q.h2_done, t.before(2))
                act.activation(xT[0][:, t.slot % 2, :], x_ps[:, 0:D], ACT.Copy).then_inc(q.x_hi, 1)

            def silu(t):
                i = t.slot % 2
                act.wait_ge(q.h1_done, t.count)
                if t.after(2):
                    act.wait_ge(q.gated_ready, t.before(2))
                act.activation(act_h[:, i, :], h1_ps[:, i, :], ACT.Silu).then_inc(q.act_ready, 1)

            def copy_gated(t):
                i = t.slot % 2
                act.wait_ge(q.g_turned, t.count)
                if t.after(2):
                    act.wait_ge(q.y_done, t.before(2))
                act.activation(gatedT[:, i, :], g_ps[:, :], ACT.Copy).then_inc(q.g_copied, 1)

            act.wait_ge(experts_loaded, 16 * 3 * E)
            for e in range(E):
                for hi, lo in (w1, w2):
                    act.activation(hi[:, e, :], lo[:, e, :].bitcast(F32), ACT.Copy).then_inc(q.w_hi, 1)
            pipeline(act, TILES, DEPTH, 4,
                     lambda at: run(at, (6, x_hi), (7, silu), (8, copy_gated)))

        @block.vector
        def _(dve):
            def gate(t):
                i = t.slot % 2
                dve.wait_ge(q.h2_done, t.count)
                dve.wait_ge(q.act_ready, t.count)
                if t.after(2):
                    dve.wait_ge(q.g_turned, t.before(2))
                dve.tensor_tensor(gated[:, i, :], h2_ps[:, i, :], act_h[:, i, :],
                                  ALU.mult).then_inc(q.gated_ready, 1)

            def copy_y(t):
                dve.wait_ge(q.y_done, t.count)
                if t.after(4):
                    dve.wait_ge(y_stored[t.slot], t.round * 16)
                dve.tensor_copy(y[:, t.slot, :], y_ps[:, t.slot % 2, 0:D]).then_inc(q.y_ready, 1)

            def x_lo(t):
                dve.wait_ge(q.x_hi, t.count)
                dve.tensor_tensor(xT[1][:, t.slot % 2, :], x_ps[:, 0:D], xT[0][:, t.slot % 2, :].bitcast(F32),
                                  ALU.subtract).then_inc(q.x_lo, 1)

            for e in range(E):
                for i, (hi, lo) in enumerate((w1, w2)):
                    dve.wait_ge(q.w_hi, 2 * e + i + 1)
                    dve.tensor_tensor(lo[:, e, :], lo[:, e, :].bitcast(F32), hi[:, e, :].bitcast(F32),
                                      ALU.subtract).then_inc(q.w_lo, 1)
            pipeline(dve, TILES, DEPTH, 4, lambda at: run(at, (11, copy_y), (8, gate), (6, x_lo)))


def prepare_causal(nc, a, k, w):
    with Scope(nc, "prep3") as s:
        q_w = s.sb("q_w", [P, KD, D])
        k_w = s.sb("k_w", [P, KD, D])
        gate_raw = s.sb("gate_raw", [P, KD, D])
        ctxT = s.sb("ctxT", [P, KD, B * EVEN])
        qk_ps = s.ps("qk_ps", [P, KD, D])
        loaded = s.sem("loaded")
        padded = s.sem("padded")
        product_done = s.sem("product_done")
        hi_ready = s.sem("hi_ready")
        qk_hi_ready = s.sem("qk_hi_ready")
        prepared = s.sem("prepared")
        loads = [
            (q_w[:, :, :], a["L1_xattn_q_w"].rearrange("(k p) n -> p k n", p=P)),
            (k_w[:, :, :], a["L1_xattn_k_w"].rearrange("(k p) n -> p k n", p=P)),
            (gate_raw[:, :, :], a["L1_xattn_gate_w"].rearrange("(k p) n -> p k n", p=P)),
            *((ctxT[:, kk, :].rearrange("p (b n) -> p b n", n=EVEN)[:, :, 0:KEYS],
               a["ctxT"][kk * P:(kk + 1) * P, :, :]) for kk in range(KD)),
            (w.ctx[:, :].rearrange("n (b d) -> n b d", d=D), a["ctx"].rearrange("b n d -> n b d")),
            (w.norm_w[:, :], a["L1_xattn_norm_w"].partition_broadcast(P)),
            (w.gate_b[:, :], a["L1_xattn_gate_b"].partition_broadcast(P)),
            (w.above[:, :], a["c_above"]),
            (w.gate8[:, :, :], a["L1_ffn_gate_W"].rearrange("(k p) n -> p k n", p=P)),
            (w.route_scale[:, :], a["L1_ffn_route_scale"].partition_broadcast(P)),
        ]
        block = s.block()

        @block.sync
        def _(sp):
            for to, of in loads:
                sp.dma_start(to, of).then_inc(loaded, 16)

        @block.gpsimd
        def _(pool):
            pool.memset(ctxT[:, :, :].rearrange("p k (b n) -> p k b n", n=EVEN)[:, :, :, KEYS:EVEN], 0.0
                        ).then_inc(padded, 1)
            pool.memset(w.neg_scale[:, :], -D ** -0.5).then_inc(prepared, 1)

        @block.tensor
        def _(pe):
            pe.wait_ge(loaded, 16 * len(loads))
            for c in range(KD):
                for kk in range(KD):
                    mm = pe.matmul(qk_ps[:, c, :], q_w[:, kk, c * P:(c + 1) * P], k_w[:, kk, :],
                                   start=(kk == 0 and c == 0), stop=(kk == KD - 1), skip_group_check=True)
            mm.then_inc(product_done, 1)

        @block.scalar
        def _(act):
            act.wait_ge(loaded, 16 * len(loads))
            act.activation(w.gate[0][:, :, :], gate_raw[:, :, :], ACT.Copy).then_inc(hi_ready, 1)
            act.wait_ge(padded, 1)
            act.activation(w.ctxT[0][:, :, :], ctxT[:, :, :], ACT.Copy).then_inc(hi_ready, 1)
            act.wait_ge(product_done, 1)
            act.activation(w.qk[0][:, :, :], qk_ps[:, :, :], ACT.Copy).then_inc(qk_hi_ready, 1)

        @block.vector
        def _(dve):
            dve.wait_ge(hi_ready, 2)
            dve.tensor_tensor(w.gate[1][:, :, :], gate_raw[:, :, :], w.gate[0][:, :, :].bitcast(F32),
                              ALU.subtract).then_inc(prepared, 1)
            dve.tensor_tensor(w.ctxT[1][:, :, :], ctxT[:, :, :], w.ctxT[0][:, :, :].bitcast(F32),
                              ALU.subtract).then_inc(prepared, 1)
            dve.wait_ge(qk_hi_ready, 1)
            dve.tensor_tensor(w.qk[1][:, :, :], qk_ps[:, :, :], w.qk[0][:, :, :].bitcast(F32),
                              ALU.subtract).then_inc(prepared, 1)
            dve.tensor_scalar(w.half_g[:, :], k.tanh_g[:, 2:3], 0.5, None, ALU.mult).then_inc(prepared, 1)


def causal_attention(nc, a, k):
    with Scope(nc, "causal") as s:
        w = Named()
        w.qk = [s.sb(f"qk{i}", [P, KD, D], F32R) for i in range(2)]
        w.gate = [s.sb(f"gate{i}", [P, KD, D], F32R) for i in range(2)]
        w.ctxT = [s.sb(f"ctxT{i}", [P, KD, B * EVEN], F32R) for i in range(2)]
        w.ctx = s.sb("ctx", [KEYS, B * D])
        w.norm_w = s.sb("norm_w", [P, D])
        w.gate_b = s.sb("gate_b", [P, D])
        w.above = s.sb("above", [P, P])
        w.gate8 = s.sb("gate8", [P, KD, E])
        w.route_scale = s.sb("route_scale", [P, 1])
        w.half_g = s.sb("half_g", [P, 1])
        w.neg_scale = s.sb("neg_scale", [P, 1])
        prepare_causal(nc, a, k, w)

        keysT = [s.sb(f"keysT{i}", [P, 2 * KD * S], F32R) for i in range(2)]
        pool_v = s.sb("pool_v", [P, 2 * POS * D])
        rows_at = s.sb("rows_at", [P, 2 * 4], I32)
        x1 = s.sb("x1", [P, 4, D])
        y0 = s.sb("y0", [P, 4, D])
        y1 = s.sb("y1", [P, 4, D])
        part1 = s.sb("part1", [P, 2, D])
        x2 = s.sb("x2", [P, 4, D])
        stats = s.sb("stats", [P, 8, 6])
        moments = s.sb("moments", [P, 8, 2])
        var_eps = s.sb("var_eps", [P, 8])
        shift = s.sb("shift", [P, 8])
        shift3 = s.sb("shift3", [P, 8])
        rstd = s.sb("rstd", [P, 8])
        h = s.sb("h", [P, 8, D])
        square = s.sb("square", [P, D])
        sum_sq = s.sb("sum_sq", [P, 8])
        mean_sq = s.sb("mean_sq", [P, 8])
        rrms = s.sb("rrms", [P, 8])
        normed = s.sb("normed", [P, 2, D])
        hT = [s.sb(f"hT{i}", [P, 2, D], F32R) for i in range(2)]
        gated_h = s.sb("gated_h", [P, 2, D])
        base = s.sb("base", [P, 8, D])
        z = s.sb("z", [P, 2, D])
        tanh_z = s.sb("tanh_z", [P, 4, D])
        qT = [s.sb(f"qT{i}", [P, 2, D], F32R) for i in range(2)]
        rowmax = s.sb("rowmax", [P, 8])
        neg_max = s.sb("neg_max", [P, 8])
        probs = s.sb("probs", [P, 2, S + P])
        den = s.sb("den", [P, 8])
        rden = s.sb("rden", [P, 8])
        probsT = s.sb("probsT", [P, 2, (POS + 1) * P])
        diff = s.sb("diff", [P, 2, D])
        mixed = s.sb("mixed", [P, 2, D])
        x3 = s.sb("x3", [P, 4, D])
        stats3 = s.sb("stats3", [P, 8, 6])
        moments3 = s.sb("moments3", [P, 8, 2])
        var_eps3 = s.sb("var_eps3", [P, 8])
        rstd3 = s.sb("rstd3", [P, 8])
        xn3 = s.sb("xn3", [P, 2, D])
        xn3T = s.sb("xn3T", [P, 4, D])
        logits = s.sb("logits", [P, 4, E])
        exp_l = s.sb("exp_l", [P, 4, E])
        one_plus = s.sb("one_plus", [P, 4, E])
        sigmoid = s.sb("sigmoid", [P, 4, E])
        gate_s = s.sb("gate_s", [P, 4, E])
        top = s.sb("top", [P, 4, 8])
        top_at = s.sb("top_at", [P, 4, 8], U32)
        total = s.sb("total", [P, 4])
        rtotal = s.sb("rtotal", [P, 4])
        chosen_at = s.sb("chosen_at", [P, 4, 2])
        chosen_w = s.sb("chosen_w", [P, 4, 2])
        chosen = s.sb("chosen", [P, 4, 2, E])
        weighed = s.sb("weighed", [P, 4, 2, E])

        logits_ps = s.ps("logits_ps", [P, 3 * BANK])
        pT_ps = s.ps("pT_ps", [P, 2, BANK])
        turn_ps = s.ps("turn_ps", [P, BANK])
        mm_ps = s.ps("mm_ps", [P, BANK])
        out_ps = s.ps("out_ps", [P, BANK])

        q = Named()
        (q.shift_ready, q.shift3_ready) = s.sems("shift_ready shift3_ready")
        (q.rows_ready, q.part1_ready, q.x2_ready, q.stats_ready) = s.sems(
            "rows_ready part1_ready x2_ready stats_ready")
        (q.moments_ready, q.var_ready, q.rstd_ready, q.h_ready, q.square_ready) = s.sems(
            "moments_ready var_ready rstd_ready h_ready square_ready")
        (q.mean_ready, q.rrms_ready, q.normed_ready, q.hT_done, q.hT_hi, q.hT_lo) = s.sems(
            "mean_ready rrms_ready normed_ready hT_done hT_hi hT_lo")
        (q.nT_done, q.nT_hi, q.nT_lo, q.gate_done, q.z_ready, q.tanh_ready, q.q_done) = s.sems(
            "nT_done nT_hi nT_lo gate_done z_ready tanh_ready q_done")
        (q.q_hi, q.q_lo, q.logits_done, q.rowmax_ready, q.neg_max_ready) = s.sems(
            "q_hi q_lo logits_done rowmax_ready neg_max_ready")
        (q.probs_ready, q.pT_done, q.pT_ready, q.pv_done, q.rden_ready, q.diff_ready) = s.sems(
            "probs_ready pT_done pT_ready pv_done rden_ready diff_ready")
        (q.mixed_ready, q.gated_h_ready, q.base_ready, q.x3_ready, q.stats3_ready) = s.sems(
            "mixed_ready gated_h_ready base_ready x3_ready stats3_ready")
        (q.moments3_ready, q.var3_ready, q.rstd3_ready, q.xn3_ready, q.xn3T_done) = s.sems(
            "moments3_ready var3_ready rstd3_ready xn3_ready xn3T_done")
        (q.xn3T_ready, q.glogits_done, q.glogits_ready, q.exp_ready) = s.sems(
            "xn3T_ready glogits_done glogits_ready exp_ready")
        (q.one_plus_ready, q.probs_cleared, q.sigmoid_ready, q.gate_s_ready) = s.sems(
            "one_plus_ready probs_cleared sigmoid_ready gate_s_ready")
        (q.top_ready, q.top_at_ready, q.total_ready, q.rtotal_ready) = s.sems(
            "top_ready top_at_ready total_ready rtotal_ready")
        (q.chosen_at_ready, q.weight_ready, q.chosen_w_ready, q.chosen_ready) = s.sems(
            "chosen_at_ready weight_ready chosen_w_ready chosen_ready")
        (q.weighed_ready, q.gates_ready, q.pooled) = s.sems(
            "weighed_ready gates_ready pooled")
        x1_loaded = [s.sem(f"x1_loaded{i}") for i in range(4)]
        y0_gathered = [s.sem(f"y0_gathered{i}") for i in range(4)]
        y1_gathered = [s.sem(f"y1_gathered{i}") for i in range(4)]
        x3_stored = [s.sem(f"x3_stored{i}") for i in range(4)]
        xn3T_stored = [s.sem(f"xn3T_stored{i}") for i in range(4)]

        DEPTH = 14
        turn_bank = Bank(NT, [("n", 5, q.nT_lo), ("h", 5, q.hT_lo), ("x3", 13, q.xn3T_ready)])
        mm_bank = Bank(NT, [("gate", 6, q.z_ready), ("queries", 6, q.q_lo)])
        out_bank = Bank(NT, [("glogits", 14, q.glogits_ready), ("attend", 10, q.diff_ready)])

        def rows(t):
            return bass.ds(t.index * P, P)

        def fours(t):
            return t.round * 2 + t.slot // 4

        def groups(pos):
            return -(-(pos + 2) // 4)

        GROUPS = sum(groups(p) for p in range(POS))

        def groups_before(t):
            return t.round * GROUPS + sum(groups(p) for p in range(t.slot))

        def half(t):
            return t.round % 2

        def keys_at(t, kk, start, n):
            return bass.ds(half(t) * (KD * S) + (kk * S + start), n)

        block = s.block()

        @block.sync
        def _(sp):
            def load(t):
                i = t.slot % 4
                if t.after(4):
                    sp.wait_ge(q.part1_ready, t.before(4))
                sp.dma_start(x1[:, i, :], k.x1s[rows(t), :]).then_inc(x1_loaded[i], 16)

            def store_x3(t):
                i = t.slot % 4
                wait_apart(sp, k, (q.x3_ready, t.count))
                sp.dma_start(k.x3[rows(t), :], x3[:, i, :]).then_inc(x3_stored[i], 16)

            def store_xn3T(t):
                i = t.slot % 4
                wait_apart(sp, k, (q.xn3T_ready, t.count))
                sp.dma_start(k.xn4T.rearrange("(k p) t -> p k t", p=P)[:, :, bass.ds(t.index * P, P)],
                             xn3T[:, i, :].rearrange("p (k t) -> p k t", k=KD)).then_inc(xn3T_stored[i], 16)

            pipeline(sp, NT, DEPTH, POS,
                     lambda at: run(at, (1, load), (11, store_x3), (12, store_xn3T)))
            for i in range(4):
                sp.wait_ge(x3_stored[i], 16 * (NT // 4))
                sp.wait_ge(xn3T_stored[i], 16 * (NT // 4))

        @block.gpsimd
        def _(pool):
            def gather(t):
                i = t.slot % 4
                if t.after(4):
                    pool.wait_ge(y0_gathered[i], fours(t) * 16)
                    pool.wait_ge(y1_gathered[i], fours(t) * 16)
                    pool.wait_ge(q.x2_ready, t.before(4))
                pool.tensor_copy(rows_at[:, 2 * i:2 * i + 2],
                                 k.slots[:, bass.ds(t.round * 2 + t.slot * (2 * B), 2)]
                                 ).then_inc(q.rows_ready, 1)
                wait_apart(pool, k, (q.rows_ready, t.count))
                for c, to, sem in ((0, y0, y0_gathered[i]), (1, y1, y1_gathered[i])):
                    pool.indirect_dma_start(
                        out=to[:, i, :], out_offset=None, in_=k.y[:, :],
                        in_offset=bass.IndirectOffsetOnAxis(ap=rows_at[:, 2 * i + c:2 * i + c + 1], axis=0)
                        ).then_inc(sem, 16)

            def power(t, to, of, moved, eps, ready, moved_ready, done):
                i = t.slot
                pool.wait_ge(ready, t.count)
                pool.tensor_tensor(moved[:, i:i + 1], of, k.eps[:, eps:eps + 1], ALU.add
                                   ).then_inc(moved_ready, 1)
                pool.wait_ge(moved_ready, t.count)
                pool.tensor_tensor(to[:, i:i + 1], moved[:, i:i + 1], k.neghalf[:, :],
                                   ALU.pow).then_inc(done, 1)

            def negate_shift(t, to, mean, std, ready, done):
                i = t.slot
                wait_apart(pool, k, (ready, t.count))
                pool.tensor_scalar(to[:, i:i + 1], mean, std[:, i:i + 1], -1.0, ALU.mult, ALU.mult
                                   ).then_inc(done, 1)

            def rstd_x2(t):
                power(t, rstd, moments[:, t.slot, 1:2], var_eps, 0, q.moments_ready, q.var_ready,
                      q.rstd_ready)
                negate_shift(t, shift, moments[:, t.slot, 0:1], rstd, q.rstd_ready, q.shift_ready)

            def rrms_h(t):
                power(t, rrms, sum_sq[:, t.slot:t.slot + 1], mean_sq, 1, q.square_ready,
                      q.mean_ready, q.rrms_ready)

            def rstd_x3(t):
                power(t, rstd3, moments3[:, t.slot, 1:2], var_eps3, 0, q.moments3_ready,
                      q.var3_ready, q.rstd3_ready)
                negate_shift(t, shift3, moments3[:, t.slot, 0:1], rstd3, q.rstd3_ready, q.shift3_ready)

            def ungated(t):
                i = t.slot
                pool.wait_ge(q.h_ready, t.count)
                pool.tensor_tensor(gated_h[:, i % 2, :], h[:, i, :],
                                   k.tanh_g[:, 2:3].to_broadcast([P, D]), ALU.mult).then_inc(q.gated_h_ready, 1)
                pool.wait_ge(q.gated_h_ready, t.count)
                pool.tensor_tensor(base[:, i, :], gated_h[:, i % 2, :], x2[:, i % 4, :],
                                   ALU.add).then_inc(q.base_ready, 1)

            def negate_max(t):
                i = t.slot
                pool.wait_ge(q.rowmax_ready, t.count)
                pool.tensor_tensor(neg_max[:, i:i + 1], rowmax[:, i:i + 1], w.neg_scale[:, :],
                                   ALU.mult).then_inc(q.neg_max_ready, 1)

            pool.memset(probs[:, :, :], 0.0).then_inc(q.probs_cleared, 1)
            pipeline(pool, NT, DEPTH, POS,
                     lambda at: run(at, (11, rstd_x3), (8, negate_max), (3, rstd_x2), (4, rrms_h),
                                    (0, gather), (5, ungated)))

        @block.tensor
        def _(pe):
            def turn(of, done):
                for c in range(KD):
                    mm = pe.transpose(turn_ps[:, c * P:(c + 1) * P], of[:, c * P:(c + 1) * P], k.ident[:, :])
                mm.then_inc(done, 1)

            def turn_h(t):
                pe.wait_ge(q.h_ready, t.count)
                if turn_bank.used("h", t):
                    pe.wait_ge(*turn_bank.freed("h", t))
                turn(h[:, t.slot, :], q.hT_done)

            def turn_n(t):
                pe.wait_ge(q.normed_ready, t.count)
                if turn_bank.used("n", t):
                    pe.wait_ge(*turn_bank.freed("n", t))
                turn(normed[:, t.slot % 2, :], q.nT_done)

            def turn_x3(t):
                pe.wait_ge(q.xn3_ready, t.count)
                if turn_bank.used("x3", t):
                    pe.wait_ge(*turn_bank.freed("x3", t))
                turn(xn3[:, t.slot % 2, :], q.xn3T_done)

            def gate_logits(t):
                pe.wait_ge(q.xn3T_ready, t.count)
                if out_bank.used("glogits", t):
                    pe.wait_ge(*out_bank.freed("glogits", t))
                for kk in range(KD):
                    mm = pe.matmul(out_ps[:, 0:E], xn3T[:, t.slot % 4, kk * P:(kk + 1) * P],
                                   w.gate8[:, kk, :], start=(kk == 0), stop=(kk == KD - 1))
                mm.then_inc(q.glogits_done, 1)

            def turn_probs(t):
                i = t.slot % 2
                pe.wait_ge(q.probs_ready, t.count)
                for group in range(groups(t.slot)):
                    n = groups_before(t) + group
                    if not isinstance(n, int) or n >= 2:
                        pe.wait_ge(q.pT_ready, n - 1)
                    bank = (sum(groups(p) for p in range(t.slot)) + group) % 2
                    for c in range(4 * group, min(4 * group + 4, t.slot + 2)):
                        mm = pe.transpose(pT_ps[:, bank, (c % 4) * P:(c % 4 + 1) * P],
                                          probs[:, i, c * P:(c + 1) * P], k.ident[:, :])
                    mm.then_inc(q.pT_done, 1)

            def gate(t):
                i = t.slot % 2
                pe.wait_ge(q.hT_lo, t.count)
                if mm_bank.used("gate", t):
                    pe.wait_ge(*mm_bank.freed("gate", t))
                for kk in range(KD):
                    mm = three_passes(pe, mm_ps[:, 0:D], [part[:, i, kk * P:(kk + 1) * P] for part in hT],
                                      [part[:, kk, :] for part in w.gate],
                                      start=(kk == 0), stop=(kk == KD - 1))
                mm.then_inc(q.gate_done, 1)

            def attend(t):
                i = t.slot % 2
                pe.wait_ge(q.pT_ready, groups_before(t) + groups(t.slot))
                pe.wait_ge(q.pooled, t.count)
                if out_bank.used("attend", t):
                    pe.wait_ge(*out_bank.freed("attend", t))
                for c in range(t.slot + 1):
                    pe.matmul(out_ps[:, 0:D], probsT[:, i, c * P:(c + 1) * P],
                              pool_v[:, bass.ds(half(t) * (POS * D) + c * D, D)],
                              start=(c == 0), stop=False)
                mm = pe.matmul(out_ps[:, 0:D], probsT[0:KEYS, i, (t.slot + 1) * P:(t.slot + 2) * P],
                               w.ctx[:, bass.ds(t.round * D, D)], start=False, stop=True)
                mm.then_inc(q.pv_done, 1)

            def queries(t):
                pe.wait_ge(q.nT_lo, t.count)
                if mm_bank.used("queries", t):
                    pe.wait_ge(*mm_bank.freed("queries", t))
                for c in range(KD):
                    for kk in range(KD):
                        mm = three_passes(pe, mm_ps[:, c * P:(c + 1) * P],
                                          [part[:, kk, c * P:(c + 1) * P] for part in w.qk],
                                          [part[:, keys_at(t, kk, t.slot * P, P)] for part in keysT],
                                          start=(kk == 0 and c == 0), stop=(kk == KD - 1))
                mm.then_inc(q.q_done, 1)

            def score(t):
                i = t.slot % 2
                pe.wait_ge(q.q_lo, t.count)
                if t.after(1):
                    pe.wait_ge(q.probs_ready, t.before(1))
                own = t.slot * P
                for at in range(0, own + P, BANK):
                    n = min(own + P - at, BANK)
                    for kk in range(KD):
                        three_passes(pe, logits_ps[:, at:at + n],
                                     [part[:, i, kk * P:(kk + 1) * P] for part in qT],
                                     [part[:, keys_at(t, kk, at, n)] for part in keysT],
                                     start=(kk == 0), stop=False)
                pe.matmul(logits_ps[:, own:own + P], k.ident[:, :], w.above[:, :], start=False, stop=True,
                          skip_group_check=True)
                at = own + P
                for kk in range(KD):
                    mm = three_passes(pe, logits_ps[:, at:at + EVEN],
                                      [part[:, i, kk * P:(kk + 1) * P] for part in qT],
                                      [part[:, kk, bass.ds(t.round * EVEN, EVEN)] for part in w.ctxT],
                                      start=(kk == 0 and at % BANK == 0), stop=(kk == KD - 1))
                mm.then_inc(q.logits_done, 1)

            pipeline(pe, NT, DEPTH, POS,
                     lambda at: run(at, (14, gate_logits), (6, gate), (5, turn_n), (6, queries),
                                    (5, turn_h), (9, turn_probs), (13, turn_x3), (10, attend),
                                    (7, score)))

        @block.scalar
        def _(act):
            def normalise(t):
                i = t.slot
                act.wait_ge(q.shift_ready, t.count)
                if t.after(8):
                    act.wait_ge(q.diff_ready, t.before(8))
                    act.wait_ge(q.base_ready, t.before(8))
                act.activation(h[:, i, :], x2[:, i % 4, :], ACT.Identity, scale=rstd[:, i:i + 1],
                               bias=shift[:, i:i + 1]).then_inc(q.h_ready, 1)

            def normalise_x3(t):
                i = t.slot
                act.wait_ge(q.shift3_ready, t.count)
                if t.after(2):
                    act.wait_ge(q.xn3T_done, t.before(2))
                act.activation(xn3[:, i % 2, :], x3[:, i % 4, :], ACT.Identity, scale=rstd3[:, i:i + 1],
                               bias=shift3[:, i:i + 1]).then_inc(q.xn3_ready, 1)

            def to_pool(t):
                act.wait_ge(q.normed_ready, t.count)
                act.activation(pool_v[:, bass.ds(half(t) * (POS * D) + t.slot * D, D)],
                               normed[:, t.slot % 2, :], ACT.Copy).then_inc(q.pooled, 1)

            def square_h(t):
                act.wait_ge(q.h_ready, t.count)
                if t.after(1):
                    act.wait_ge(q.square_ready, t.before(1))
                act.activation(square[:, :], h[:, t.slot, :], ACT.Square, scale=D ** -0.5,
                               accum_out=sum_sq[:, t.slot:t.slot + 1]).then_inc(q.square_ready, 1)

            def h_hi(t):
                if t.after(2):
                    act.wait_ge(q.gate_done, t.before(2))
                act.wait_ge(q.hT_done, t.count)
                act.activation(hT[0][:, t.slot % 2, :], turn_ps[:, 0:D], ACT.Copy).then_inc(q.hT_hi, 1)

            def n_hi(t):
                act.wait_ge(q.nT_done, t.count)
                for kk in range(KD):
                    ins = act.activation(keysT[0][:, keys_at(t, kk, t.slot * P, P)],
                                         turn_ps[:, kk * P:(kk + 1) * P], ACT.Copy)
                ins.then_inc(q.nT_hi, 1)

            def copy_probsT(t):
                i = t.slot % 2
                if t.after(2):
                    act.wait_ge(q.pv_done, t.before(2))
                for group in range(groups(t.slot)):
                    n = (min(4 * group + 4, t.slot + 2) - 4 * group) * P
                    bank = (sum(groups(p) for p in range(t.slot)) + group) % 2
                    act.wait_ge(q.pT_done, groups_before(t) + (group + 1))
                    act.activation(probsT[:, i, group * BANK:group * BANK + n], pT_ps[:, bank, 0:n],
                                   ACT.Copy).then_inc(q.pT_ready, 1)

            def copy_x3(t):
                i = t.slot % 4
                if t.after(4):
                    act.wait_ge(xn3T_stored[i], fours(t) * 16)
                    act.wait_ge(q.glogits_done, t.before(4))
                act.wait_ge(q.xn3T_done, t.count)
                act.activation(xn3T[:, i, :], turn_ps[:, 0:D], ACT.Copy).then_inc(q.xn3T_ready, 1)

            def tanh(t):
                act.wait_ge(q.z_ready, t.count)
                if t.after(4):
                    act.wait_ge(q.mixed_ready, t.before(4))
                act.activation(tanh_z[:, t.slot % 4, :], z[:, t.slot % 2, :], ACT.Tanh,
                               scale=0.5).then_inc(q.tanh_ready, 1)

            def q_hi(t):
                if t.after(2):
                    act.wait_ge(q.logits_done, t.before(2))
                act.wait_ge(q.q_done, t.count)
                act.activation(qT[0][:, t.slot % 2, :], mm_ps[:, 0:D], ACT.Copy).then_inc(q.q_hi, 1)

            def exponent(t):
                i = t.slot
                n = KEYS + (i + 1) * P
                act.wait_ge(q.neg_max_ready, t.count)
                if t.after(2):
                    act.wait_ge(q.pT_done, groups_before(t) - groups((i - 1) % POS))
                act.activation(probs[:, i % 2, 0:n], logits_ps[:, 0:n], ACT.Exp, bias=neg_max[:, i:i + 1],
                               scale=D ** -0.5, accum_out=den[:, i:i + 1]).then_inc(q.probs_ready, 1)

            def exp_logits(t):
                if t.slot % 4 == 3:
                    act.wait_ge(q.glogits_ready, t.count)
                    act.activation(exp_l[:, :, :], logits[:, :, :], ACT.Exp, scale=-1.0
                                   ).then_inc(q.exp_ready, 1)

            act.wait_ge(q.probs_cleared, 1)
            pipeline(act, NT, DEPTH, POS,
                     lambda at: run(at, (4, normalise), (4, square_h), (5, n_hi), (13, normalise_x3),
                                    (14, exp_logits), (5, h_hi), (8, exponent), (9, copy_probsT),
                                    (5, to_pool), (13, copy_x3), (7, tanh), (6, q_hi)))

        @block.vector
        def _(dve):
            def combine(t):
                i, j = t.slot % 4, t.slot % 2
                at = t.slot * (2 * B) + t.round * 2
                dve.wait_ge(x1_loaded[i], fours(t) * 16 + 16)
                dve.wait_ge(y0_gathered[i], fours(t) * 16 + 16)
                dve.scalar_tensor_tensor(out=part1[:, j, :], in0=y0[:, i, :], scalar=k.weights[:, bass.ds(at, 1)],
                                         in1=x1[:, i, :], op0=ALU.mult, op1=ALU.add
                                         ).then_inc(q.part1_ready, 1)
                dve.wait_ge(q.part1_ready, t.count)
                dve.wait_ge(y1_gathered[i], fours(t) * 16 + 16)
                if t.after(4):
                    dve.wait_ge(q.base_ready, t.before(4))
                dve.scalar_tensor_tensor(out=x2[:, i, :], in0=y1[:, i, :],
                                         scalar=k.weights[:, bass.ds(at + 1, 1)], in1=part1[:, j, :],
                                         op0=ALU.mult, op1=ALU.add).then_inc(q.x2_ready, 1)
                dve.wait_ge(q.x2_ready, t.count)
                dve.bn_stats(stats[:, t.slot, :], x2[:, i, :]).then_inc(q.stats_ready, 1)
                wait_apart(dve, k, (q.stats_ready, t.count))
                dve.bn_aggr(moments[:, t.slot, :], stats[:, t.slot, :]).then_inc(q.moments_ready, 1)

            def rms_norm(t):
                i = t.slot
                dve.wait_ge(q.rrms_ready, t.count)
                if t.after(2):
                    dve.wait_ge(q.nT_done, t.before(2))
                    dve.wait_ge(q.pooled, t.before(2))
                dve.scalar_tensor_tensor(out=normed[:, i % 2, :], in0=h[:, i, :],
                                         scalar=rrms[:, i:i + 1], in1=w.norm_w[:, :],
                                         op0=ALU.mult, op1=ALU.mult).then_inc(q.normed_ready, 1)

            def difference(t):
                i, j = t.slot, t.slot % 2
                dve.wait_ge(q.probs_ready, t.count)
                dve.reciprocal(rden[:, i:i + 1], den[:, i:i + 1]).then_inc(q.rden_ready, 1)
                dve.wait_ge(q.rden_ready, t.count)
                dve.wait_ge(q.pv_done, t.count)
                dve.scalar_tensor_tensor(out=diff[:, j, :], in0=out_ps[:, 0:D], scalar=rden[:, i:i + 1],
                                         in1=h[:, i, :], op0=ALU.mult, op1=ALU.subtract
                                         ).then_inc(q.diff_ready, 1)
                dve.wait_ge(q.diff_ready, t.count)
                dve.wait_ge(q.tanh_ready, t.count)
                dve.scalar_tensor_tensor(out=mixed[:, j, :], in0=tanh_z[:, i % 4, :], scalar=1.0,
                                         in1=diff[:, j, :], op0=ALU.add, op1=ALU.mult
                                         ).then_inc(q.mixed_ready, 1)
                dve.wait_ge(q.mixed_ready, t.count)
                dve.wait_ge(q.base_ready, t.count)
                if t.after(4):
                    dve.wait_ge(x3_stored[i % 4], fours(t) * 16)
                    dve.wait_ge(q.xn3_ready, t.before(4))
                dve.scalar_tensor_tensor(out=x3[:, i % 4, :], in0=mixed[:, j, :], scalar=w.half_g[:, :],
                                         in1=base[:, i, :], op0=ALU.mult, op1=ALU.add
                                         ).then_inc(q.x3_ready, 1)
                dve.wait_ge(q.x3_ready, t.count)
                dve.bn_stats(stats3[:, i, :], x3[:, i % 4, :]).then_inc(q.stats3_ready, 1)
                wait_apart(dve, k, (q.stats3_ready, t.count))
                dve.bn_aggr(moments3[:, i, :], stats3[:, i, :]).then_inc(q.moments3_ready, 1)

            def h_lo(t):
                j = t.slot % 2
                dve.wait_ge(q.hT_hi, t.count)
                dve.tensor_tensor(hT[1][:, j, :], turn_ps[:, 0:D], hT[0][:, j, :].bitcast(F32),
                                  ALU.subtract).then_inc(q.hT_lo, 1)

            def n_lo(t):
                dve.wait_ge(q.nT_hi, t.count)
                for kk in range(KD):
                    ins = dve.tensor_tensor(keysT[1][:, keys_at(t, kk, t.slot * P, P)],
                                            turn_ps[:, kk * P:(kk + 1) * P],
                                            keysT[0][:, keys_at(t, kk, t.slot * P, P)].bitcast(F32),
                                            ALU.subtract)
                ins.then_inc(q.nT_lo, 1)

            def copy_glogits(t):
                i = t.slot % 4
                dve.wait_ge(q.glogits_done, t.count)
                if t.after(4):
                    dve.wait_ge(q.exp_ready, fours(t))
                dve.tensor_copy(logits[:, i, :], out_ps[:, 0:E]).then_inc(q.glogits_ready, 1)

            def add_gate_b(t):
                dve.wait_ge(q.gate_done, t.count)
                if t.after(2):
                    dve.wait_ge(q.tanh_ready, t.before(2))
                dve.tensor_tensor(z[:, t.slot % 2, :], mm_ps[:, 0:D], w.gate_b[:, :],
                                  ALU.add).then_inc(q.z_ready, 1)

            def q_lo(t):
                j = t.slot % 2
                dve.wait_ge(q.q_hi, t.count)
                dve.tensor_tensor(qT[1][:, j, :], mm_ps[:, 0:D], qT[0][:, j, :].bitcast(F32),
                                  ALU.subtract).then_inc(q.q_lo, 1)

            def row_max(t):
                i = t.slot
                dve.wait_ge(q.logits_done, t.count)
                dve.tensor_reduce(rowmax[:, i:i + 1], logits_ps[:, 0:KEYS + (i + 1) * P], AX.X,
                                  ALU.max).then_inc(q.rowmax_ready, 1)

            def route(t):
                if t.slot % 4 != 3:
                    return
                r = fours(t)
                dve.wait_ge(q.exp_ready, r + 1)
                dve.tensor_scalar(one_plus[:, :, :], exp_l[:, :, :], 1.0, None,
                                  ALU.add).then_inc(q.one_plus_ready, 1)
                dve.wait_ge(q.one_plus_ready, r + 1)
                dve.reciprocal(sigmoid[:, :, :], one_plus[:, :, :]).then_inc(q.sigmoid_ready, 1)
                dve.wait_ge(q.sigmoid_ready, r + 1)
                dve.tensor_scalar(gate_s[:, :, :], sigmoid[:, :, :], w.route_scale[:, :], None,
                                  ALU.mult).then_inc(q.gate_s_ready, 1)
                wait_apart(dve, k, (q.gate_s_ready, r + 1))
                for i in range(4):
                    ins = dve.max(top[:, i, :], gate_s[:, i, :])
                ins.then_inc(q.top_ready, 1)
                wait_apart(dve, k, (q.top_ready, r + 1))
                for i in range(4):
                    ins = dve.max_index(top_at[:, i, :], top[:, i, :], gate_s[:, i, :])
                ins.then_inc(q.top_at_ready, 1)
                dve.tensor_tensor(total[:, :], top[:, :, 0], top[:, :, 1], ALU.add).then_inc(q.total_ready, 1)
                dve.wait_ge(q.total_ready, r + 1)
                dve.reciprocal(rtotal[:, :], total[:, :]).then_inc(q.rtotal_ready, 1)
                dve.wait_ge(q.top_at_ready, r + 1)
                dve.tensor_copy(chosen_at[:, :, :], top_at[:, :, 0:2]).then_inc(q.chosen_at_ready, 1)
                dve.wait_ge(q.rtotal_ready, r + 1)
                for c in range(2):
                    ins = dve.scalar_tensor_tensor(out=chosen_w[:, :, c], in0=top[:, :, c],
                                                   scalar=k.tanh_g[:, 3:4], in1=rtotal[:, :],
                                                   op0=ALU.mult, op1=ALU.mult)
                ins.then_inc(q.chosen_w_ready, 1)
                dve.wait_ge(q.chosen_at_ready, r + 1)
                dve.tensor_tensor(chosen[:, :, :, :].rearrange("p b c e -> p (b c) e"),
                                  k.iota8[:, :].unsqueeze(1).to_broadcast([P, 8, E]),
                                  chosen_at[:, :, :].rearrange("p b c -> p (b c)").unsqueeze(2)
                                  .to_broadcast([P, 8, E]), ALU.is_equal).then_inc(q.chosen_ready, 1)
                dve.wait_ge(q.chosen_ready, r + 1)
                dve.wait_ge(q.chosen_w_ready, r + 1)
                dve.tensor_tensor(weighed[:, :, :, :].rearrange("p b c e -> p (b c) e"),
                                  chosen[:, :, :, :].rearrange("p b c e -> p (b c) e"),
                                  chosen_w[:, :, :].rearrange("p b c -> p (b c)").unsqueeze(2)
                                  .to_broadcast([P, 8, E]), ALU.mult).then_inc(q.weighed_ready, 1)
                dve.wait_ge(q.weighed_ready, r + 1)
                here = k.gates[:, bass.ds(r * (4 * (E + 1)), 4 * (E + 1))].rearrange("p (b e) -> p b e", e=E + 1)
                dve.tensor_tensor(here[:, :, 0:E], weighed[:, :, 0, :], weighed[:, :, 1, :],
                                  ALU.add).then_inc(q.gates_ready, 1)

            dve.tensor_scalar(k.gates[:, E::E + 1], k.ones32[:, :], k.tanh_g[:, 3:4], None,
                              ALU.mult).then_inc(q.weight_ready, 1)
            pipeline(dve, NT, DEPTH, POS,
                     lambda at: run(at, (5, rms_norm), (11, difference), (6, add_gate_b), (5, n_lo),
                                    (14, copy_glogits), (8, row_max), (5, h_lo), (2, combine),
                                    (14, route), (6, q_lo)))


def dense_experts(nc, a, k, out):
    with Scope(nc, "dense") as s:
        N = BANK
        SUB = N // P
        GROUPS = T // N
        X = E + 1
        UNITS = X + 1
        WIDTH = 2 * UNITS
        W1, W2, b1 = (s.sb(n, sh) for n, sh in (("W1", [P, X, KD, H1]), ("W2", [P, X, D]), ("b1", [P, X])))
        W1_parts = [s.sb(f"W1_{i}", [P, X, KD, H1], F32R) for i in range(2)]
        W2_parts = [s.sb(f"W2_{i}", [P, X, D], F32R) for i in range(2)]
        b2 = s.sb("b2", [X, D])
        xT = s.sb("xT", [P, 2, KD, N])
        xT_parts = [s.sb(f"xT{i}", [P, 2, KD, N], F32R) for i in range(2)]
        x3 = s.sb("x3", [P, 2, SUB, D])
        acc = s.sb("acc", [P, 2, SUB, D])
        h = s.sb("h", [P, 2, N])
        h_parts = [s.sb(f"h{i}", [P, 2, N], F32R) for i in range(2)]
        gates_now = s.sb("gates_now", [P, SUB * X])
        gatesT = s.sb("gatesT", [X, N])
        hid_ps = s.ps("hid_ps", [P, 2, BANK])
        y_ps = s.ps("y_ps", [P, SUB, BANK])
        gates_ps = s.ps("gates_ps", [P, BANK])

        weights_loaded = s.sem("weights_loaded")
        x_loaded = [s.sem(f"x_loaded{i}") for i in range(2)]
        x3_loaded = [s.sem(f"x3_loaded{i}") for i in range(2)]
        stored = [s.sem(f"stored{i}") for i in range(2)]
        q = Named()
        (q.w_hi, q.w_lo, q.x_hi, q.x_lo, q.hid_done, q.h_ready, q.h_hi, q.h_lo) = s.sems(
            "w_hi w_lo x_hi x_lo hid_done h_ready h_hi h_lo")
        (q.y_done, q.added, q.gates_copied, q.gates_turned, q.gatesT_ready) = s.sems(
            "y_done added gates_copied gates_turned gatesT_ready")
        DEPTH = 10
        block = s.block()

        def expert(t):
            return t.slot % UNITS

        def parity(t):
            return t.slot // UNITS

        def group(t, ahead=0):
            return t.round * 2 + (parity(t) + ahead)

        def hidden_count(t, ahead=0):
            return t.round * (2 * X) + (parity(t) * X + expert(t) + 1 + ahead)

        def buffer(t):
            return (parity(t) * X + expert(t)) % 2

        def at_expert(stage, *which):
            return lambda t: stage(t) if expert(t) in which else None

        def many(stage):
            return at_expert(stage, *range(X))

        def tile(t, j):
            return t.round * (2 * SUB) + (parity(t) * SUB + j)

        loads = [
            (W1[:, 0:E, :, :], a["L1_ffn_W1"].rearrange("e (k p) n -> p e k n", p=P)),
            (W1[:, E, :, :], a["L1_ffn_Ws1"].rearrange("(k p) n -> p k n", p=P)),
            (b1[:, :], a["L1_ffn_b1"]),
            (W2[:, 0:E, :], a["L1_ffn_W2"].rearrange("e p n -> p e n")),
            (W2[:, E, :], a["L1_ffn_Ws2"]),
            (b2[:, :], a["L1_ffn_b2"]),
        ]

        @block.sync
        def _(sp):
            def load(t):
                g = parity(t)
                if t.after(WIDTH):
                    sp.wait_ge(q.x_lo, group(t, -1))
                    sp.wait_ge(q.added, t.before(WIDTH) * SUB)
                sp.dma_start(xT[:, g, :, :], k.xn4T.rearrange("(k p) t -> p k t", p=P)
                             [:, :, bass.ds(group(t) * N, N)]).then_inc(x_loaded[g], 16)
                sp.dma_start(x3[:, g, :, :], k.x3[bass.ds(group(t) * N, N), :]
                             .rearrange("(j p) d -> p j d", p=P)).then_inc(x3_loaded[g], 16)

            def store(t):
                g = parity(t)
                sp.wait_ge(q.added, t.count * SUB)
                sp.dma_start(out[bass.ds(group(t) * N, N), :].rearrange("(j p) d -> p j d", p=P),
                             acc[:, g, :, :]).then_inc(stored[g], 16)

            for to, of in loads:
                sp.dma_start(to, of).then_inc(weights_loaded, 16)
            pipeline(sp, GROUPS * UNITS, DEPTH, WIDTH,
                     lambda at: run(at, (10, at_expert(store, X)), (0, at_expert(load, 0))))
            for g in range(2):
                sp.wait_ge(stored[g], 16 * (GROUPS // 2))

        @block.gpsimd
        def _(pool):
            def copy_gates(t):
                if t.after(UNITS):
                    pool.wait_ge(q.gates_turned, group(t))
                pool.tensor_copy(gates_now[:, :], k.gates[:, bass.ds(group(t) * (SUB * X), SUB * X)]
                                 ).then_inc(q.gates_copied, 1)

            pipeline(pool, GROUPS * UNITS, DEPTH, WIDTH,
                     lambda at: run(at, (3, at_expert(copy_gates, X))))

        @block.tensor
        def _(pe):
            def hidden(t):
                i = buffer(t)
                pe.wait_ge(q.x_lo, group(t, 1))
                if t.after(2):
                    pe.wait_ge(q.h_ready, hidden_count(t, -2))
                e = expert(t)
                for c in range(KD):
                    mm = three_passes(pe, hid_ps[:, i, :], [part[:, e, c, :] for part in W1_parts],
                                      [part[:, parity(t), c, :] for part in xT_parts],
                                      start=(c == 0), stop=(c == KD - 1))
                mm.then_inc(q.hid_done, 1)

            def turn_gates(t):
                pe.wait_ge(q.gates_copied, group(t, 1))
                if t.after(UNITS):
                    pe.wait_ge(q.gatesT_ready, group(t))
                for j in range(SUB):
                    mm = pe.transpose(gates_ps[0:X, j * P:(j + 1) * P], gates_now[:, j * X:(j + 1) * X],
                                      k.ident[:, :])
                mm.then_inc(q.gates_turned, 1)

            def bank_free(t, j):
                if t.after(1):
                    pe.wait_ge(q.added, t.before(1) * SUB - (SUB - 1 - j))

            def product(t):
                i, e = buffer(t), expert(t)
                pe.wait_ge(q.h_lo, hidden_count(t))
                for j in range(SUB):
                    bank_free(t, j)
                    three_passes(pe, y_ps[:, j, 0:D], [part[:, i, j * P:(j + 1) * P] for part in h_parts],
                                 [part[:, e, :] for part in W2_parts], start=True, stop=True
                                 ).then_inc(q.y_done, 1)

            def bias(t):
                pe.wait_ge(q.gatesT_ready, group(t, 1))
                for j in range(SUB):
                    bank_free(t, j)
                    pe.matmul(y_ps[:, j, 0:D], gatesT[:, j * P:(j + 1) * P], b2[:, :],
                              start=True, stop=True).then_inc(q.y_done, 1)

            pe.wait_ge(q.w_lo, 2)
            pipeline(pe, GROUPS * UNITS, DEPTH, WIDTH,
                     lambda at: run(at, (8, at_expert(turn_gates, X)), (8, many(hidden)),
                                    (10, at_expert(bias, X)), (10, many(product))))

        @block.scalar
        def _(act):
            def split(t):
                g = parity(t)
                act.wait_ge(x_loaded[g], t.round * 16 + 16)
                if t.after(WIDTH):
                    act.wait_ge(q.hid_done, hidden_count(t, -X - 1))
                act.activation(xT_parts[0][:, g, :, :], xT[:, g, :, :], ACT.Copy).then_inc(q.x_hi, 1)

            def gelu(t):
                i, e = buffer(t), expert(t)
                act.wait_ge(q.hid_done, hidden_count(t))
                if t.after(2):
                    act.wait_ge(q.h_lo, hidden_count(t, -2))
                act.activation(h[:, i, :], hid_ps[:, i, :], ACT.Gelu, bias=b1[:, e:e + 1]
                               ).then_inc(q.h_ready, 1)
                act.wait_ge(q.h_ready, hidden_count(t))
                if t.after(2):
                    act.wait_ge(q.y_done, (t.before(3) if e < 2 else t.before(2)) * SUB)
                act.activation(h_parts[0][:, i, :], h[:, i, :], ACT.Copy).then_inc(q.h_hi, 1)

            def copy_gatesT(t):
                act.wait_ge(q.gates_turned, group(t, 1))
                if t.after(UNITS):
                    act.wait_ge(q.y_done, t.before(UNITS) * SUB)
                act.activation(gatesT[:, :], gates_ps[0:X, :], ACT.Copy).then_inc(q.gatesT_ready, 1)

            act.wait_ge(weights_loaded, 16 * len(loads))
            act.activation(W1_parts[0][:, :, :, :], W1[:, :, :, :], ACT.Copy).then_inc(q.w_hi, 1)
            act.activation(W2_parts[0][:, :, :], W2[:, :, :], ACT.Copy).then_inc(q.w_hi, 1)
            pipeline(act, GROUPS * UNITS, DEPTH, WIDTH,
                     lambda at: run(at, (3, at_expert(split, 0)), (9, at_expert(copy_gatesT, X)),
                                    (8, many(gelu))))

        @block.vector
        def _(dve):
            def split(t):
                g = parity(t)
                dve.wait_ge(q.x_hi, group(t, 1))
                dve.tensor_tensor(xT_parts[1][:, g, :, :], xT[:, g, :, :],
                                  xT_parts[0][:, g, :, :].bitcast(F32), ALU.subtract).then_inc(q.x_lo, 1)

            def add(t):
                g, e = parity(t), expert(t)
                if e == 0:
                    dve.wait_ge(x3_loaded[g], t.round * 16 + 16)
                    if t.after(WIDTH):
                        dve.wait_ge(stored[g], t.round * 16)
                for j in range(SUB):
                    dve.wait_ge(q.y_done, t.before(1) * SUB + (j + 1))
                    if e == 0:
                        so_far = x3[:, g, j, :]
                    else:
                        so_far = acc[:, g, j, :]
                        dve.wait_ge(q.added, t.before(1) * SUB - (SUB - 1 - j))
                    if e < X:
                        ins = dve.scalar_tensor_tensor(out=acc[:, g, j, :], in0=y_ps[:, j, 0:D],
                                                       scalar=k.gates[:, bass.ds(tile(t, j) * X + e, 1)],
                                                       in1=so_far, op0=ALU.mult, op1=ALU.add)
                    else:
                        ins = dve.tensor_tensor(acc[:, g, j, :], y_ps[:, j, 0:D], so_far, ALU.add)
                    ins.then_inc(q.added, 1)

            def h_lo(t):
                i = buffer(t)
                dve.wait_ge(q.h_hi, hidden_count(t))
                dve.tensor_tensor(h_parts[1][:, i, :], h[:, i, :], h_parts[0][:, i, :].bitcast(F32),
                                  ALU.subtract).then_inc(q.h_lo, 1)

            dve.wait_ge(q.w_hi, 2)
            dve.tensor_tensor(W1_parts[1][:, :, :, :], W1[:, :, :, :], W1_parts[0][:, :, :, :].bitcast(F32),
                              ALU.subtract).then_inc(q.w_lo, 1)
            dve.tensor_tensor(W2_parts[1][:, :, :], W2[:, :, :], W2_parts[0][:, :, :].bitcast(F32),
                              ALU.subtract).then_inc(q.w_lo, 1)
            pipeline(dve, GROUPS * UNITS, DEPTH, WIDTH,
                     lambda at: run(at, (10, add), (3, at_expert(split, 0)), (8, many(h_lo))))


def flamingo(nc, a, out):
    with Scope(nc, "kept") as s:
        k = allocate_kept(nc, s)
        cross_attention(nc, a, k)
        expert_tiles(nc, a, k)
        causal_attention(nc, a, k)
        dense_experts(nc, a, k, out)


def constants():
    c = {}
    c["c_ident"] = np.eye(P, dtype=np.float32)
    c["c_upper"] = np.triu(np.ones((P, P), np.float32), 1)
    c["c_iota8"] = np.tile(np.arange(E, dtype=np.float32), (P, 1))
    c["c_region"] = np.tile(np.arange(E, dtype=np.float32) * T, (P, 1))
    c["c_above"] = np.triu(np.full((P, P), -1e30, np.float32), 1)
    token = np.arange(P)[:, None, None] + P * np.arange(POS)[None, :, None] + S * np.arange(B)[None, None, :]
    c["c_token"] = token.reshape(P, NT).astype(np.int32)
    c["c_head_mask"] = (np.arange(P)[:, None] // HEAD == np.arange(HEADS // KD)[None, :]).astype(np.float32)
    v = np.zeros((P, PCH, MAXH * VW), np.float32)
    for r in range(HEADS * KEYS):
        v[r % P, r // P, (r // KEYS - chunk_heads(r // P)[0]) * VW + HEAD] = 1.0
    c["c_values"] = v
    return c


def laid_out(x):
    a = {n: np.ascontiguousarray(v) for n, v in x.items()}
    t = {"x": a["x"].reshape(T, D), "mask": a["mask_1x1xSxS2_ik1"].reshape(S, KEYS),
         "ctx": a["ctx_1024"], "ctxT": a["ctx_1024"].transpose(2, 0, 1)}
    t["gates"] = np.stack([a["g_xattn"], a["g_ffn"]], 1).reshape(4)
    for n in ("L0_xattn_bq", "L0_xattn_bk"):
        t[n] = a[n].reshape(KD, P).T
    for n in ("L0_xattn_bv", "L0_xattn_bo",
              "L0_ffn_gate_w", "L0_ffn_ew1", "L0_ffn_ew2", "L0_ffn_ew3", "L0_ffn_sw1", "L0_ffn_sw2",
              "L0_ffn_sw3", "L1_xattn_q_w", "L1_xattn_k_w", "L1_xattn_norm_w", "L1_xattn_gate_b",
              "L1_ffn_gate_W", "L1_ffn_W1", "L1_ffn_W2", "L1_ffn_Ws1", "L1_ffn_Ws2"):
        t[n] = a[n]
    t["L1_ffn_b1"] = np.concatenate([a["L1_ffn_b1"], a["L1_ffn_bs1"].reshape(1, H1)]).T
    t["L1_ffn_b2"] = np.concatenate([a["L1_ffn_b2"], a["L1_ffn_bs2"].reshape(1, D)])
    t["L1_ffn_route_scale"] = a["L1_ffn_route_scale"].reshape(1)
    for n in ("L0_xattn_wq", "L0_xattn_wk", "L0_xattn_wv", "L0_xattn_wo", "L1_xattn_gate_w"):
        t[n] = a[n].T
    return {n: np.ascontiguousarray(v) for n, v in {**t, **constants()}.items()}


def kernel(**inputs):
    from concourse import bacc
    from concourse.bass_utils import run_bass_kernel_spmd

    nc = bacc.Bacc("TRN2", target_bir_lowering=False, num_devices=1)
    arrays = {f"in_{n}": v for n, v in laid_out({n: np.asarray(v) for n, v in inputs.items()}).items()}
    a = {n[3:]: nc.dram_tensor(n, v.shape, mybir.dt.from_np(v.dtype), kind="ExternalInput").ap()
         for n, v in arrays.items()}
    out = nc.dram_tensor("out_0", (B, S, D), F32, kind="ExternalOutput").ap()
    flamingo(nc, a, out.rearrange("b s d -> (b s) d"))
    result = run_bass_kernel_spmd(nc, [arrays], core_ids=[0])
    return result.results[0]["out_0"]
```
